# Optimizing a Trainium2 kernel written in Bass

```python
import numpy as np
import jax
import jax.numpy as jnp

def _softmax(x, axis=-1):
    return jax.nn.softmax(x, axis=axis)

def _gelu(x):
    return jax.nn.gelu(x, approximate=True)

def _silu(x):
    return jax.nn.silu(x)

def _sigmoid(x):
    return jax.nn.sigmoid(x)

def _layernorm(x, axis=-1, eps=1e-05):
    m = jnp.mean(x, axis=axis, keepdims=True)
    v = jnp.var(x, axis=axis, keepdims=True)
    return (x - m) / jnp.sqrt(v + eps)

def _scatter_add(tgt, idx, src, axis=0):
    return tgt.at[idx].add(src)

def _segment_sum(src, seg, n):
    return jax.ops.segment_sum(src, seg, n)
kernel_name = 'mk_vit_tower_postln_d2_tok_img768_r4_7edb49'

def setup_inputs(seed: int=0):
    np.random.seed(seed)
    _w = jnp.asarray

    def _rec_inputs():
        import jax
        import jax.numpy as jnp
        _rk = jax.random.key(seed)
        x = -0.000356955 + 1 * jax.random.normal(jax.random.fold_in(_rk, 1), (64, 224, 224, 3), jnp.float32)
        return x
    x = _rec_inputs()

    def _L0_tok_setup():
        import jax, jax.numpy as jnp
        import numpy as np
        PATCH = 16
        IMG = 224
        NP_SIDE = IMG // PATCH
        EMBED = 192

        def _patchify(batch_image):
            B = batch_image.shape[0]
            x = batch_image.reshape(B, NP_SIDE, PATCH, NP_SIDE, PATCH, 3)
            x = x.transpose(0, 1, 3, 5, 2, 4)
            return x.reshape(B, NP_SIDE * NP_SIDE, 3 * PATCH * PATCH)
        key = jax.random.key(seed)
        k1, k2, k3, k4, k5 = jax.random.split(key, 5)
        return {'batch_image': jax.random.normal(k1, (128, IMG, IMG, 3), dtype=jnp.float32), 'W': jax.random.normal(k2, (EMBED, 3 * PATCH * PATCH), dtype=jnp.float32) * 0.02, 'b': jax.random.normal(k3, (EMBED,), dtype=jnp.float32) * 0.02, 'cls_token': jax.random.normal(k4, (1, 1, EMBED), dtype=jnp.float32), 'pos_embed': jax.random.normal(k5, (1, NP_SIDE * NP_SIDE + 1, EMBED), dtype=jnp.float32)}
    _L0_tok_all = _L0_tok_setup()
    _L0_tok_in = {k: v for k, v in _L0_tok_all.items() if k in ('W', 'b', 'cls_token', 'pos_embed')}
    del _L0_tok_all

    def _L0_attn_setup():
        import jax, jax.numpy as jnp
        import numpy as np
        DIM = 192
        HEADS = 12
        SCALE = DIM ** (-0.5)
        key = jax.random.key(seed)
        ks = jax.random.split(key, 5)
        B, N, C = (8, 256, DIM)
        x = jax.random.normal(ks[0], (B, N, C), dtype=jnp.float32)
        W_qkv = jax.random.normal(ks[1], (C, 3 * C), dtype=jnp.float32) * C ** (-0.5)
        b_qkv = jnp.zeros((3 * C,), dtype=jnp.float32)
        W_out = jax.random.normal(ks[2], (C, C), dtype=jnp.float32) * C ** (-0.5)
        b_out = jnp.zeros((C,), dtype=jnp.float32)
        return {'x': x, 'W_qkv': W_qkv, 'b_qkv': b_qkv, 'W_out': W_out, 'b_out': b_out}
    _L0_attn_all = _L0_attn_setup()
    _L0_attn_in = {k: v for k, v in _L0_attn_all.items() if k in ('W_qkv', 'b_qkv', 'W_out', 'b_out')}
    del _L0_attn_all

    def _L0_ffn_setup():
        import jax, jax.numpy as jnp
        import numpy as np
        B, T, E = (2, 256, 192)
        H = 768
        N_EXP = 4
        key = jax.random.key(seed)
        ks = jax.random.split(key, 8)
        s_e = 1.0 / np.sqrt(E)
        s_h = 1.0 / np.sqrt(H)
        return {'x': jax.random.normal(ks[0], (B, T, E), dtype=jnp.float32), 'Wg': jax.random.uniform(ks[1], (E, N_EXP), minval=-s_e, maxval=s_e, dtype=jnp.float32), 'bg': jax.random.uniform(ks[2], (N_EXP,), minval=-s_e, maxval=s_e, dtype=jnp.float32), 'W1': jax.random.uniform(ks[3], (N_EXP, E, H), minval=-s_e, maxval=s_e, dtype=jnp.float32), 'b1': jax.random.uniform(ks[4], (N_EXP, H), minval=-s_e, maxval=s_e, dtype=jnp.float32), 'W2': jax.random.uniform(ks[5], (N_EXP, H, E), minval=-s_h, maxval=s_h, dtype=jnp.float32), 'b2': jax.random.uniform(ks[6], (N_EXP, E), minval=-s_h, maxval=s_h, dtype=jnp.float32)}
    _L0_ffn_all = _L0_ffn_setup()
    _L0_ffn_in = {k: v for k, v in _L0_ffn_all.items() if k in ('Wg', 'bg', 'W1', 'b1', 'W2', 'b2')}
    del _L0_ffn_all

    def _L1_attn_setup():
        import jax, jax.numpy as jnp
        import numpy as np
        key = jax.random.key(seed)
        k1, k2, k3, k4, k5 = jax.random.split(key, 5)
        B, N, C = (16, 256, 192)
        x = jax.random.normal(k1, (B, N, C), dtype=jnp.float32)
        sc_token = jax.random.normal(k2, (1, 196, C), dtype=jnp.float32) * 0.02
        W_qkv = jax.random.normal(k3, (C, 3 * C), dtype=jnp.float32) * 0.02
        W_proj = jax.random.normal(k4, (C, C), dtype=jnp.float32) * 0.02
        b_proj = jax.random.normal(k5, (C,), dtype=jnp.float32) * 0.02
        return {'x': x, 'sc_token': sc_token, 'W_qkv': W_qkv, 'W_proj': W_proj, 'b_proj': b_proj}
    _L1_attn_all = _L1_attn_setup()
    _L1_attn_in = {k: v for k, v in _L1_attn_all.items() if k in ('sc_token', 'W_qkv', 'W_proj', 'b_proj')}
    del _L1_attn_all

    def _L1_ffn_setup():
        import jax, jax.numpy as jnp
        import numpy as np
        DIM = 192
        HID = 4 * DIM
        NUM_EXPERTS = 3
        TOP_K = 2
        R = 8
        ALPHA = 8
        SCALING = ALPHA / R
        key = jax.random.key(seed)
        ks = jax.random.split(key, 9)
        B, N = (64, 196)
        return {'x': jax.random.normal(ks[0], (B, N, DIM), jnp.float32), 'w1': jax.random.normal(ks[1], (DIM, HID), jnp.float32) * (1.0 / np.sqrt(DIM)), 'b1': jax.random.normal(ks[2], (HID,), jnp.float32) * 0.01, 'w2': jax.random.normal(ks[3], (HID, DIM), jnp.float32) * (1.0 / np.sqrt(HID)), 'b2': jax.random.normal(ks[4], (DIM,), jnp.float32) * 0.01, 'router_w': jax.random.normal(ks[5], (DIM, NUM_EXPERTS), jnp.float32) * (1.0 / np.sqrt(DIM)), 'router_b': jax.random.normal(ks[6], (NUM_EXPERTS,), jnp.float32) * 0.01, 'w_down': jax.random.normal(ks[7], (NUM_EXPERTS, DIM, R), jnp.float32) * (1.0 / np.sqrt(DIM)), 'w_up': jax.random.normal(ks[8], (NUM_EXPERTS, R, DIM), jnp.float32) * 0.02}
    _L1_ffn_all = _L1_ffn_setup()
    _L1_ffn_in = {k: v for k, v in _L1_ffn_all.items() if k in ('w1', 'b1', 'w2', 'b2', 'router_w', 'router_b', 'w_down', 'w_up')}
    del _L1_ffn_all
    return {'x': x, 'L0_tok_W': _L0_tok_in['W'], 'L0_tok_b': _L0_tok_in['b'], 'L0_tok_cls_token': _L0_tok_in['cls_token'], 'L0_tok_pos_embed': _L0_tok_in['pos_embed'], 'L0_attn_W_qkv': _L0_attn_in['W_qkv'], 'L0_attn_b_qkv': _L0_attn_in['b_qkv'], 'L0_attn_W_out': _L0_attn_in['W_out'], 'L0_attn_b_out': _L0_attn_in['b_out'], 'L0_ffn_Wg': _L0_ffn_in['Wg'], 'L0_ffn_bg': _L0_ffn_in['bg'], 'L0_ffn_W1': _L0_ffn_in['W1'], 'L0_ffn_b1': _L0_ffn_in['b1'], 'L0_ffn_W2': _L0_ffn_in['W2'], 'L0_ffn_b2': _L0_ffn_in['b2'], 'L1_attn_sc_token': _L1_attn_in['sc_token'], 'L1_attn_W_qkv': _L1_attn_in['W_qkv'], 'L1_attn_W_proj': _L1_attn_in['W_proj'], 'L1_attn_b_proj': _L1_attn_in['b_proj'], 'L1_ffn_w1': _L1_ffn_in['w1'], 'L1_ffn_b1': _L1_ffn_in['b1'], 'L1_ffn_w2': _L1_ffn_in['w2'], 'L1_ffn_b2': _L1_ffn_in['b2'], 'L1_ffn_router_w': _L1_ffn_in['router_w'], 'L1_ffn_router_b': _L1_ffn_in['router_b'], 'L1_ffn_w_down': _L1_ffn_in['w_down'], 'L1_ffn_w_up': _L1_ffn_in['w_up']}

def reference(x, L0_tok_W, L0_tok_b, L0_tok_cls_token, L0_tok_pos_embed, L0_attn_W_qkv, L0_attn_b_qkv, L0_attn_W_out, L0_attn_b_out, L0_ffn_Wg, L0_ffn_bg, L0_ffn_W1, L0_ffn_b1, L0_ffn_W2, L0_ffn_b2, L1_attn_sc_token, L1_attn_W_qkv, L1_attn_W_proj, L1_attn_b_proj, L1_ffn_w1, L1_ffn_b1, L1_ffn_w2, L1_ffn_b2, L1_ffn_router_w, L1_ffn_router_b, L1_ffn_w_down, L1_ffn_w_up):
    import jax
    import jax.numpy as jnp

    def _L0_tok_ref(batch_image, W, b, cls_token, pos_embed):
        import jax, jax.numpy as jnp
        import numpy as np
        PATCH = 16
        IMG = 224
        NP_SIDE = IMG // PATCH
        EMBED = 192

        def _patchify(batch_image):
            B = batch_image.shape[0]
            x = batch_image.reshape(B, NP_SIDE, PATCH, NP_SIDE, PATCH, 3)
            x = x.transpose(0, 1, 3, 5, 2, 4)
            return x.reshape(B, NP_SIDE * NP_SIDE, 3 * PATCH * PATCH)
        B = batch_image.shape[0]
        patches = _patchify(batch_image)
        Zp = jnp.einsum('bpd,ed->bpe', patches, W) + b
        Zcls = jnp.broadcast_to(cls_token, (B, 1, EMBED))
        Zcls_p = jnp.concatenate([Zcls, Zp], axis=1)
        return Zcls_p + pos_embed

    def _L0_attn_ref(x, W_qkv, b_qkv, W_out, b_out):
        import jax, jax.numpy as jnp
        import numpy as np
        DIM = 192
        HEADS = 12
        SCALE = DIM ** (-0.5)
        B, N, C = x.shape
        H, D = (HEADS, C // HEADS)
        qkv = x @ W_qkv + b_qkv
        q, k, v = jnp.split(qkv, 3, axis=-1)
        q = q.reshape(B, N, H, D).transpose(0, 2, 1, 3)
        k = k.reshape(B, N, H, D).transpose(0, 2, 1, 3)
        v = v.reshape(B, N, H, D).transpose(0, 2, 1, 3)
        attn = jnp.einsum('bhnd,bhmd->bhnm', q, k) * SCALE
        attn = jax.nn.softmax(attn, axis=-1)
        out = jnp.einsum('bhnm,bhmd->bhnd', attn, v)
        out = out.transpose(0, 2, 1, 3).reshape(B, N, C)
        return out @ W_out + b_out

    def _L0_ffn_ref(x, Wg, bg, W1, b1, W2, b2):
        import jax, jax.numpy as jnp
        import numpy as np
        B, T, E = (2, 256, 192)
        H = 768
        N_EXP = 4
        gate_logits = jnp.einsum('bte,en->btn', x, Wg) + bg
        top = jnp.argmax(gate_logits, axis=-1)
        h = jax.nn.gelu(jnp.einsum('bte,neh->nbth', x, W1) + b1[:, None, None, :], approximate=False)
        y = jnp.einsum('nbth,nhe->nbte', h, W2) + b2[:, None, None, :]
        onehot = jax.nn.one_hot(top, N_EXP, dtype=x.dtype)
        out = jnp.einsum('nbte,btn->bte', y, onehot)
        return out

    def _L1_attn_ref(x, sc_token, W_qkv, W_proj, b_proj):
        import jax, jax.numpy as jnp
        import numpy as np
        B, N, C = x.shape
        H = 12
        Dh = C // H
        scale = Dh ** (-0.5)
        xt = jnp.concatenate([x, jnp.broadcast_to(sc_token, (B,) + sc_token.shape[1:])], axis=1)
        N1 = xt.shape[1]
        qkv = (xt @ W_qkv).reshape(B, N1, 3, H, Dh)
        q = qkv[:, :, 0].transpose(0, 2, 1, 3)
        k = qkv[:, :, 1].transpose(0, 2, 1, 3)
        v = qkv[:, :, 2].transpose(0, 2, 1, 3)
        attn = jax.nn.softmax(jnp.einsum('bhqd,bhkd->bhqk', q, k) * scale, axis=-1)
        out = jnp.einsum('bhqk,bhkd->bhqd', attn, v)
        out = out.transpose(0, 2, 1, 3).reshape(B, N1, C)
        out = out[:, :N, :]
        return out @ W_proj + b_proj

    def _L1_ffn_ref(x, w1, b1, w2, b2, router_w, router_b, w_down, w_up):
        import jax, jax.numpy as jnp
        import numpy as np
        DIM = 192
        HID = 4 * DIM
        NUM_EXPERTS = 3
        TOP_K = 2
        R = 8
        ALPHA = 8
        SCALING = ALPHA / R
        orig_out = jax.nn.gelu(x @ w1 + b1, approximate=False) @ w2 + b2
        orig_shape = x.shape
        xf = x.reshape(-1, orig_shape[-1])
        gate_probs = jax.nn.softmax(xf @ router_w + router_b, axis=-1)
        topk_probs, topk_idx = jax.lax.top_k(gate_probs, TOP_K)
        topk_probs = topk_probs / (topk_probs.sum(axis=-1, keepdims=True) + 1e-06)
        onehot = jax.nn.one_hot(topk_idx, NUM_EXPERTS, dtype=xf.dtype)
        comb_w = (onehot * topk_probs[..., None]).sum(axis=1)
        down = jnp.einsum('td,edr->ter', xf, w_down)
        act = jax.nn.gelu(down, approximate=False)
        up = jnp.einsum('ter,erd->ted', act, w_up) * SCALING
        moe_out = jnp.einsum('ted,te->td', up, comb_w)
        return orig_out + moe_out.reshape(orig_shape)
    h = _L0_tok_ref(x, L0_tok_W, L0_tok_b, L0_tok_cls_token, L0_tok_pos_embed)
    h = _layernorm(h + _L0_attn_ref(h, L0_attn_W_qkv, L0_attn_b_qkv, L0_attn_W_out, L0_attn_b_out), axis=-1)
    h = _layernorm(h + _L0_ffn_ref(h, L0_ffn_Wg, L0_ffn_bg, L0_ffn_W1, L0_ffn_b1, L0_ffn_W2, L0_ffn_b2), axis=-1)
    h = _layernorm(h + _L1_attn_ref(h, L1_attn_sc_token, L1_attn_W_qkv, L1_attn_W_proj, L1_attn_b_proj), axis=-1)
    h = _layernorm(h + _L1_ffn_ref(h, L1_ffn_w1, L1_ffn_b1, L1_ffn_w2, L1_ffn_b2, L1_ffn_router_w, L1_ffn_router_b, L1_ffn_w_down, L1_ffn_w_up), axis=-1)
    return h

_drawn_inputs = setup_inputs


def setup_inputs(seed=0):
    import zlib

    import numpy as np

    out = dict(_drawn_inputs(seed))
    spreads = {'L0_attn_b_qkv': (0.0, 0.1), 'L0_attn_b_out': (0.0, 0.1)}
    factors = {'L0_ffn_b1': 3.878,
     'L1_attn_sc_token': 64.0,
     'L1_attn_W_qkv': 8.0,
     'L1_attn_W_proj': 8.0,
     'L1_attn_b_proj': 9.455,
     'L1_ffn_b1': 8.0,
     'L1_ffn_b2': 7.025,
     'L1_ffn_router_w': 3.756,
     'L1_ffn_router_b': 190.182,
     'L1_ffn_w_down': 2.671}
    for name, (base, spread) in spreads.items():
        noise = np.random.default_rng([zlib.crc32(name.encode()), seed]).standard_normal(out[name].shape)
        drawn = base * np.exp(spread * noise) if base else spread * noise
        out[name] = jnp.asarray(drawn.astype(out[name].dtype))
    for name, factor in factors.items():
        out[name] = (out[name] * factor).astype(out[name].dtype)
    return out
```

```python
import concourse.bass as bass
from concourse import mybir
from contextlib import ExitStack

F32 = mybir.dt.float32
F16 = mybir.dt.float16
ALU = mybir.AluOpType
ACT = mybir.ActivationFunctionType
AX = mybir.AxisListType

P = 128
E = 192
EA = 128
EB = E - EA
NT = 197
NSC = 196
T1 = NT - P
HEADS, HD = 12, 16
HG = 4
NG = HEADS // HG
KD = 768 // P
NEXP = 4
CT = 3
CHUNK = CT * P
EPS = 1e-5

C_HEAD, C_HEADHI, C_HEADONE, C_LO, C_HI, C_ROW1, C_ROW01, C_N = 0, 4, 8, 12, 13, 14, 15, 16


def wait(eng, semaphore, value):
    if isinstance(value, int) and value <= 0:
        return
    eng.wait_ge(semaphore, value)


def token_tiles(n):
    return [(0, P), (P, n - P)]


def five_passes(nc, out, xh, xl, wh, wl, cols, tok, x_stationary, first=True, last=True):
    pairs = [(xh[:, 0, tok], wh[:, 0, cols]), (xl[:, tok], wh[:, 0, cols]), (xh[:, 0, tok], wl[:, 0, cols]),
             (xh[:, 1, tok], wh[:, 1, cols]), (xh[:, 1, tok], wl[:, 1, cols])]
    for n, (x, w) in enumerate(pairs):
        l, r = (x, w) if x_stationary else (w, x)
        ins = nc.tensor.matmul(out, l, r, start=first and n == 0, stop=last and n == len(pairs) - 1)
    return ins


def run_steps(eng, n, body):
    body(-1, 1, True, False, False)
    body(0, 0, n > 1, True, False)
    pairs = max(0, (n - 2) // 2)
    if pairs:
        with eng.Fori(0, pairs) as pair:
            body(pair * 2 + 1, 1, True, True, True)
            body(pair * 2 + 2, 0, True, True, True)
    for t in range(2 * pairs + 1, n + 1):
        body(t, t % 2, t + 1 < n, t < n, True)


def setup(nc, loads_all, consts_d, masks, ident, ident16, sem, sb, sums, scratch, fill_d, tokens):
    loads = [x for x in loads_all if x[1].dtype == F16]
    stage = [sb("stage0", [P, 6144], F32), sb("stage1", [P, 6144], F32)]
    staged, hi_done, lo_done, const_done = sem("staged"), sem("hi_done"), sem("lo_done"), sem("const_done")
    padded = sem("padded")
    with nc.Block() as block:

        @block.sync
        def _(sp):
            sp.dma_start(masks[:, :], consts_d[:, 0:C_N]).then_inc(const_done, 16)
            sp.dma_start(ident[:, :], consts_d[:, C_N:C_N + P]).then_inc(const_done, 16)
            direct = [x for x in loads_all if x[1].dtype == F32]
            for src, dst, _, _, _ in direct:
                sp.dma_start(dst, src).then_inc(const_done, 16)
            sp.wait_ge(const_done, 32 + 16 * len(direct))
            pads = scratch[0].shape[0] - tokens
            for n, h in enumerate(scratch if pads else []):
                for at in range(tokens, tokens + pads, P):
                    m = min(P, tokens + pads - at)
                    sp.dma_start(h[at:at + m, :], fill_d[0:m, 0, :]).then_inc(padded, 16)
            if pads:
                sp.wait_ge(padded, 16 * len(scratch) * -(-pads // P))
            for n, (src, hi, lo, size, rows) in enumerate(loads):
                if n >= 2:
                    sp.wait_ge(lo_done, n - 1)
                sp.dma_start(stage[n % 2][0:rows, 0:size], src).then_inc(staged, 16)
                sp.wait_ge(staged, 16 * (n + 1))

        @block.scalar
        def _(act):
            act.wait_ge(const_done, 16 * (2 + len(loads_all) - len(loads)))
            nc.scalar.activation(ident16[:, :], ident[:, :], ACT.Copy)
            for n, (src, hi, lo, size, rows) in enumerate(loads):
                act.wait_ge(staged, 16 * (n + 1))
                if lo is None:
                    nc.scalar.activation(hi, stage[n % 2][0:rows, 0:size], ACT.Copy,
                                         scale=masks[:, C_ROW1:C_ROW1 + 1]).then_inc(hi_done, 1)
                else:
                    nc.scalar.activation(hi, stage[n % 2][0:rows, 0:size], ACT.Copy).then_inc(hi_done, 1)

        @block.vector
        def _(dve):
            for n, (src, hi, lo, size, rows) in enumerate(loads):
                dve.wait_ge(hi_done, n + 1)
                target = hi if lo is None else lo
                nc.vector.tensor_tensor(target, stage[n % 2][0:rows, 0:size], hi, ALU.subtract).then_inc(lo_done, 1)
            dve.wait_ge(lo_done, len(loads))
            pos, tokb, addend = sums
            nc.vector.tensor_tensor(addend[:, :, :], pos[:, :, :], tokb[:, :, :], ALU.add)


def attention(nc, layer, NB, src_d, dst_d, W, masks, ident, ident16, sem, sb, pb):
    L0 = layer == 0
    wh, wl = W["wh"], W["wl"]
    qcol = lambda g: slice(P * g, P * g + P)
    kcol = lambda g: slice(NG * P + P * g, NG * P + P * g + P)
    vcol, ocol = slice(2 * NG * P, 2 * NG * P + E), slice(2 * NG * P + E, 2 * NG * P + 2 * E)
    scale = float(E) ** -0.5 if L0 else float(HD) ** -0.5
    ktiles = [("own", 0, P), ("own", 1, T1)] + ([] if L0 else [("ctx", 0, P), ("ctx", 1, NSC - P)])
    NK = len(ktiles)
    SLOTS = NG * NK
    NKEYS = NT if L0 else NT + NSC

    n_ = lambda s: f"a{layer}_{s}"
    xtok = [sb(n_(f"xtok{i}"), [P, 2, 256], F32) for i in range(2)]
    xres = [sb(n_(f"xres{i}"), [P, 2, E], F32) for i in range(2)]
    xh = [sb(n_(f"xh{i}"), [P, 2, NT], F16) for i in range(2)]
    xl = [sb(n_(f"xl{i}"), [P, NT], F16) for i in range(2)]
    patches = [sb(n_(f"patch{i}"), [P, KD, NT], F32) for i in range(2)] if L0 else None
    khi = sb(n_("khi"), [P, NG, NT], F16)
    khl = sb(n_("khl"), [P, NG, NT], F16)
    k1 = [sb(n_(f"k1_{i}"), [P, NG, HG, NT], F16) for i in range(2)]
    k2 = [sb(n_(f"k2_{i}"), [P, NG, HG, NT], F16) for i in range(2)]
    q1 = [sb(n_(f"q1_{i}"), [P, NG, NT], F16) for i in range(2)]
    ql = sb(n_("ql"), [P, NG, NT], F16)
    q2 = [sb(n_(f"q2_{i}"), [P, NG, NT], F16) for i in range(2)]
    vaug = [sb(n_(f"v{i}"), [P, 2, HEADS, 32], F32) for i in range(2)]
    nmax = sb(n_("nmax"), [P, 2, NG * P], F16)
    probs = [sb(n_(f"p{i}"), [P, HG, NT], F32) for i in range(2)]
    osb = [sb(n_(f"o{i}"), [P, NG, NT], F32) for i in range(2)]
    rsum = sb(n_("rsum"), [P, 2, HEADS], F32)
    otok = sb(n_("otok"), [P, 2, 256], F32)
    oh = sb(n_("oh"), [P, 2, NT], F16)
    ol = sb(n_("ol"), [P, NT], F16)
    r = sb(n_("r"), [P, 2, E], F32)
    st6 = sb(n_("st6"), [P, 2, 6], F32)
    mv = sb(n_("mv"), [P, 2, 2], F32)
    ve = sb(n_("ve"), [P, 2], F32)
    rstd = sb(n_("rstd"), [P, 2], F32)
    mhalf = sb(n_("mhalf"), [P, 2], F32)
    hout = [sb(n_(f"h{i}"), [P, 2, E], F32) for i in range(2)]
    bk_lo = sb(n_("bk_lo"), [P, NG], F32)
    if not L0:
        sctok = sb(n_("sctok"), [P, 2, 256], F32)
        k1s = sb(n_("k1s"), [P, NG, HG, NSC], F16)
        k2s = sb(n_("k2s"), [P, NG, HG, NSC], F16)
        vs = sb(n_("vs"), [P, 2, HEADS, 32], F32)
    F = [pb(n_(f"F{i}"), [P, 512], F32) for i in range(3)]
    S = [pb(n_(f"S{i}"), [P, 2, NT], F32) for i in range(2)]
    O = pb(n_("O"), [P, NT], F32)
    C = [pb(n_(f"C{i}"), [P, 512], F32) for i in range(2)]

    qtiles = token_tiles(NT)
    maxes = [(tt, g, pr) for tt in range(2) for g in range(NG) for pr in (range(2) if L0 else range(HG))]
    jobs = [("h0", 0), ("h0", 1)] if L0 else []
    jobs += [("xT",)] + [("K", g) for g in range(NG)] + [("Q", g) for g in range(NG)] + [("V",)]
    jobs += [("max", *m) for m in maxes] + [("nmaxT",)]
    J = -(-len(jobs) // 3) * 3
    pad = J - len(jobs)
    job_at = {j: n for n, j in enumerate(jobs)}
    JS = 6
    sjobs = [] if L0 else [("xT",)] + [("K", g) for g in range(NG)] + [("V",)]
    spad = 0 if L0 else JS - len(sjobs)
    base = 0 if L0 else JS
    cx = 0 if L0 else 1

    def plan(front, core, tail):
        fj = list(jobs) if front else []
        out = []
        tails = {0: ["divide"], NK: ["oT"], 2 * NK: ["oproj"], 3 * NK - 1: ["norm"]} if tail else {}
        slots = SLOTS if core else 1
        for n in range(slots):
            if core:
                out.append(("scores", n))
            take = -(-len(fj) // (slots - n))
            for m in range(take):
                out.append(("job", fj.pop(0)))
            if core and n > 0:
                out.append(("pv", n - 1))
            if core:
                out += [("tail", x) for x in tails.get(n, [])]
        if core:
            out.append(("pv", slots - 1))
        elif tail:
            out += [("tail", x) for x in ("divide", "oT", "oproj", "norm")]
        return out

    loaded = [sem(n_(f"loaded{i}")) for i in range(2)]
    job_done = sem(n_("job_done"))
    job_read = sem(n_("job_read"))
    hi_ready = sem(n_("hi_ready"))
    k_ready = sem(n_("k_ready"))
    scores_done = sem(n_("scores_done"))
    probs_ready = sem(n_("probs_ready"))
    pv_done = sem(n_("pv_done"))
    o_ready = sem(n_("o_ready"))
    div_done = sem(n_("div_done"))
    rec_ready = sem(n_("rec_ready"))
    otok_ready = sem(n_("otok_ready"))
    oT_done = sem(n_("oT_done"))
    oh_ready = sem(n_("oh_ready"))
    ol_ready = sem(n_("ol_ready"))
    oproj_done = sem(n_("oproj_done"))
    xres_ready = sem(n_("xres_ready"))
    r_ready = sem(n_("r_ready"))
    st_ready = sem(n_("st_ready"))
    rstd_ready = sem(n_("rstd_ready"))
    h_ready = sem(n_("h_ready"))
    stored = [sem(n_(f"stored{i}")) for i in range(2)]
    const_ready = sem(n_("const_ready"))
    bias_ready = sem(n_("bias_ready"))
    MX = len(maxes)

    def nth(t, job):
        if isinstance(t, int) and t < 0:
            return sjobs.index(job) + 1 if t == -1 and job in sjobs else 0
        return base + t * J + job_at[job] + 1

    last_q, last_tok = ("Q", NG - 1), ("h0", 1)

    def loads_until(t, i):
        half = t // 2 if isinstance(t, int) else (t - i) // 2
        return 16 * ((1 if not L0 and i == 0 else 0) + DL * (half + 1))

    def run(eng, body):
        run_steps(eng, NB, body)

    DL = 1 if L0 else 4
    rows = lambda d, t: d[bass.ds(t * NT, P), :] if not isinstance(t, int) else d[t * NT:t * NT + P, :]
    rows1 = lambda d, t: (d[bass.ds(t * NT + P, T1), :] if not isinstance(t, int)
                          else d[t * NT + P:t * NT + NT, :])

    with nc.Block() as block:

        @block.sync
        def _(sp):
            if not L0:
                sp.dma_start(sctok[:, :, :], W["sc_d"]).then_inc(loaded[0], 16)
                sp.wait_ge(loaded[0], 16)
            def load(t, i):
                if L0:
                    src = W["xp_d"][:, bass.ds(t, 1)] if not isinstance(t, int) else W["xp_d"][:, t:t + 1]
                    sp.dma_start(patches[i][:, :, :], src.rearrange("p a k t -> p (a k) t")).then_inc(loaded[i], 16)
                else:
                    a, b = rows(src_d, t), rows1(src_d, t)
                    sp.dma_start(xtok[i][:, 0, 0:E], a).then_inc(loaded[i], 16)
                    sp.dma_start(xtok[i][:, 0, E:256], a[:, EA:E]).then_inc(loaded[i], 16)
                    sp.dma_start(xtok[i][0:T1, 1, 0:E], b).then_inc(loaded[i], 16)
                    sp.dma_start(xtok[i][0:T1, 1, E:256], b[:, EA:E]).then_inc(loaded[i], 16)

            def step(t, i, more, tail):
                j = 1 - i
                if more:
                    if L0:
                        sp.wait_ge(job_done, nth(t, last_tok))
                    else:
                        sp.wait_ge(xres_ready, t + 1)
                        sp.wait_ge(job_done, nth(t, ("xT",)))
                    load(t + 2, i)
                if tail:
                    sp.wait_ge(h_ready, 2 * t)
                    sp.dma_start(rows(dst_d, t - 1), hout[j][:, 0, :]).then_inc(stored[j], 16)
                    sp.dma_start(rows1(dst_d, t - 1), hout[j][0:T1, 1, :]).then_inc(stored[j], 16)

            load(0, 0)
            load(1, 1)
            step(0, 0, NB > 2, False)
            if NB > 4:
                with sp.Fori(0, (NB - 4) // 2) as pair:
                    step(pair * 2 + 1, 1, True, True)
                    step(pair * 2 + 2, 0, True, True)
            for t in range(max(1, NB - 3), NB + 1):
                step(t, t % 2, t + 2 < NB, True)
            for i in range(2):
                sp.wait_ge(stored[i], 32 * (NB // 2))

        @block.tensor
        def _(pe):
            def bank_of(n):
                return F[n % 3]

            pe.wait_ge(const_ready, 1)

            def front_job(job, n, t, i, count, buffers, ntok, ctx=False):
                xt, xhi, xlo = buffers
                bank = bank_of(n)
                kind = job[0]
                tiles = token_tiles(ntok)
                wait(pe, job_read, count - 2)
                img = t + cx
                if kind == "h0":
                    if job[1] == 0:
                        pe.wait_ge(loaded[i], loads_until(t, i))
                    t0, m = tiles[job[1]]
                    for k in range(KD):
                        ins = nc.tensor.matmul(bank[0:m, 0:E], patches[i][:, k, t0:t0 + m], W["wtok"][:, k, :],
                                               start=k == 0, stop=k == KD - 1)
                elif kind == "xT":
                    if L0:
                        pe.wait_ge(job_read, nth(t, last_tok))
                    elif not ctx:
                        pe.wait_ge(loaded[i], loads_until(t, i))
                    else:
                        pe.wait_ge(loaded[0], 16)
                    for f, col in ((0, 0), (EA, ntok)):
                        for tt, (t0, m) in enumerate(tiles):
                            ins = nc.tensor.transpose(bank[:, col + t0:col + t0 + m], xt[0:m, tt, f:f + P],
                                                      ident[0:m, 0:m])
                elif kind in "KQ":
                    if kind == "K" and job[1] == 0:
                        pe.wait_ge(job_read, nth(t, ("xT",)))
                    cols = kcol(job[1]) if kind == "K" else qcol(job[1])
                    ins = five_passes(nc, bank[:, 0:ntok], xhi, xlo, wh, wl, cols, slice(0, ntok), False)
                elif kind == "V":
                    for tt, (t0, m) in enumerate(tiles):
                        ins = v_passes(bank[0:m, tt * E:tt * E + E], xhi, xlo, slice(t0, t0 + m), vcol, tt)
                elif kind == "max":
                    _, tt, g, pr = job
                    t0, m = tiles[tt]
                    if tt == 0 and pr == 0:
                        pe.wait_ge(k_ready, 3 * img + g + 1)
                        pe.wait_ge(hi_ready, 7 * t + 5 + g + 4 * cx)
                    q = q1[i][:, g, t0:t0 + m]
                    if L0:
                        ins = nc.tensor.matmul(bank[0:m, 0:2 * NT].rearrange("p (h k) -> p h k", h=2), q,
                                               k1[i][:, g, 2 * pr:2 * pr + 2, :], start=True, stop=True)
                    else:
                        nc.tensor.matmul(bank[0:m, 0:NT], q, k1[i][:, g, pr, :], start=True, stop=True)
                        ins = nc.tensor.matmul(bank[0:m, NT:NKEYS], q, k1s[:, g, pr, :], start=True, stop=True)
                else:
                    pe.wait_ge(job_read, nth(t, ("max", *maxes[-1])))
                    b16 = bank[:, 0:NG * P].bitcast(F16)
                    for g in range(NG):
                        for tt, (t0, m) in enumerate(tiles):
                            ins = nc.tensor.transpose(b16[:, 2 * P * g + t0:2 * P * g + t0 + m + m % 2],
                                                      nmax[0:m + m % 2, tt, P * g:P * g + P],
                                                      ident16[0:m + m % 2, 0:m + m % 2])
                return ins

            def v_passes(out, xhi, xlo, tok, cols, tt):
                pairs = [(xhi[:, 0, tok], wh[:, 0, cols]), (xlo[:, tok], wh[:, 0, cols]),
                         (xhi[:, 0, tok], wl[:, 0, cols]), (xhi[:, 1, tok], wh[:, 1, cols]),
                         (xhi[:, 1, tok], wl[:, 1, cols])]
                for n, (l, rr) in enumerate(pairs):
                    ins = nc.tensor.matmul(out, l, rr, start=n == 0 and tt == 0, stop=n == 4,
                                           skip_group_check=True)
                return ins

            if not L0:
                for n, job in enumerate(sjobs):
                    ins = front_job(job, n, -1, 0, n, (sctok, xh[1], xl[1]), NSC, ctx=True)
                    ins.then_inc(job_done, 1 + (spad if n == len(sjobs) - 1 else 0))

            def body(t, i, front, core, tail):
                j = 1 - i
                for step in plan(front, core, tail):
                    if step[0] == "job":
                        job = step[1]
                        n = job_at[job]
                        ins = front_job(job, n, t + 1, j, base + (t + 1) * J + n, (xtok[j], xh[j], xl[j]), NT)
                        ins.then_inc(job_done, 1 + (pad if n == len(jobs) - 1 else 0))
                    elif step[0] == "scores":
                        n = step[1]
                        g, (src, kt, m) = n // NK, ktiles[n % NK]
                        ka, kb = (k1[i], k2[i]) if src == "own" else (k1s, k2s)
                        if n == 0:
                            pe.wait_ge(job_read, nth(t, ("nmaxT",)))
                        for pr in range(2):
                            wait(pe, probs_ready, 2 * (t * SLOTS + n) - 1 + pr)
                            for hh in range(2):
                                h = 2 * pr + hh
                                keys = slice(kt * P, kt * P + m)
                                nc.tensor.matmul(S[pr][0:m, hh, :], ka[:, g, h, keys], q1[i][:, g, :],
                                                 start=hh == 0, stop=False, skip_group_check=True)
                                ins = nc.tensor.matmul(S[pr][0:m, hh, :], kb[:, g, h, keys], q2[i][:, g, :],
                                                       start=False, stop=True, skip_group_check=True)
                            ins.then_inc(scores_done, 1)
                    elif step[0] == "pv":
                        n = step[1]
                        g, (src, kt, m) = n // NK, ktiles[n % NK]
                        v = vaug[i] if src == "own" else vs
                        pe.wait_ge(probs_ready, 2 * (t * SLOTS + n) + 2)
                        if n % NK == 0:
                            wait(pe, o_ready, 3 * t + g)
                        for h in range(HG):
                            ins = nc.tensor.matmul(O[32 * h:32 * h + 32, :], v[0:m, kt, HG * g + h, :],
                                                   probs[n % 2][0:m, h, :], start=n % NK == 0, stop=n % NK == NK - 1)
                        ins.then_inc(pv_done, 1)
                    elif step[1] == "divide":
                        pe.wait_ge(o_ready, 3 * t)
                        for tt, (t0, m) in enumerate(qtiles):
                            wait(pe, ol_ready if tt == 0 else r_ready, (t - 1) if tt == 0 else 2 * (t - 1))
                            for g in range(NG):
                                ins = nc.tensor.transpose(C[tt][0:m, P * g:P * g + P], osb[j][:, g, t0:t0 + m],
                                                          ident[:, :])
                            ins.then_inc(div_done, 1)
                    elif step[1] == "oT":
                        pe.wait_ge(otok_ready, 2 * t)
                        for f, col in ((0, 0), (EA, NT)):
                            for tt, (t0, m) in enumerate(qtiles):
                                ins = nc.tensor.transpose(C[0][:, col + t0:col + t0 + m], otok[0:m, tt, f:f + P],
                                                          ident[0:m, 0:m])
                        ins.then_inc(oT_done, 1)
                    elif step[1] == "oproj":
                        pe.wait_ge(ol_ready, t)
                        for tt, (t0, m) in enumerate(qtiles):
                            ins = v_passes(C[1][0:m, tt * E:tt * E + E], oh, ol, slice(t0, t0 + m), ocol, tt)
                        ins.then_inc(oproj_done, 1)

            run(pe, body)

        @block.scalar
        def _(act):
            def front(job, t, i, count, xhi, ntok, ctx=False):
                kind, bank = job[0], F[(job_at[job] if not ctx else sjobs.index(job)) % 3]
                if kind == "xT":
                    act.wait_ge(job_done, count + 1)
                    src = bank[:, 0:2 * ntok].rearrange("p (a t) -> p a t", a=2)
                    nc.scalar.activation(xhi[:, :, 0:ntok], src, ACT.Copy).then_inc(hi_ready, 1)
                elif kind == "K":
                    g = job[1]
                    act.wait_ge(job_done, count + 1)
                    if g == 0:
                        wait(act, job_read, nth(t - 1, ("K", NG - 1)))
                    nc.scalar.activation(khi[:, g, 0:ntok], bank[:, 0:ntok], ACT.Identity,
                                         bias=bk_lo[:, g:g + 1],
                                         scale=masks[:, C_LO:C_LO + 1]).then_inc(hi_ready, 1)
                elif kind == "Q":
                    g = job[1]
                    act.wait_ge(job_done, count + 1)
                    nc.scalar.activation(q1[i][:, g, :], bank[:, 0:NT], ACT.Identity,
                                         bias=W["bqk"][:, g:g + 1]).then_inc(hi_ready, 1)

            act.wait_ge(bias_ready, 1)
            if not L0:
                for n, job in enumerate(sjobs):
                    front(job, -1, 0, n, xh[1], NSC, ctx=True)

            def body(t, i, has_front, core, tail):
                j = 1 - i

                def copy_out(n):
                    act.wait_ge(pv_done, t * SLOTS + n + 1)
                    nc.scalar.activation(osb[i][:, n // NK, :], O[:, :], ACT.Copy).then_inc(o_ready, 1)

                for step in plan(has_front, core, tail):
                    if step[0] == "job":
                        front(step[1], t + 1, j, base + (t + 1) * J + job_at[step[1]], xh[j], NT)
                    elif step[0] == "scores":
                        n = step[1]
                        m = ktiles[n % NK][2]
                        for pr in range(2):
                            act.wait_ge(scores_done, 2 * (t * SLOTS + n) + pr + 1)
                            if pr == 0:
                                wait(act, pv_done, t * SLOTS + n - 1)
                            nc.scalar.activation(probs[n % 2][0:m, 2 * pr:2 * pr + 2, :], S[pr][0:m, :, :], ACT.Exp,
                                                 scale=scale).then_inc(probs_ready, 1)
                    elif step[0] == "pv":
                        if step[1] % NK == NK - 1:
                            copy_out(step[1])
                    elif step[1] == "oT":
                        act.wait_ge(oT_done, t)
                        src = C[0][:, 0:2 * NT].rearrange("p (a t) -> p a t", a=2)
                        wait(act, oproj_done, t - 1)
                        nc.scalar.activation(oh[:, :, :], src, ACT.Copy).then_inc(oh_ready, 1)

            run(act, body)

        @block.vector
        def _(dve):
            def front(job, t, i, count, buffers, ntok, kd, vd, ctx=False):
                xhi, xlo = buffers
                kind = job[0]
                n = job_at[job] if not ctx else sjobs.index(job)
                total, extra = (len(jobs), pad) if not ctx else (len(sjobs), spad)
                bank = F[n % 3]
                inc = 1 + (extra if n == total - 1 else 0)
                img = t + cx if not ctx else 0
                hbase = 7 * t + 4 * cx if not ctx else 0
                tiles = token_tiles(ntok)
                if kind == "h0":
                    tt = job[1]
                    t0, m = tiles[tt]
                    dve.wait_ge(job_done, count + 1)
                    wait(dve, xres_ready, t - 1)
                    nc.vector.tensor_tensor(xtok[i][0:m, tt, 0:E], bank[0:m, 0:E], W["addend"][0:m, tt, :], ALU.add)
                    nc.vector.tensor_tensor(xtok[i][0:m, tt, E:256], bank[0:m, EA:E], W["addend"][0:m, tt, EA:E],
                                            ALU.add).then_inc(job_read, 1)
                elif kind == "xT":
                    dve.wait_ge(hi_ready, hbase + 1)
                    nc.vector.tensor_tensor(xlo[:, 0:ntok], bank[:, 0:ntok], xhi[:, 0, 0:ntok], ALU.subtract)
                    nc.vector.tensor_tensor(xhi[EB:P, 1, 0:ntok], bank[EB:P, ntok:2 * ntok], xhi[EB:P, 1, 0:ntok],
                                            ALU.subtract).then_inc(job_read, 1)
                elif kind == "K":
                    g = job[1]
                    dve.wait_ge(hi_ready, hbase + 2 + g)
                    wait(dve, k_ready, 3 * (img - 1) + g + 1)
                    nc.vector.scalar_tensor_tensor(khl[:, g, 0:ntok], bank[:, 0:ntok],
                                                   W["bqk"][:, NG + g:NG + g + 1], khi[:, g, 0:ntok],
                                                   ALU.add, ALU.subtract).then_inc(job_read, 1)
                elif kind == "Q":
                    g = job[1]
                    dve.wait_ge(hi_ready, hbase + 5 + g)
                    nc.vector.scalar_tensor_tensor(ql[:, g, :], bank[:, 0:NT], W["bqk"][:, g:g + 1], q1[i][:, g, :],
                                                   ALU.add, ALU.subtract).then_inc(job_read, 1)
                elif kind == "V":
                    dve.wait_ge(job_done, count + 1)
                    for tt, (t0, m) in enumerate(tiles):
                        src = bank[0:m, tt * E:tt * E + E].rearrange("p (h d) -> p h d", h=HEADS)
                        bv = W["bv"][0:m, :].rearrange("p (h d) -> p h d", h=HEADS)
                        ins = nc.vector.tensor_tensor(vd[0:m, tt, :, 0:HD], src, bv, ALU.add)
                    ins.then_inc(job_read, inc)
                elif kind == "max":
                    _, tt, g, pr = job
                    m = tiles[tt][1]
                    dve.wait_ge(job_done, count + 1)
                    if L0:
                        src = bank[0:m, 0:2 * NT].rearrange("p (h k) -> p h k", h=2)
                        out = nmax[0:m, tt, P * g + 64 * pr:P * g + 64 * pr + 64].rearrange(
                            "p (h c) -> p h c", h=2)[:, :, HD]
                    else:
                        src = bank[0:m, 0:NKEYS]
                        out = nmax[0:m, tt, P * g + 32 * pr + HD:P * g + 32 * pr + HD + 1]
                    with nc.allow_low_precision("a shift of the exponent, the same for all keys"):
                        nc.vector.tensor_reduce(out=out, in_=src, op=ALU.max, axis=AX.X,
                                                negate=True).then_inc(job_read, 1)
                else:
                    dve.wait_ge(job_done, count + 1)
                    dve.wait_ge(job_read, nth(t, last_q))
                    b16 = bank[:, 0:NG * P].bitcast(F16)
                    for g in range(NG):
                        ins = nc.vector.scalar_tensor_tensor(q2[i][:, g, :], ql[:, g, :], masks[:, C_HI:C_HI + 1],
                                                             b16[:, 2 * P * g:2 * P * g + NT], ALU.mult, ALU.add)
                    ins.then_inc(job_read, inc)

            nc.vector.tensor_scalar(bk_lo[:, :], W["bqk"][:, NG:2 * NG], masks[:, C_LO:C_LO + 1], None,
                                    ALU.mult).then_inc(bias_ready, 1)
            dve.wait_ge(const_ready, 1)
            if not L0:
                for n, job in enumerate(sjobs):
                    front(job, -1, 0, n, (xh[1], xl[1]), NSC, None, vs, ctx=True)

            def body(t, i, has_front, core, tail):
                j = 1 - i
                for step in plan(has_front, core, tail):
                    if step[0] == "job":
                        front(step[1], t + 1, j, base + (t + 1) * J + job_at[step[1]], (xh[j], xl[j]), NT, k1[j],
                              vaug[j])
                    elif step[0] != "tail":
                        continue
                    elif step[1] == "divide":
                        for tt, (t0, m) in enumerate(qtiles):
                            dve.wait_ge(div_done, 2 * (t - 1) + tt + 1)
                            o = C[tt][0:m, 0:NG * P].rearrange("p (h c) -> p h c", h=HEADS)
                            nc.vector.reciprocal(rsum[0:m, tt, :], o[:, :, HD]).then_inc(rec_ready, 1)
                            dve.wait_ge(rec_ready, 2 * (t - 1) + tt + 1)
                            inv = rsum[0:m, tt, :].unsqueeze(2)
                            nc.vector.tensor_tensor(otok[0:m, tt, 0:E].rearrange("p (h d) -> p h d", h=HEADS),
                                                    o[:, :, 0:HD], inv.broadcast_to([m, HEADS, HD]), ALU.mult)
                            nc.vector.tensor_tensor(otok[0:m, tt, E:256].rearrange("p (h d) -> p h d", h=HG),
                                                    o[:, EA // HD:, 0:HD],
                                                    inv[:, EA // HD:].broadcast_to([m, HG, HD]),
                                                    ALU.mult).then_inc(otok_ready, 1)
                    elif step[1] == "oT":
                        dve.wait_ge(oh_ready, t)
                        nc.vector.tensor_tensor(ol[:, :], C[0][:, 0:NT], oh[:, 0, :], ALU.subtract)
                        nc.vector.tensor_tensor(oh[EB:P, 1, :], C[0][EB:P, NT:2 * NT], oh[EB:P, 1, :],
                                                ALU.subtract).then_inc(ol_ready, 1)
                    elif step[1] == "oproj":
                        dve.wait_ge(oproj_done, t)
                        dve.wait_ge(xres_ready, t)
                        wait(dve, h_ready, 2 * (t - 1))
                        for tt, (t0, m) in enumerate(qtiles):
                            nc.vector.tensor_tensor(r[0:m, tt, :], C[1][0:m, tt * E:tt * E + E], xres[j][0:m, tt, :],
                                                    ALU.add).then_inc(r_ready, 1)
                        for tt, (t0, m) in enumerate(qtiles):
                            dve.wait_ge(r_ready, 2 * (t - 1) + tt + 1)
                            nc.vector.bn_stats(st6[0:m, tt, :], r[0:m, tt, :]).then_inc(st_ready, 1)
                        dve.wait_ge(st_ready, 6 * (t - 1) + 2)
                        nc.vector.memset(ve[:, :], 0.0)
                        for tt, (t0, m) in enumerate(qtiles):
                            nc.vector.bn_aggr(mv[0:m, tt, :], st6[0:m, tt, :]).then_inc(st_ready, 1)
                        for tt, (t0, m) in enumerate(qtiles):
                            dve.wait_ge(st_ready, 6 * (t - 1) + tt + 3)
                            nc.vector.tensor_scalar(ve[0:m, tt:tt + 1], mv[0:m, tt, 1:2], EPS, None,
                                                    ALU.add).then_inc(st_ready, 1)
                    elif step[1] == "norm":
                        dve.wait_ge(rstd_ready, 2 * t)
                        wait_stored(t, j)
                        for tt, (t0, m) in enumerate(qtiles):
                            nc.vector.tensor_scalar(hout[j][0:m, tt, :], r[0:m, tt, :], mv[0:m, tt, 0:1],
                                                    rstd[0:m, tt:tt + 1], ALU.subtract, ALU.mult).then_inc(h_ready, 1)

            def wait_stored(t, j):
                if isinstance(t, int):
                    wait(dve, stored[j], 32 * ((t - 1 - j) // 2))
                else:
                    dve.wait_ge(stored[j], (t - 1 - j) * 16)

            run(dve, body)

        @block.gpsimd
        def _(pool):
            pool.memset(nmax[:, :, :], 0.0)
            for v in vaug + ([] if L0 else [vs]):
                pool.memset(v[:, :, :, HD + 1:32], 0.0)
                pool.memset(v[:, :, :, HD:HD + 1], 1.0)
            pool.memset(mhalf[:, :], -0.5).then_inc(const_ready, 1)
            pool.wait_ge(const_ready, 1)

            def mask_keys(g, t, kd1, kd2, ntok):
                pool.wait_ge(job_read, nth(t, ("K", g)))
                for h in range(HG):
                    pool.tensor_tensor(kd1[:, g, h, 0:ntok], khl[:, g, 0:ntok],
                                       masks[:, C_HEAD + h:C_HEAD + h + 1].broadcast_to([P, ntok]), ALU.mult)
                    ins = pool.tensor_scalar(kd2[:, g, h, 0:ntok], khl[:, g, 0:ntok],
                                             masks[:, C_HEADHI + h:C_HEADHI + h + 1],
                                             masks[:, C_HEADONE + h:C_HEADONE + h + 1], ALU.mult, ALU.add)
                ins.then_inc(k_ready, 1)

            if not L0:
                for g in range(NG):
                    mask_keys(g, -1, k1s, k2s, NSC)

            def body(t, i, has_front, core, tail):
                j = 1 - i
                for step in plan(has_front, core, tail):
                    if step[0] == "job" and step[1][0] == "K":
                        mask_keys(step[1][1], t + 1, k1[j], k2[j], NT)
                    elif step[0] == "job" and step[1][0] == "nmaxT":
                        if L0:
                            pool.wait_ge(job_read, nth(t + 1, last_tok))
                        else:
                            pool.wait_ge(loaded[j], loads_until(t + 1, j))
                        wait(pool, r_ready, 2 * t)
                        for tt, (t0, m) in enumerate(qtiles):
                            ins = pool.tensor_tensor(xres[j][0:m, tt, :], xtok[j][0:m, tt, 0:E], W["bo"][0:m, :],
                                                     ALU.add)
                        ins.then_inc(xres_ready, 1)
                    elif step == ("tail", "oproj"):
                        for tt, (t0, m) in enumerate(qtiles):
                            pool.wait_ge(st_ready, 6 * (t - 1) + tt + 5)
                            wait(pool, h_ready, 2 * (t - 1))
                            pool.tensor_tensor(rstd[0:m, tt:tt + 1], ve[0:m, tt:tt + 1], mhalf[0:m, tt:tt + 1],
                                               ALU.pow).then_inc(rstd_ready, 1)

            run(pool, body)


def ffn(nc, layer, NC, src_d, dst_d, W, masks, ident, sem, sb, pb):
    L0 = layer == 0
    NE = NEXP if L0 else 1
    SL = NE * KD
    LAG = 2
    GC = 4 if L0 else 32
    NR = 3
    n_ = lambda s: f"f{layer}_{s}"
    w1h, w1l, w2h, w2l = W["w1h"], W["w1l"], W["w2h"], W["w2l"]

    xtok = [sb(n_(f"xtok{i}"), [P, CT, 256], F32) for i in range(2)]
    xh = [sb(n_(f"xh{i}"), [P, 2, CHUNK], F16) for i in range(2)]
    xl = [sb(n_(f"xl{i}"), [P, CHUNK], F16) for i in range(2)]
    hid = [sb(n_(f"hid{i}"), [P, CHUNK], F32) for i in range(2)]
    hh = [sb(n_(f"hh{i}"), [P, CHUNK], F16) for i in range(3)]
    hl = [sb(n_(f"hl{i}"), [P, CHUNK], F16) for i in range(3)]
    acc = sb(n_("acc"), [P, CT, E], F32)
    ones2 = sb(n_("ones2"), [P, P], F16)
    hout = [sb(n_(f"h{i}"), [P, CT, E], F32) for i in range(2)]
    st6 = sb(n_("st6"), [P, CT, 6], F32)
    mv = sb(n_("mv"), [P, CT, 2], F32)
    ve = sb(n_("ve"), [P, CT], F32)
    rstd = sb(n_("rstd"), [P, CT], F32)
    mhalf = sb(n_("mhalf"), [P, CT], F32)
    lg = sb(n_("lg"), [P, CT, 4], F32)
    top = sb(n_("top"), [P, CT], F32)
    if L0:
        seen = sb(n_("seen"), [P, CT, NEXP + 1], F32)
        chosen = [sb(n_(f"chosen{i}"), [P, CT, NEXP], F32) for i in range(2)]
    else:
        base_e = sb(n_("base_e"), [P, CT, NR], F32)
        pr = sb(n_("pr"), [P, CT, NR], F32)
        den = sb(n_("den"), [P, CT], F32)
        least = sb(n_("least"), [P, CT], F32)
        eq = sb(n_("eq"), [P, CT, NR + 1], F32)
        out_ = sb(n_("out"), [P, CT, NR], F32)
        comb = sb(n_("comb"), [P, CT, NR], F32)
        low = sb(n_("low"), [P, CT, NR * 8], F32)
        lowc = sb(n_("lowc"), [P, CT, 32], F32)
        lowT = [sb(n_(f"lowT{i}"), [32, CHUNK], F32) for i in range(2)]
    U = [pb(n_(f"U{i}"), [P, CHUNK], F32) for i in range(2)]
    Y = [pb(n_(f"Y{i}"), [P, E], F32) for i in range(CT)]
    X = [pb(n_(f"X{i}"), [P, CHUNK], F32) for i in range(2)]
    G = pb(n_("G"), [P, CHUNK], F32)

    loaded = [sem(n_(f"loaded{i}")) for i in range(2)]
    xT_done = sem(n_("xT_done"))
    xh_ready = sem(n_("xh_ready"))
    xl_ready = sem(n_("xl_ready"))
    gate_done = sem(n_("gate_done"))
    gate_step = sem(n_("gate_step"))
    low_ready = sem(n_("low_ready"))
    lowT_done = sem(n_("lowT_done"))
    lowT_ready = sem(n_("lowT_ready"))
    up_done = sem(n_("up_done"))
    gelu_done = sem(n_("gelu_done"))
    hh_ready = sem(n_("hh_ready"))
    hl_ready = sem(n_("hl_ready"))
    down_done = sem(n_("down_done"))
    y_done = sem(n_("y_done"))
    y_read = sem(n_("y_read"))
    st_ready = sem(n_("st_ready"))
    rstd_ready = sem(n_("rstd_ready"))
    h_ready = sem(n_("h_ready"))
    stored = [sem(n_(f"stored{i}")) for i in range(2)]
    const_ready = sem(n_("const_ready"))
    GS = 7 if L0 else 19
    NS = 2 * CT + 1
    FRONT = 3
    LOWT = 4

    def loads_until(t, i):
        half = t // 2 if isinstance(t, int) else (t - i) // 2
        return 32 * (half + 1)

    def tok_view(d, t):
        s = slice(t * CHUNK, t * CHUNK + CHUNK) if isinstance(t, int) else bass.ds(t * CHUNK, CHUNK)
        return d[s, :].rearrange("(c p) f -> p c f", c=CT)

    def run(eng, body):
        run_steps(eng, NC, body)

    def carried(t, n, core, tail):
        if n >= LAG:
            return (t, n - LAG) if core else None
        return (t - 1, SL - LAG + n) if tail else None

    with nc.Block() as block:

        @block.sync
        def _(sp):
            def body(t, i, front, core, tail):
                j = 1 - i
                if front:
                    wait(sp, y_read, CT * NE * t)
                    v = tok_view(src_d, t + 1)
                    sp.dma_start(xtok[j][:, :, 0:E], v).then_inc(loaded[j], 16)
                    sp.dma_start(xtok[j][:, :, E:256], v[:, :, EA:E]).then_inc(loaded[j], 16)
                if tail:
                    sp.wait_ge(h_ready, CT * t)
                    sp.dma_start(tok_view(dst_d, t - 1), hout[j][:, :, :]).then_inc(stored[j], 16)

            run(sp, body)
            for i in range(2):
                sp.wait_ge(stored[i], 16 * ((NC + 1 - i) // 2))

        @block.tensor
        def _(pe):
            pe.wait_ge(const_ready, 1)

            def up(t, i, n):
                wait(pe, gelu_done, t * SL + n - 1)
                if n == 0:
                    pe.wait_ge(xl_ready, 2 * t + 2)
                five_passes(nc, U[n % 2][:, :], xh[i], xl[i], w1h, w1l, slice(n * P, n * P + P),
                            slice(0, CHUNK), False).then_inc(up_done, 1)

            def down(t, i, n):
                e, k = n // KD, n % KD
                pe.wait_ge(hl_ready, t * SL + n + 1)
                hi, lo = hh[n % 3], hl[n % 3]
                if not L0 and k == KD - 1:
                    pe.wait_ge(lowT_ready, t + 1)
                for c in range(CT):
                    tok = slice(c * P, c * P + P)
                    if k == 0:
                        wait(pe, y_read, CT * (t * NE + e) - CT + c + 1)
                        nc.tensor.matmul(Y[c][:, :], ones2[:, :], W["b2"][:, e, :], start=True, stop=False)
                    nc.tensor.matmul(Y[c][:, :], hi[:, tok], w2h[:, n, :], start=False, stop=False)
                    nc.tensor.matmul(Y[c][:, :], hi[:, tok], w2l[:, n, :], start=False, stop=False)
                    ins = nc.tensor.matmul(Y[c][:, :], lo[:, tok], w2h[:, n, :], start=False,
                                           stop=k == KD - 1 and L0)
                    if k == KD - 1:
                        if not L0:
                            ins = nc.tensor.matmul(Y[c][:, :], lowT[i][:, tok], W["wup"][:, :], start=False, stop=True)
                        ins.then_inc(y_done, 1)
                    elif c == CT - 1:
                        ins.then_inc(down_done, 1)

            def transposes(t, i):
                pe.wait_ge(loaded[i], loads_until(t, i))
                for a in range(2):
                    wait(pe, xl_ready, 2 * (t - 1) + a + 1)
                    for c in range(CT):
                        ins = nc.tensor.transpose(X[a][:, c * P:c * P + P], xtok[i][:, c, a * EA:a * EA + P],
                                                  ident[:, :])
                    ins.then_inc(xT_done, 1)

            def body(t, i, front, core, tail):
                j = 1 - i
                for n in range(SL if core else LAG):
                    if core:
                        up(t, i, n)
                    if core and n == 0:
                        wait(pe, gate_step if L0 else lowT_ready, GS * t if L0 else t)
                        for c in range(CT):
                            ins = v5(G[:, c * GC:c * GC + GC], i, slice(c * P, c * P + P), c)
                        ins.then_inc(gate_done, 1)
                    if n == FRONT and front:
                        transposes(t + 1, j)
                    if n == LOWT and not L0:
                        pe.wait_ge(gate_step, GS * (t + 1))
                        for c in range(CT):
                            ins = nc.tensor.transpose(G[0:32, c * P:c * P + P], lowc[:, c, :], ident[:, :])
                        ins.then_inc(lowT_done, 1)
                    if (d := carried(t, n, core, tail)) is not None:
                        down(d[0], i if n >= LAG else j, d[1])

            def v5(out, i, tok, c):
                pairs = [(xh[i][:, 0, tok], W["wgh"][:, 0, :]), (xl[i][:, tok], W["wgh"][:, 0, :]),
                         (xh[i][:, 0, tok], W["wgl"][:, 0, :]), (xh[i][:, 1, tok], W["wgh"][:, 1, :]),
                         (xh[i][:, 1, tok], W["wgl"][:, 1, :])]
                for m, (l, r) in enumerate(pairs):
                    ins = nc.tensor.matmul(out, l, r, start=m == 0 and c == 0, stop=m == 4, skip_group_check=True)
                return ins

            transposes(0, 0)
            def shifted(t, i, front, core, tail):
                if not isinstance(t, int) or t >= 0:
                    body(t, i, front, core, tail)
            run(pe, shifted)

        @block.scalar
        def _(act):
            def split(t, i):
                for a in range(2):
                    act.wait_ge(xT_done, 2 * t + a + 1)
                    nc.scalar.activation(xh[i][:, a, :], X[a][:, :], ACT.Copy).then_inc(xh_ready, 1)

            def body(t, i, front, core, tail):
                j = 1 - i
                if core:
                    for n in range(SL):
                        act.wait_ge(up_done, t * SL + n + 1)
                        wait(act, hl_ready, t * SL + n - 1)
                        nc.scalar.activation(hid[n % 2][:, :], U[n % 2][:, :], ACT.Gelu,
                                             bias=W["b1"][:, n:n + 1]).then_inc(gelu_done, 1)
                        act.wait_ge(gelu_done, t * SL + n + 1)
                        act_free(t, n)
                        nc.scalar.activation(hh[n % 3][:, :], hid[n % 2][:, :], ACT.Copy).then_inc(hh_ready, 1)
                        if n == 0 and not L0:
                            act.wait_ge(gate_done, t + 1)
                            g = G[:, 0:CT * GC].rearrange("p (c k) -> p c k", c=CT)
                            wait(act, gate_step, GS * t)
                            nc.scalar.activation(low[:, :, :], g[:, :, 8:32], ACT.Gelu).then_inc(low_ready, 1)
                        if n == FRONT and front:
                            split(t + 1, j)
                        if n == LOWT and not L0:
                            act.wait_ge(lowT_done, t + 1)
                            nc.scalar.activation(lowT[i][:, :], G[0:32, :], ACT.Copy).then_inc(lowT_ready, 1)

            def act_free(t, n):
                m = t * SL + n - 3
                if isinstance(m, int) and m < 0:
                    return
                k = (n - 3) % KD
                e_before = (n - 3) // KD
                if k == KD - 1:
                    act.wait_ge(y_done, CT * (t * NE + e_before + 1))
                else:
                    act.wait_ge(down_done, (t * NE + e_before) * (KD - 1) + k + 1)

            split(0, 0)
            def shifted(t, i, front, core, tail):
                if not isinstance(t, int) or t >= 0:
                    body(t, i, front, core, tail)
            run(act, shifted)

        @block.vector
        def _(dve):
            def split(t, i):
                for a in range(2):
                    dve.wait_ge(xh_ready, 2 * t + a + 1)
                    if a == 0:
                        nc.vector.tensor_tensor(xl[i][:, :], X[0][:, :], xh[i][:, 0, :], ALU.subtract).then_inc(xl_ready, 1)
                    else:
                        nc.vector.tensor_tensor(xh[i][EB:P, 1, :], X[1][EB:P, :], xh[i][EB:P, 1, :],
                                                ALU.subtract).then_inc(xl_ready, 1)

            def gate(t, i):
                s = [0]

                def then(ins):
                    s[0] += 1
                    ins.then_inc(gate_step, 1)
                    dve.wait_ge(gate_step, GS * t + s[0])

                g = G[:, 0:CT * GC].rearrange("p (c k) -> p c k", c=CT)
                dve.wait_ge(gate_done if L0 else low_ready, t + 1)
                n = NEXP if L0 else NR
                wide = lambda a: a.unsqueeze(2).broadcast_to([P, CT, n])
                bias = W["bg"][:, 0:n].unsqueeze(1).broadcast_to([P, CT, n])
                then(nc.vector.tensor_tensor(lg[:, :, 0:n], g[:, :, 0:n], bias, ALU.add))
                then(nc.vector.tensor_reduce(out=top[:, :], in_=lg[:, :, 0:n], op=ALU.max, axis=AX.X))
                if L0:
                    then(nc.vector.tensor_tensor(seen[:, :, 1:NEXP + 1], lg[:, :, :], wide(top[:, :]), ALU.is_ge))
                    for k in range(2, NEXP + 1):
                        then(nc.vector.tensor_tensor(seen[:, :, k:k + 1], seen[:, :, k:k + 1], seen[:, :, k - 1:k], ALU.max))
                    then(nc.vector.tensor_tensor(chosen[i][:, :, :], seen[:, :, 1:], seen[:, :, 0:NEXP], ALU.subtract))
                    assert s[0] == GS
                    return
                then(nc.vector.tensor_tensor(lg[:, :, 0:n], lg[:, :, 0:n], wide(top[:, :]), ALU.subtract))
                s[0] += 1
                dve.wait_ge(gate_step, GS * t + s[0])
                then(nc.vector.tensor_reduce(out=den[:, :], in_=pr[:, :, :], op=ALU.add, axis=AX.X))
                then(nc.vector.reciprocal(den[:, :], den[:, :]))
                then(nc.vector.tensor_tensor(pr[:, :, :], pr[:, :, :], wide(den[:, :]), ALU.mult))
                then(nc.vector.tensor_reduce(out=least[:, :], in_=pr[:, :, :], op=ALU.min, axis=AX.X))
                then(nc.vector.tensor_tensor(eq[:, :, 0:NR], pr[:, :, :], wide(least[:, :]), ALU.is_le))
                then(nc.vector.tensor_tensor(eq[:, :, 1:2], eq[:, :, 1:2], eq[:, :, 2:3], ALU.max))
                then(nc.vector.memset(eq[:, :, 0:1], 1.0))
                then(nc.vector.tensor_tensor(out_[:, :, :], eq[:, :, 0:NR], eq[:, :, 1:NR + 1], ALU.subtract))
                then(nc.vector.tensor_tensor(out_[:, :, :], out_[:, :, :], pr[:, :, :], ALU.mult))
                then(nc.vector.tensor_tensor(pr[:, :, :], pr[:, :, :], out_[:, :, :], ALU.subtract))
                then(nc.vector.tensor_reduce(out=den[:, :], in_=pr[:, :, :], op=ALU.add, axis=AX.X))
                return s[0]

            def body(t, i, front, core, tail):
                j = 1 - i
                for n in range(SL if core else LAG + 3):
                    if core:
                        dve.wait_ge(hh_ready, t * SL + n + 1)
                        nc.vector.tensor_tensor(hl[n % 3][:, :], hid[n % 2][:, :], hh[n % 3][:, :],
                                                ALU.subtract).then_inc(hl_ready, 1)
                    if core and n == 0:
                        gate_all(t, i)
                    if n == FRONT and front:
                        split(t + 1, j)
                    d = carried(t, n, core, tail)
                    if d is not None and d[1] % KD == KD - 1:
                        combine(d[0], i if n >= LAG else j, d[1] // KD)
                    if tail and n == LAG:
                        stats(t - 1)
                    if tail and n == LAG + 2:
                        dve.wait_ge(rstd_ready, t)
                        wait_stored(t, j)
                        for c in range(CT):
                            nc.vector.tensor_scalar(hout[j][:, c, :], acc[:, c, :], mv[:, c, 0:1], rstd[:, c:c + 1],
                                                    ALU.subtract, ALU.mult).then_inc(h_ready, 1)

            def gate_all(t, i):
                k = gate(t, i)
                if L0:
                    return
                s = [k]

                def then(ins):
                    s[0] += 1
                    ins.then_inc(gate_step, 1)
                    dve.wait_ge(gate_step, GS * t + s[0])

                then(nc.vector.tensor_scalar(den[:, :], den[:, :], 1e-6, None, ALU.add))
                then(nc.vector.reciprocal(den[:, :], den[:, :]))
                then(nc.vector.tensor_tensor(comb[:, :, :], pr[:, :, :],
                                             den[:, :].unsqueeze(2).broadcast_to([P, CT, NR]), ALU.mult))
                then(nc.vector.tensor_tensor(lowc[:, :, 8:32].rearrange("p c (e r) -> p c e r", e=NR),
                                             low[:, :, :].rearrange("p c (e r) -> p c e r", e=NR),
                                             comb[:, :, :].unsqueeze(3).broadcast_to([P, CT, NR, 8]), ALU.mult))
                assert s[0] == GS, s[0]

            def combine(t, i, e):
                if e == 0:
                    wait(dve, h_ready, CT * t)
                for c in range(CT):
                    g = CT * (t * NE + e) + c
                    dve.wait_ge(y_done, g + 1)
                    if not L0:
                        nc.vector.tensor_tensor(acc[:, c, :], Y[c][:, :], xtok[i][:, c, 0:E], ALU.add).then_inc(y_read, 1)
                        continue
                    if e:
                        dve.wait_ge(y_read, g - CT + 1)
                    prev = acc[:, c, :] if e else xtok[i][:, c, 0:E]
                    nc.vector.scalar_tensor_tensor(acc[:, c, :], Y[c][:, :], chosen[i][:, c, e:e + 1], prev,
                                                   ALU.mult, ALU.add).then_inc(y_read, 1)

            def stats(t):
                for c in range(CT):
                    dve.wait_ge(y_read, CT * (t * NE + NE - 1) + c + 1)
                    nc.vector.bn_stats(st6[:, c, :], acc[:, c, :]).then_inc(st_ready, 1)
                dve.wait_ge(st_ready, NS * t + CT)
                nc.vector.memset(ve[:, :], 0.0)
                for c in range(CT):
                    nc.vector.bn_aggr(mv[:, c, :], st6[:, c, :]).then_inc(st_ready, 1)
                dve.wait_ge(st_ready, NS * t + 2 * CT)
                nc.vector.tensor_scalar(ve[:, :], mv[:, :, 1], EPS, None, ALU.add).then_inc(st_ready, 1)

            def wait_stored(t, j):
                if isinstance(t, int):
                    wait(dve, stored[j], 16 * ((t - 1 - j) // 2))
                else:
                    dve.wait_ge(stored[j], (t - 1 - j) * 8)

            dve.wait_ge(const_ready, 1)
            split(0, 0)
            def shifted(t, i, front, core, tail):
                if not isinstance(t, int) or t >= 0:
                    body(t, i, front, core, tail)
            run(dve, shifted)

        @block.gpsimd
        def _(pool):
            pool.memset(mhalf[:, :], -0.5)
            if L0:
                pool.memset(seen[:, :, 0:1], 0.0)
            else:
                pool.memset(base_e[:, :, :], 2.718281828459045)
                pool.memset(lowc[:, :, 0:8], 0.0)
                pool.memset(eq[:, :, NR:NR + 1], 0.0)
            pool.tensor_scalar(ones2[:, :], ident[:, :], 0.0, masks[:, C_ROW01:C_ROW01 + 1], ALU.mult,
                               ALU.add).then_inc(const_ready, 1)

            def body(t, i, front, core, tail):
                if core and not L0:
                    pool.wait_ge(gate_step, GS * t + 3)
                    pool.tensor_tensor(pr[:, :, :], base_e[:, :, :], lg[:, :, 0:NR], ALU.pow).then_inc(gate_step, 1)
                if tail:
                    pool.wait_ge(st_ready, NS * t)
                    pool.tensor_tensor(rstd[:, :], ve[:, :], mhalf[:, :], ALU.pow).then_inc(rstd_ready, 1)

            def shifted(t, i, front, core, tail):
                if not isinstance(t, int) or t >= 0:
                    body(t, i, front, core, tail)
            run(pool, shifted)


def vit_tower(nc, NB, a, out):
    NC = -(-NB * NT // CHUNK)
    TOK = NC * CHUNK
    scratch = [nc.dram_tensor(f"h{n}", (TOK, E), F32, kind="Internal").ap() for n in range(3)]
    flat = lambda t: t[:, :].rearrange("p a -> p a") if len(t.shape) == 2 else t[:, :, :].rearrange("p a b -> p (a b)")
    with ExitStack() as whole:
        keep = lambda name, shape, dt: whole.enter_context(nc.sbuf_tensor("sb_" + name, shape, dt))
        masks, ident, ident16 = keep("masks", [P, C_N], F32), keep("ident", [P, P], F32), keep("ident16", [P, P], F16)
        loads = []

        def halves(name, src, shape, rows=P):
            hi, lo = keep(name + "_hi", shape, F16), keep(name + "_lo", shape, F16)
            size = 1
            for s in shape[1:]:
                size *= s
            loads.append((flat(src), flat(hi), flat(lo), size, rows))
            return hi, lo

        def single(name, src, shape):
            t = keep(name, shape, F32)
            size = 1
            for s in shape[1:]:
                size *= s
            loads.append((flat(src), flat(t), None, size, shape[0]))
            return t

        def two_rows(name, src, shape):
            t = keep(name, shape, F16)
            loads.append((flat(src), flat(t), None, shape[1] * shape[2], P))
            return t

        wa = []
        for n in range(2):
            w = {}
            w["wh"], w["wl"] = halves(f"attn{n}", a[f"wattn{n}"], [P, 2, 2 * NG * P + 2 * E])
            w["bqk"] = single(f"bqk{n}", a[f"bqk{n}"], [P, 2 * NG])
            w["bv"] = single(f"bv{n}", a[f"bv{n}"], [P, E])
            w["bo"] = single(f"bo{n}", a[f"bo{n}"], [P, E])
            wa.append(w)
        wa[0]["wtok"] = single("wtok", a["wtok"], [P, KD, E])
        pos = single("pos", a["pos"], [P, 2, E])
        tokb = single("tokb", a["tokb"], [P, 2, E])
        wa[0]["addend"] = keep("addend", [P, 2, E], F32)
        wa[0]["xp_d"] = a["xp"]
        wa[1]["sc_d"] = a["sc"]
        wf = []
        for n, ne in ((0, NEXP), (1, 1)):
            w = {}
            w["w1h"], w["w1l"] = halves(f"w1_{n}", a[f"w1_{n}"], [P, 2, ne * KD * P])
            w["w2h"], w["w2l"] = halves(f"w2_{n}", a[f"w2_{n}"], [P, ne * KD, E])
            w["b1"] = single(f"b1_{n}", a[f"b1_{n}"], [P, ne * KD])
            w["b2"] = two_rows(f"b2_{n}", a[f"b2_{n}"], [P, ne, E])
            w["wgh"], w["wgl"] = halves(f"wg{n}", a[f"wg{n}"], [P, 2, 4 if n == 0 else 32])
            w["bg"] = single(f"bg{n}", a[f"bg{n}"], [P, 4])
            wf.append(w)
        wf[1]["wup"] = single("wup", a["wup"], [32, E])

        def phase(f, *args):
            with ExitStack() as own:
                sb = lambda name, shape, dt: own.enter_context(nc.sbuf_tensor(name, shape, dt))
                pb = lambda name, shape, dt: own.enter_context(nc.psum_tensor(name, shape, dt))
                sem = lambda name: own.enter_context(nc.semaphore(name))
                f(sem, sb, pb, *args)

        phase(lambda sem, sb, pb: setup(nc, loads, a["consts"], masks, ident, ident16, sem, sb,
                                        (pos, tokb, wa[0]["addend"]), scratch, a["pos"], NB * NT))
        phase(lambda sem, sb, pb: attention(nc, 0, NB, None, scratch[0], wa[0], masks, ident, ident16, sem, sb, pb))
        phase(lambda sem, sb, pb: ffn(nc, 0, NC, scratch[0], scratch[1], wf[0], masks, ident, sem, sb, pb))
        phase(lambda sem, sb, pb: attention(nc, 1, NB, scratch[1], scratch[2], wa[1], masks, ident, ident16, sem, sb, pb))
        phase(lambda sem, sb, pb: ffn(nc, 1, NC, scratch[2], out, wf[1], masks, ident, sem, sb, pb))


def lay_out(inputs, np):
    f = {k: np.asarray(v) for k, v in inputs.items()}
    NB = f["x"].shape[0]
    d = {}
    x = f["x"].reshape(NB, 14, 16, 14, 16, 3).transpose(5, 2, 4, 0, 1, 3).reshape(KD, P, NB, NSC)
    xp = np.zeros((P, NB, KD, NT), np.float32)
    xp[:, :, :, 1:] = x.transpose(1, 2, 0, 3)
    d["xp"] = xp
    d["wtok"] = f["L0_tok_W"].T.reshape(KD, P, E).transpose(1, 0, 2)
    pos = np.zeros((P, 2, E), np.float32)
    pos[:, 0], pos[:T1, 1] = f["L0_tok_pos_embed"][0, :P], f["L0_tok_pos_embed"][0, P:]
    d["pos"] = pos
    tokb = np.broadcast_to(f["L0_tok_b"], (P, 2, E)).copy()
    tokb[0, 0] = f["L0_tok_cls_token"][0, 0]
    d["tokb"] = tokb

    def two_tiles(w):
        return np.stack([w[:EA], np.concatenate([w[EA:], w[EA:]])], 1)

    def heads_twice(w):
        w = w.reshape(*w.shape[:-1], HEADS, 1, HD)
        return np.concatenate([w, w], -2).reshape(*w.shape[:-3], HEADS * 2 * HD)

    for n, (qkv, o) in enumerate((("L0_attn_W_qkv", "L0_attn_W_out"), ("L1_attn_W_qkv", "L1_attn_W_proj"))):
        w = f[qkv]
        d[f"wattn{n}"] = two_tiles(np.concatenate(
            [heads_twice(w[:, :E]), heads_twice(w[:, E:2 * E]), w[:, 2 * E:], f[o]], 1))
    bq = f["L0_attn_b_qkv"]
    b = np.concatenate([heads_twice(bq[:E]), heads_twice(bq[E:2 * E])])
    rows = lambda v: np.broadcast_to(v, (P, v.shape[0]))
    d["bqk0"], d["bqk1"] = b.reshape(2 * NG, P).T, np.zeros((P, 2 * NG), np.float32)
    d["bv0"], d["bv1"] = rows(bq[2 * E:]), np.zeros((P, E), np.float32)
    d["bo0"], d["bo1"] = rows(f["L0_attn_b_out"]), rows(f["L1_attn_b_proj"])
    sc = np.zeros((P, 2, 256), np.float32)
    s = f["L1_attn_sc_token"][0]
    s = np.concatenate([s, s[:, EA:]], 1)
    sc[:, 0], sc[:NSC - P, 1] = s[:P], s[P:]
    d["sc"] = sc

    def two_rows(b):
        out = np.zeros((P, *b.shape), np.float32)
        out[0], out[1] = b, b
        return out

    w1 = f["L0_ffn_W1"].transpose(1, 0, 2).reshape(E, NEXP * KD * P)
    d["w1_0"], d["w1_1"] = two_tiles(w1), two_tiles(f["L1_ffn_w1"])
    d["w2_0"] = f["L0_ffn_W2"].reshape(NEXP * KD, P, E).transpose(1, 0, 2)
    d["w2_1"] = f["L1_ffn_w2"].reshape(KD, P, E).transpose(1, 0, 2)
    d["b1_0"] = f["L0_ffn_b1"].reshape(NEXP * KD, P).T
    d["b1_1"] = f["L1_ffn_b1"].reshape(KD, P).T
    d["b2_0"], d["b2_1"] = two_rows(f["L0_ffn_b2"]), two_rows(f["L1_ffn_b2"][None])
    d["wg0"] = two_tiles(f["L0_ffn_Wg"])
    low = f["L1_ffn_w_down"].transpose(1, 0, 2).reshape(E, 24)
    d["wg1"] = two_tiles(np.concatenate([f["L1_ffn_router_w"], np.zeros((E, 5), np.float32), low], 1))
    d["bg0"] = rows(f["L0_ffn_bg"])
    d["bg1"] = rows(np.concatenate([f["L1_ffn_router_b"], np.zeros(1, np.float32)]))
    wup = np.zeros((32, E), np.float32)
    wup[8:] = f["L1_ffn_w_up"].reshape(24, E)
    d["wup"] = wup
    consts = np.zeros((P, C_N + P), np.float32)
    p = np.arange(P)
    for h in range(HG):
        consts[:, C_HEAD + h] = p // 32 == h
        consts[:, C_HEADHI + h] = (p // 32 == h) & (p % 32 < HD)
        consts[:, C_HEADONE + h] = p == 32 * h + HD
    consts[:, C_LO], consts[:, C_HI] = p % 32 >= HD, p % 32 < HD
    consts[:, C_ROW1], consts[:, C_ROW01] = p == 1, p < 2
    consts[:, C_N:] = np.eye(P)
    d["consts"] = consts
    return {k: np.ascontiguousarray(v) for k, v in d.items()}


def kernel(**inputs):
    import numpy as _np
    import concourse.bacc as _bacc
    from concourse import mybir as _mybir
    from concourse.bass_utils import run_bass_kernel_spmd as _run

    arrays = lay_out(inputs, _np)
    NB = _np.asarray(inputs["x"]).shape[0]
    tokens = -(-NB * NT // CHUNK) * CHUNK
    nc = _bacc.Bacc("TRN2", target_bir_lowering=False, num_devices=1)
    args = {k: nc.dram_tensor(k, v.shape, _mybir.dt.from_np(v.dtype), kind="ExternalInput").ap()
            for k, v in arrays.items()}
    out = nc.dram_tensor("out", (tokens, E), F32, kind="ExternalOutput").ap()
    vit_tower(nc, NB, args, out)
    r = _run(nc, [arrays], core_ids=[0])
    return r.results[0]["out"][:NB * NT].reshape(NB, NT, E)
```

```python
import concourse.bass as bass
from concourse import mybir
from contextlib import ExitStack

F32 = mybir.dt.float32
F16 = mybir.dt.float16
ALU = mybir.AluOpType
ACT = mybir.ActivationFunctionType
AX = mybir.AxisListType

P = 128
E = 192
EA = 128
EB = E - EA
NT = 197
NSC = 196
T1 = NT - P
HEADS, HD = 12, 16
HG = 4
NG = HEADS // HG
KD = 768 // P
NEXP = 4
CT = 3
CHUNK = CT * P
EPS = 1e-5

C_HEAD, C_HEADHI, C_HEADONE, C_LO, C_HI, C_ROW1, C_ROW01, C_N = 0, 4, 8, 12, 13, 14, 15, 16


def wait(eng, semaphore, value):
    if isinstance(value, int) and value <= 0:
        return
    eng.wait_ge(semaphore, value)


def token_tiles(n):
    return [(0, P), (P, n - P)]


def five_passes(nc, out, xh, xl, wh, wl, cols, tok, x_stationary, first=True, last=True):
    pairs = [(xh[:, 0, tok], wh[:, 0, cols]), (xl[:, tok], wh[:, 0, cols]), (xh[:, 0, tok], wl[:, 0, cols]),
             (xh[:, 1, tok], wh[:, 1, cols]), (xh[:, 1, tok], wl[:, 1, cols])]
    for n, (x, w) in enumerate(pairs):
        l, r = (x, w) if x_stationary else (w, x)
        ins = nc.tensor.matmul(out, l, r, start=first and n == 0, stop=last and n == len(pairs) - 1)
    return ins


def run_steps(eng, n, body):
    body(-1, 1, True, False, False)
    body(0, 0, n > 1, True, False)
    pairs = max(0, (n - 2) // 2)
    if pairs:
        with eng.Fori(0, pairs) as pair:
            body(pair * 2 + 1, 1, True, True, True)
            body(pair * 2 + 2, 0, True, True, True)
    for t in range(2 * pairs + 1, n + 1):
        body(t, t % 2, t + 1 < n, t < n, True)


def setup(nc, loads_all, consts_d, masks, ident, ident16, sem, sb, sums, scratch, fill_d, tokens):
    loads = [x for x in loads_all if x[1].dtype == F16]
    stage = [sb("stage0", [P, 6144], F32), sb("stage1", [P, 6144], F32)]
    staged, hi_done, lo_done, const_done = sem("staged"), sem("hi_done"), sem("lo_done"), sem("const_done")
    padded = sem("padded")
    with nc.Block() as block:

        @block.sync
        def _(sp):
            sp.dma_start(masks[:, :], consts_d[:, 0:C_N]).then_inc(const_done, 16)
            sp.dma_start(ident[:, :], consts_d[:, C_N:C_N + P]).then_inc(const_done, 16)
            direct = [x for x in loads_all if x[1].dtype == F32]
            for src, dst, _, _, _ in direct:
                sp.dma_start(dst, src).then_inc(const_done, 16)
            sp.wait_ge(const_done, 32 + 16 * len(direct))
            pads = scratch[0].shape[0] - tokens
            for n, h in enumerate(scratch if pads else []):
                for at in range(tokens, tokens + pads, P):
                    m = min(P, tokens + pads - at)
                    sp.dma_start(h[at:at + m, :], fill_d[0:m, 0, :]).then_inc(padded, 16)
            if pads:
                sp.wait_ge(padded, 16 * len(scratch) * -(-pads // P))
            for n, (src, hi, lo, size, rows) in enumerate(loads):
                if n >= 2:
                    sp.wait_ge(lo_done, n - 1)
                sp.dma_start(stage[n % 2][0:rows, 0:size], src).then_inc(staged, 16)
                sp.wait_ge(staged, 16 * (n + 1))

        @block.scalar
        def _(act):
            act.wait_ge(const_done, 16 * (2 + len(loads_all) - len(loads)))
            nc.scalar.activation(ident16[:, :], ident[:, :], ACT.Copy)
            for n, (src, hi, lo, size, rows) in enumerate(loads):
                act.wait_ge(staged, 16 * (n + 1))
                if lo is None:
                    nc.scalar.activation(hi, stage[n % 2][0:rows, 0:size], ACT.Copy,
                                         scale=masks[:, C_ROW1:C_ROW1 + 1]).then_inc(hi_done, 1)
                else:
                    nc.scalar.activation(hi, stage[n % 2][0:rows, 0:size], ACT.Copy).then_inc(hi_done, 1)

        @block.vector
        def _(dve):
            for n, (src, hi, lo, size, rows) in enumerate(loads):
                dve.wait_ge(hi_done, n + 1)
                target = hi if lo is None else lo
                nc.vector.tensor_tensor(target, stage[n % 2][0:rows, 0:size], hi, ALU.subtract).then_inc(lo_done, 1)
            dve.wait_ge(lo_done, len(loads))
            pos, tokb, addend = sums
            nc.vector.tensor_tensor(addend[:, :, :], pos[:, :, :], tokb[:, :, :], ALU.add)


def attention(nc, layer, NB, src_d, dst_d, W, masks, ident, ident16, sem, sb, pb):
    L0 = layer == 0
    wh, wl = W["wh"], W["wl"]
    qcol = lambda g: slice(P * g, P * g + P)
    kcol = lambda g: slice(NG * P + P * g, NG * P + P * g + P)
    vcol, ocol = slice(2 * NG * P, 2 * NG * P + E), slice(2 * NG * P + E, 2 * NG * P + 2 * E)
    scale = float(E) ** -0.5 if L0 else float(HD) ** -0.5
    ktiles = [("own", 0, P), ("own", 1, T1)] + ([] if L0 else [("ctx", 0, P), ("ctx", 1, NSC - P)])
    NK = len(ktiles)
    SLOTS = NG * NK
    NKEYS = NT if L0 else NT + NSC

    n_ = lambda s: f"a{layer}_{s}"
    xtok = [sb(n_(f"xtok{i}"), [P, 2, 256], F32) for i in range(2)]
    xres = [sb(n_(f"xres{i}"), [P, 2, E], F32) for i in range(2)]
    xh = [sb(n_(f"xh{i}"), [P, 2, NT], F16) for i in range(2)]
    xl = [sb(n_(f"xl{i}"), [P, NT], F16) for i in range(2)]
    patches = [sb(n_(f"patch{i}"), [P, KD, NT], F32) for i in range(2)] if L0 else None
    khi = sb(n_("khi"), [P, NG, NT], F16)
    khl = sb(n_("khl"), [P, NG, NT], F16)
    k1 = [sb(n_(f"k1_{i}"), [P, NG, HG, NT], F16) for i in range(2)]
    k2 = [sb(n_(f"k2_{i}"), [P, NG, HG, NT], F16) for i in range(2)]
    q1 = [sb(n_(f"q1_{i}"), [P, NG, NT], F16) for i in range(2)]
    ql = [sb(n_(f"ql{i}"), [P, NG, NT], F16) for i in range(2)]
    q2 = [sb(n_(f"q2_{i}"), [P, NG, NT], F16) for i in range(2)]
    vaug = [sb(n_(f"v{i}"), [P, 2, HEADS, 32], F32) for i in range(2)]
    nmax = sb(n_("nmax"), [P, 2, NG * P], F16)
    probs = [sb(n_(f"p{i}"), [P, HG, NT], F32) for i in range(2)]
    osb = [sb(n_(f"o{i}"), [P, NG, NT], F32) for i in range(2)]
    rsum = sb(n_("rsum"), [P, 2, HEADS], F32)
    otok = sb(n_("otok"), [P, 2, 256], F32)
    oh = sb(n_("oh"), [P, 2, NT], F16)
    ol = sb(n_("ol"), [P, NT], F16)
    r = sb(n_("r"), [P, 2, E], F32)
    st6 = sb(n_("st6"), [P, 2, 6], F32)
    mv = sb(n_("mv"), [P, 2, 2], F32)
    ve = sb(n_("ve"), [P, 2], F32)
    rstd = sb(n_("rstd"), [P, 2], F32)
    mhalf = sb(n_("mhalf"), [P, 2], F32)
    hout = [sb(n_(f"h{i}"), [P, 2, E], F32) for i in range(2)]
    bk_lo = sb(n_("bk_lo"), [P, NG], F32)
    if not L0:
        sctok = sb(n_("sctok"), [P, 2, 256], F32)
        k1s = sb(n_("k1s"), [P, NG, HG, NSC], F16)
        k2s = sb(n_("k2s"), [P, NG, HG, NSC], F16)
        vs = sb(n_("vs"), [P, 2, HEADS, 32], F32)
    F = [pb(n_(f"F{i}"), [P, 512], F32) for i in range(3)]
    S = [pb(n_(f"S{i}"), [P, 2, NT], F32) for i in range(2)]
    O = pb(n_("O"), [P, NT], F32)
    C = [pb(n_(f"C{i}"), [P, 512], F32) for i in range(2)]

    qtiles = token_tiles(NT)
    K, Q = [("K", g) for g in range(NG)], [("Q", g) for g in range(NG)]
    V, xT, h0, neg = ("V",), ("xT",), [("h0", 0), ("h0", 1)], [("nmaxT", g) for g in range(NG)]
    do, take = (lambda part: ("do", part)), (lambda part: ("take", part))
    if L0:
        mx = [[("max", g, tt, pr) for tt in range(2) for pr in range(2)] for g in range(NG)]
        a, b, c = mx
        by_slot = [[xT, c[0], c[1]],
                   [K[0], Q[0], do("divide"), neg[1], c[2], K[1], take("divide0")],
                   [c[3], Q[1], take("divide1"), K[2], Q[2], V],
                   [do("oT"), neg[2], h0[0], take("oT"), a[0], a[1]],
                   [a[2], do("oproj"), a[3], take("oproj"), take("stats"), h0[1], take("spread"), b[0], neg[0]],
                   [b[1], b[2], b[3], take("norm")]]
        this_image = [*c, neg[1], neg[2]]
    else:
        mx = [[("max", g, tt, pr) for tt in range(2) for pr in range(HG)] for g in range(NG)]
        a, b, c = mx
        by_slot = [[K[0], Q[0], c[3], c[4]],
                   [K[1], Q[1], do("divide"), c[5], take("divide0")],
                   [K[2], Q[2], c[6], take("divide1"), c[7]], [V, neg[2], a[0]], [a[1], do("oT"), a[2], take("oT")],
                   [xT, a[3], a[4]], [a[5], a[6], a[7]], [b[0], neg[0], b[1]],
                   [b[2], do("oproj"), take("oproj")], [b[3], take("stats"), b[4], take("spread"), b[5]],
                   [b[6], b[7], take("norm")], [c[0], neg[1], c[1], c[2]]]
        this_image = [*c[3:], neg[2]]
    jobs = [j for slot in by_slot for j in slot if j[0] not in ("do", "take")]
    job_at = {j: n for n, j in enumerate(jobs)}
    J = -(-len(jobs) // 3) * 3
    splits = [j for j in jobs if j[0] in ("xT", "K", "Q")]

    def ahead(job):
        return 2 if job[0] == ("h0" if L0 else "xT") else 0 if job in this_image else 1

    JS = 6
    sjobs = [] if L0 else [("xT",)] + [("K", g) for g in range(NG)] + [("V",)]
    base = 0 if L0 else JS
    cx = 0 if L0 else 1

    def present(job, flags):
        return flags[2 - ahead(job)]

    def before(job, flags, among):
        return max([n for n, x in enumerate(among[:among.index(job)]) if present(x, flags)], default=-1)

    def amount(job, flags, among, total):
        at = among.index(job)
        last = not any(present(x, flags) for x in among[at + 1:])
        return (total if last else at + 1) - 1 - before(job, flags, among)

    def plan(flags, core, tail, pe=False):
        out = []
        for n in range(SLOTS):
            js = [[("tail", j[1]) if j[0] in ("do", "take") else ("job", j)]
                  if ((j[0] == "do") == pe and tail if j[0] in ("do", "take") else present(j, flags)) else []
                  for j in by_slot[n]]
            pv = [("pv", SLOTS - 1)] if n == 0 and tail else [("pv", n - 1)] if n > 0 and core else []
            scores = [("scores", n, half) for half in range(2)] if core else []
            out += scores[0:1] + js[0] + scores[1:2] + sum(js[1:2], []) + pv + sum(js[2:], [])
        return out

    loaded = [sem(n_(f"loaded{i}")) for i in range(2)]
    job_done = sem(n_("job_done"))
    job_read = sem(n_("job_read"))
    hi_ready = sem(n_("hi_ready"))
    k_ready = sem(n_("k_ready"))
    scores_done = sem(n_("scores_done"))
    probs_ready = sem(n_("probs_ready"))
    pv_done = sem(n_("pv_done"))
    o_ready = sem(n_("o_ready"))
    div_done = sem(n_("div_done"))
    rec_ready = sem(n_("rec_ready"))
    otok_ready = sem(n_("otok_ready"))
    oT_done = sem(n_("oT_done"))
    oh_ready = sem(n_("oh_ready"))
    ol_ready = sem(n_("ol_ready"))
    oproj_done = sem(n_("oproj_done"))
    xres_ready = sem(n_("xres_ready"))
    r_ready = sem(n_("r_ready"))
    st_ready = sem(n_("st_ready"))
    rstd_ready = sem(n_("rstd_ready"))
    h_ready = sem(n_("h_ready"))
    stored = [sem(n_(f"stored{i}")) for i in range(2)]
    const_ready = sem(n_("const_ready"))
    bias_ready = sem(n_("bias_ready"))

    def nth(t, job, among=jobs, total=J):
        if isinstance(t, int) and t < 0:
            return sjobs.index(job) + 1 if t == -1 and job in sjobs else 0
        return base + (t - ahead(job) + 2) * total + among.index(job) + 1

    def nth_hi(t, job):
        if isinstance(t, int) and t < 0:
            return sjobs.index(job) + 1
        return 4 * cx + (t - ahead(job) + ahead(("xT",))) * len(splits) + splits.index(job) + 1

    last_tok = ("h0", 1)
    m_last = lambda g: mx[g][-1]

    def loads_until(t, i):
        half = t // 2 if isinstance(t, int) else (t - i) // 2
        return 16 * ((1 if not L0 and i == 0 else 0) + DL * (half + 1))

    def run(eng, body):
        def one(t):
            body(t, t % 2, (t + 2 < NB, 0 <= t + 1 < NB, 0 <= t < NB), 0 <= t < NB, 1 <= t)

        for t in (-2, -1, 0):
            one(t)
        pairs = max(0, (NB - 3) // 2)
        if pairs:
            with eng.Fori(0, pairs) as pair:
                body(pair * 2 + 1, 1, (True, True, True), True, True)
                body(pair * 2 + 2, 0, (True, True, True), True, True)
        for t in range(2 * pairs + 1, NB + 1):
            one(t)

    DL = 1 if L0 else 4
    rows = lambda d, t: d[bass.ds(t * NT, P), :] if not isinstance(t, int) else d[t * NT:t * NT + P, :]
    rows1 = lambda d, t: (d[bass.ds(t * NT + P, T1), :] if not isinstance(t, int)
                          else d[t * NT + P:t * NT + NT, :])

    with nc.Block() as block:

        @block.sync
        def _(sp):
            if not L0:
                sp.dma_start(sctok[:, :, :], W["sc_d"]).then_inc(loaded[0], 16)
                sp.wait_ge(loaded[0], 16)
            def load(t, i):
                if L0:
                    src = W["xp_d"][:, bass.ds(t, 1)] if not isinstance(t, int) else W["xp_d"][:, t:t + 1]
                    sp.dma_start(patches[i][:, :, :], src.rearrange("p a k t -> p (a k) t")).then_inc(loaded[i], 16)
                else:
                    a, b = rows(src_d, t), rows1(src_d, t)
                    sp.dma_start(xtok[i][:, 0, 0:E], a).then_inc(loaded[i], 16)
                    sp.dma_start(xtok[i][:, 0, E:256], a[:, EA:E]).then_inc(loaded[i], 16)
                    sp.dma_start(xtok[i][0:T1, 1, 0:E], b).then_inc(loaded[i], 16)
                    sp.dma_start(xtok[i][0:T1, 1, E:256], b[:, EA:E]).then_inc(loaded[i], 16)

            def step(t, i, more, tail):
                j = 1 - i
                if more and L0:
                    sp.wait_ge(job_done, nth(t + 1, last_tok))
                    load(t + 3, j)
                elif more:
                    sp.wait_ge(xres_ready, t + 1)
                    sp.wait_ge(job_done, nth(t, ("xT",)))
                    load(t + 2, i)
                if tail:
                    sp.wait_ge(h_ready, 2 * t)
                    sp.dma_start(rows(dst_d, t - 1), hout[j][:, 0, :]).then_inc(stored[j], 16)
                    sp.dma_start(rows1(dst_d, t - 1), hout[j][0:T1, 1, :]).then_inc(stored[j], 16)

            far = 3 if L0 else 2
            load(0, 0)
            load(1, 1)
            if L0 and NB > 2:
                sp.wait_ge(job_done, nth(0, last_tok))
                load(2, 0)
            step(0, 0, far < NB, False)
            pairs = max(0, (NB - far - 1) // 2)
            if pairs:
                with sp.Fori(0, pairs) as pair:
                    step(pair * 2 + 1, 1, True, True)
                    step(pair * 2 + 2, 0, True, True)
            for t in range(2 * pairs + 1, NB + 1):
                step(t, t % 2, t + far < NB, True)
            for i in range(2):
                sp.wait_ge(stored[i], 32 * (NB // 2))

        @block.tensor
        def _(pe):
            def bank_of(n):
                return F[n % 3]

            pe.wait_ge(const_ready, 1)

            def front_job(job, n, t, i, free, buffers, ntok, ctx=False):
                xt, xhi, xlo = buffers
                bank = bank_of(n)
                kind = job[0]
                tiles = token_tiles(ntok)
                wait(pe, job_read, free)
                img = t + cx
                if kind == "h0":
                    if job[1] == 0:
                        pe.wait_ge(loaded[i], loads_until(t, i))
                    t0, m = tiles[job[1]]
                    for k in range(KD):
                        ins = nc.tensor.matmul(bank[0:m, 0:E], patches[i][:, k, t0:t0 + m], W["wtok"][:, k, :],
                                               start=k == 0, stop=k == KD - 1)
                elif kind == "xT":
                    if L0:
                        pe.wait_ge(job_read, nth(t, last_tok))
                    elif not ctx:
                        pe.wait_ge(loaded[i], loads_until(t, i))
                    else:
                        pe.wait_ge(loaded[0], 16)
                    for f, col in ((0, 0), (EA, ntok)):
                        for tt, (t0, m) in enumerate(tiles):
                            ins = nc.tensor.transpose(bank[:, col + t0:col + t0 + m], xt[0:m, tt, f:f + P],
                                                      ident[0:m, 0:m])
                elif kind in "KQ":
                    if kind == "K" and job[1] == 0:
                        pe.wait_ge(job_read, nth(t, ("xT",)))
                    cols = kcol(job[1]) if kind == "K" else qcol(job[1])
                    ins = five_passes(nc, bank[:, 0:ntok], xhi, xlo, wh, wl, cols, slice(0, ntok), False)
                elif kind == "V":
                    for tt, (t0, m) in enumerate(tiles):
                        ins = v_passes(bank[0:m, tt * E:tt * E + E], xhi, xlo, slice(t0, t0 + m), vcol, tt)
                elif kind == "max":
                    _, g, tt, pr = job
                    t0, m = tiles[tt]
                    if tt == 0 and pr == 0:
                        pe.wait_ge(k_ready, 3 * img + g + 1)
                        pe.wait_ge(hi_ready, nth_hi(t, ("Q", g)))
                    q = q1[i][:, g, t0:t0 + m]
                    if L0:
                        ins = nc.tensor.matmul(bank[0:m, 0:2 * NT].rearrange("p (h k) -> p h k", h=2), q,
                                               k1[i][:, g, 2 * pr:2 * pr + 2, :], start=True, stop=True)
                    else:
                        nc.tensor.matmul(bank[0:m, 0:NT], q, k1[i][:, g, pr, :], start=True, stop=True)
                        ins = nc.tensor.matmul(bank[0:m, NT:NKEYS], q, k1s[:, g, pr, :], start=True, stop=True)
                else:
                    g = job[1]
                    pe.wait_ge(job_read, nth(t, m_last(g)))
                    b16 = bank[:, 0:P].bitcast(F16)
                    for tt, (t0, m) in enumerate(tiles):
                        ins = nc.tensor.transpose(b16[:, t0:t0 + m + m % 2], nmax[0:m + m % 2, tt, P * g:P * g + P],
                                                  ident16[0:m + m % 2, 0:m + m % 2])
                return ins

            def v_passes(out, xhi, xlo, tok, cols, tt):
                pairs = [(xhi[:, 0, tok], wh[:, 0, cols]), (xlo[:, tok], wh[:, 0, cols]),
                         (xhi[:, 0, tok], wl[:, 0, cols]), (xhi[:, 1, tok], wh[:, 1, cols]),
                         (xhi[:, 1, tok], wl[:, 1, cols])]
                for n, (l, rr) in enumerate(pairs):
                    ins = nc.tensor.matmul(out, l, rr, start=n == 0 and tt == 0, stop=n == 4,
                                           skip_group_check=True)
                return ins

            if not L0:
                for n, job in enumerate(sjobs):
                    ins = front_job(job, n, -1, 0, n - 2, (sctok, xh[1], xl[1]), NSC, ctx=True)
                    ins.then_inc(job_done, 1 if n < len(sjobs) - 1 else JS - n)

            def body(t, i, flags, core, tail):
                j = 1 - i
                for step in plan(flags, core, tail, pe=True):
                    if step[0] == "job":
                        job = step[1]
                        n, k = job_at[job], j if ahead(job) == 1 else i
                        free = base + (t + 2) * J + min(n - 2, before(job, flags, jobs) + 1)
                        ins = front_job(job, n, t + ahead(job), k, free, (xtok[k], xh[k], xl[k]), NT)
                        ins.then_inc(job_done, amount(job, flags, jobs, J))
                    elif step[0] == "scores":
                        _, n, pr = step
                        g, (src, kt, m) = n // NK, ktiles[n % NK]
                        ka, kb = (k1[i], k2[i]) if src == "own" else (k1s, k2s)
                        if n % NK == 0 and pr == 0:
                            pe.wait_ge(job_read, nth(t, ("nmaxT", g)))
                        wait(pe, probs_ready, 2 * (t * SLOTS + n) - 1 + pr)
                        keys = slice(kt * P, kt * P + m)
                        for hh in range(2):
                            h = 2 * pr + hh
                            nc.tensor.matmul(S[pr][0:m, hh, :], ka[:, g, h, keys], q1[i][:, g, :],
                                             start=hh == 0, stop=False, skip_group_check=True)
                            ins = nc.tensor.matmul(S[pr][0:m, hh, :], kb[:, g, h, keys], q2[i][:, g, :],
                                                   start=False, stop=True, skip_group_check=True)
                        ins.then_inc(scores_done, 1)
                    elif step[0] == "pv":
                        n = step[1]
                        ti, vi = (t, i) if n < SLOTS - 1 else (t - 1, j)
                        g, (src, kt, m) = n // NK, ktiles[n % NK]
                        v = vaug[vi] if src == "own" else vs
                        pe.wait_ge(probs_ready, 2 * (ti * SLOTS + n) + 2)
                        if n % NK == 0:
                            wait(pe, o_ready, 3 * ti + g)
                        for h in range(HG):
                            ins = nc.tensor.matmul(O[32 * h:32 * h + 32, :], v[0:m, kt, HG * g + h, :],
                                                   probs[n % 2][0:m, h, :], start=n % NK == 0, stop=n % NK == NK - 1)
                        ins.then_inc(pv_done, 1)
                    elif step[1] == "divide":
                        pe.wait_ge(o_ready, 3 * t)
                        for tt, (t0, m) in enumerate(qtiles):
                            wait(pe, ol_ready if tt == 0 else r_ready, (t - 1) if tt == 0 else 2 * (t - 1))
                            for g in range(NG):
                                ins = nc.tensor.transpose(C[tt][0:m, P * g:P * g + P], osb[j][:, g, t0:t0 + m],
                                                          ident[:, :])
                            ins.then_inc(div_done, 1)
                    elif step[1] == "oT":
                        pe.wait_ge(otok_ready, 2 * t)
                        for f, col in ((0, 0), (EA, NT)):
                            for tt, (t0, m) in enumerate(qtiles):
                                ins = nc.tensor.transpose(C[0][:, col + t0:col + t0 + m], otok[0:m, tt, f:f + P],
                                                          ident[0:m, 0:m])
                        ins.then_inc(oT_done, 1)
                    elif step[1] == "oproj":
                        pe.wait_ge(ol_ready, t)
                        for tt, (t0, m) in enumerate(qtiles):
                            ins = v_passes(C[1][0:m, tt * E:tt * E + E], oh, ol, slice(t0, t0 + m), ocol, tt)
                        ins.then_inc(oproj_done, 1)

            run(pe, body)

        @block.scalar
        def _(act):
            def front(job, t, i, flags, xhi, ntok, ctx=False):
                kind, bank = job[0], F[(job_at[job] if not ctx else sjobs.index(job)) % 3]
                inc = 1 if ctx else amount(job, flags, splits, len(splits))
                if kind == "xT":
                    act.wait_ge(job_done, nth(t, job))
                    src = bank[:, 0:2 * ntok].rearrange("p (a t) -> p a t", a=2)
                    nc.scalar.activation(xhi[:, :, 0:ntok], src, ACT.Copy).then_inc(hi_ready, inc)
                elif kind == "K":
                    g = job[1]
                    act.wait_ge(job_done, nth(t, job))
                    if g == 0:
                        wait(act, job_read, nth(t - 1, ("K", NG - 1)))
                    nc.scalar.activation(khi[:, g, 0:ntok], bank[:, 0:ntok], ACT.Identity,
                                         bias=bk_lo[:, g:g + 1],
                                         scale=masks[:, C_LO:C_LO + 1]).then_inc(hi_ready, inc)
                elif kind == "Q":
                    g = job[1]
                    act.wait_ge(job_done, nth(t, job))
                    nc.scalar.activation(q1[i][:, g, :], bank[:, 0:NT], ACT.Identity,
                                         bias=W["bqk"][:, g:g + 1]).then_inc(hi_ready, inc)

            act.wait_ge(bias_ready, 1)
            if not L0:
                for job in sjobs[:-1]:
                    front(job, -1, 0, None, xh[1], NSC, ctx=True)

            def body(t, i, flags, core, tail):
                j = 1 - i

                def copy_out(n):
                    ti, oi = (t, i) if n < SLOTS - 1 else (t - 1, j)
                    act.wait_ge(pv_done, ti * SLOTS + n + 1)
                    nc.scalar.activation(osb[oi][:, n // NK, :], O[:, :], ACT.Copy).then_inc(o_ready, 1)

                for step in plan(flags, core, tail):
                    if step[0] == "job":
                        k = j if ahead(step[1]) == 1 else i
                        if step[1] in splits:
                            front(step[1], t + ahead(step[1]), k, flags, xh[k], NT)
                    elif step[0] == "scores":
                        _, n, pr = step
                        m = ktiles[n % NK][2]
                        act.wait_ge(scores_done, 2 * (t * SLOTS + n) + pr + 1)
                        if pr == 0:
                            wait(act, pv_done, t * SLOTS + n - 1)
                        nc.scalar.activation(probs[n % 2][0:m, 2 * pr:2 * pr + 2, :], S[pr][0:m, :, :], ACT.Exp,
                                             scale=scale).then_inc(probs_ready, 1)
                    elif step[0] == "pv":
                        if step[1] % NK == NK - 1:
                            copy_out(step[1])
                    elif step[1] == "oT":
                        act.wait_ge(oT_done, t)
                        src = C[0][:, 0:2 * NT].rearrange("p (a t) -> p a t", a=2)
                        wait(act, oproj_done, t - 1)
                        nc.scalar.activation(oh[:, :, :], src, ACT.Copy).then_inc(oh_ready, 1)

            run(act, body)

        @block.vector
        def _(dve):
            def front(job, t, i, flags, buffers, ntok, vd, ctx=False):
                xhi, xlo = buffers
                kind = job[0]
                n = job_at[job] if not ctx else sjobs.index(job)
                bank = F[n % 3]
                if ctx:
                    inc = 1 if n < len(sjobs) - 1 else JS - n
                else:
                    inc = amount(job, flags, jobs, J)
                img = t + cx
                tiles = token_tiles(ntok)
                if kind == "h0":
                    tt = job[1]
                    t0, m = tiles[tt]
                    dve.wait_ge(job_done, nth(t, job))
                    wait(dve, xres_ready, t - 1)
                    nc.vector.tensor_tensor(xtok[i][0:m, tt, 0:E], bank[0:m, 0:E], W["addend"][0:m, tt, :], ALU.add)
                    nc.vector.tensor_tensor(xtok[i][0:m, tt, E:256], bank[0:m, EA:E], W["addend"][0:m, tt, EA:E],
                                            ALU.add).then_inc(job_read, inc)
                elif kind == "xT":
                    dve.wait_ge(hi_ready, nth_hi(t, job))
                    nc.vector.tensor_tensor(xlo[:, 0:ntok], bank[:, 0:ntok], xhi[:, 0, 0:ntok], ALU.subtract)
                    nc.vector.tensor_tensor(xhi[EB:P, 1, 0:ntok], bank[EB:P, ntok:2 * ntok], xhi[EB:P, 1, 0:ntok],
                                            ALU.subtract).then_inc(job_read, inc)
                elif kind == "K":
                    g = job[1]
                    dve.wait_ge(hi_ready, nth_hi(t, job))
                    wait(dve, k_ready, 3 * (img - 1) + g + 1)
                    nc.vector.scalar_tensor_tensor(khl[:, g, 0:ntok], bank[:, 0:ntok],
                                                   W["bqk"][:, NG + g:NG + g + 1], khi[:, g, 0:ntok],
                                                   ALU.add, ALU.subtract).then_inc(job_read, inc)
                elif kind == "Q":
                    g = job[1]
                    dve.wait_ge(hi_ready, nth_hi(t, job))
                    nc.vector.scalar_tensor_tensor(ql[i][:, g, :], bank[:, 0:NT], W["bqk"][:, g:g + 1], q1[i][:, g, :],
                                                   ALU.add, ALU.subtract).then_inc(job_read, inc)
                elif kind == "V":
                    dve.wait_ge(job_done, nth(t, job))
                    wait(dve, pv_done, (t - 1) * SLOTS)
                    for tt, (t0, m) in enumerate(tiles):
                        src = bank[0:m, tt * E:tt * E + E].rearrange("p (h d) -> p h d", h=HEADS)
                        bv = W["bv"][0:m, :].rearrange("p (h d) -> p h d", h=HEADS)
                        ins = nc.vector.tensor_tensor(vd[0:m, tt, :, 0:HD], src, bv, ALU.add)
                    ins.then_inc(job_read, inc)
                elif kind == "max":
                    _, g, tt, pr = job
                    m = tiles[tt][1]
                    dve.wait_ge(job_done, nth(t, job))
                    if L0:
                        src = bank[0:m, 0:2 * NT].rearrange("p (h k) -> p h k", h=2)
                        out = nmax[0:m, tt, P * g + 64 * pr:P * g + 64 * pr + 64].rearrange(
                            "p (h c) -> p h c", h=2)[:, :, HD]
                    else:
                        src = bank[0:m, 0:NKEYS]
                        out = nmax[0:m, tt, P * g + 32 * pr + HD:P * g + 32 * pr + HD + 1]
                    with nc.allow_low_precision("a shift of the exponent, the same for all keys"):
                        nc.vector.tensor_reduce(out=out, in_=src, op=ALU.max, axis=AX.X,
                                                negate=True).then_inc(job_read, inc)
                else:
                    dve.wait_ge(job_done, nth(t, job))
                    g = job[1]
                    dve.wait_ge(job_read, nth(t, ("Q", g)))
                    ins = nc.vector.scalar_tensor_tensor(q2[i][:, g, :], ql[i][:, g, :], masks[:, C_HI:C_HI + 1],
                                                         bank[:, 0:P].bitcast(F16)[:, 0:NT], ALU.mult, ALU.add)
                    ins.then_inc(job_read, inc)

            nc.vector.tensor_scalar(bk_lo[:, :], W["bqk"][:, NG:2 * NG], masks[:, C_LO:C_LO + 1], None,
                                    ALU.mult).then_inc(bias_ready, 1)
            dve.wait_ge(const_ready, 1)
            if not L0:
                for n, job in enumerate(sjobs):
                    front(job, -1, 0, None, (xh[1], xl[1]), NSC, vs, ctx=True)

            def body(t, i, flags, core, tail):
                j = 1 - i
                for step in plan(flags, core, tail):
                    if step[0] == "job":
                        k = j if ahead(step[1]) == 1 else i
                        front(step[1], t + ahead(step[1]), k, flags, (xh[k], xl[k]), NT, vaug[k])
                    elif step[0] != "tail":
                        continue
                    elif step[1] in ("divide0", "divide1"):
                        for tt, (t0, m) in list(enumerate(qtiles))[int(step[1][-1]):][:1]:
                            dve.wait_ge(div_done, 2 * (t - 1) + tt + 1)
                            o = C[tt][0:m, 0:NG * P].rearrange("p (h c) -> p h c", h=HEADS)
                            nc.vector.reciprocal(rsum[0:m, tt, :], o[:, :, HD]).then_inc(rec_ready, 1)
                            dve.wait_ge(rec_ready, 2 * (t - 1) + tt + 1)
                            inv = rsum[0:m, tt, :].unsqueeze(2)
                            nc.vector.tensor_tensor(otok[0:m, tt, 0:E].rearrange("p (h d) -> p h d", h=HEADS),
                                                    o[:, :, 0:HD], inv.broadcast_to([m, HEADS, HD]), ALU.mult)
                            nc.vector.tensor_tensor(otok[0:m, tt, E:256].rearrange("p (h d) -> p h d", h=HG),
                                                    o[:, EA // HD:, 0:HD],
                                                    inv[:, EA // HD:].broadcast_to([m, HG, HD]),
                                                    ALU.mult).then_inc(otok_ready, 1)
                    elif step[1] == "oT":
                        dve.wait_ge(oh_ready, t)
                        nc.vector.tensor_tensor(ol[:, :], C[0][:, 0:NT], oh[:, 0, :], ALU.subtract)
                        nc.vector.tensor_tensor(oh[EB:P, 1, :], C[0][EB:P, NT:2 * NT], oh[EB:P, 1, :],
                                                ALU.subtract).then_inc(ol_ready, 1)
                    elif step[1] == "oproj":
                        dve.wait_ge(oproj_done, t)
                        dve.wait_ge(xres_ready, t)
                        wait(dve, h_ready, 2 * (t - 1))
                        for tt, (t0, m) in enumerate(qtiles):
                            nc.vector.tensor_tensor(r[0:m, tt, :], C[1][0:m, tt * E:tt * E + E], xres[j][0:m, tt, :],
                                                    ALU.add).then_inc(r_ready, 1)
                    elif step[1] == "stats":
                        for tt, (t0, m) in enumerate(qtiles):
                            dve.wait_ge(r_ready, 2 * (t - 1) + tt + 1)
                            nc.vector.bn_stats(st6[0:m, tt, :], r[0:m, tt, :]).then_inc(st_ready, 1)
                    elif step[1] == "spread":
                        dve.wait_ge(st_ready, 6 * (t - 1) + 2)
                        nc.vector.memset(ve[:, :], 0.0)
                        for tt, (t0, m) in enumerate(qtiles):
                            nc.vector.bn_aggr(mv[0:m, tt, :], st6[0:m, tt, :]).then_inc(st_ready, 1)
                        for tt, (t0, m) in enumerate(qtiles):
                            dve.wait_ge(st_ready, 6 * (t - 1) + tt + 3)
                            nc.vector.tensor_scalar(ve[0:m, tt:tt + 1], mv[0:m, tt, 1:2], EPS, None,
                                                    ALU.add).then_inc(st_ready, 1)
                    elif step[1] == "norm":
                        dve.wait_ge(rstd_ready, 2 * t)
                        wait_stored(t, j)
                        for tt, (t0, m) in enumerate(qtiles):
                            nc.vector.tensor_scalar(hout[j][0:m, tt, :], r[0:m, tt, :], mv[0:m, tt, 0:1],
                                                    rstd[0:m, tt:tt + 1], ALU.subtract, ALU.mult).then_inc(h_ready, 1)

            def wait_stored(t, j):
                if isinstance(t, int):
                    wait(dve, stored[j], 32 * ((t - 1 - j) // 2))
                else:
                    dve.wait_ge(stored[j], (t - 1 - j) * 16)

            run(dve, body)

        @block.gpsimd
        def _(pool):
            pool.memset(nmax[:, :, :], 0.0)
            for v in vaug + ([] if L0 else [vs]):
                pool.memset(v[:, :, :, HD + 1:32], 0.0)
                pool.memset(v[:, :, :, HD:HD + 1], 1.0)
            pool.memset(mhalf[:, :], -0.5).then_inc(const_ready, 1)
            pool.wait_ge(const_ready, 1)

            def mask_keys(g, t, kd1, kd2, ntok):
                pool.wait_ge(job_read, nth(t, ("K", g)))
                for h in range(HG):
                    pool.tensor_tensor(kd1[:, g, h, 0:ntok], khl[:, g, 0:ntok],
                                       masks[:, C_HEAD + h:C_HEAD + h + 1].broadcast_to([P, ntok]), ALU.mult)
                    ins = pool.tensor_scalar(kd2[:, g, h, 0:ntok], khl[:, g, 0:ntok],
                                             masks[:, C_HEADHI + h:C_HEADHI + h + 1],
                                             masks[:, C_HEADONE + h:C_HEADONE + h + 1], ALU.mult, ALU.add)
                ins.then_inc(k_ready, 1)

            if not L0:
                for g in range(NG):
                    mask_keys(g, -1, k1s, k2s, NSC)

            def body(t, i, flags, core, tail):
                j = 1 - i
                for step in plan(flags, core, tail):
                    if step[0] == "job" and step[1][0] == "K":
                        mask_keys(step[1][1], t + 1, k1[j], k2[j], NT)
                    elif step == ("tail", "spread"):
                        for tt, (t0, m) in enumerate(qtiles):
                            pool.wait_ge(st_ready, 6 * (t - 1) + tt + 5)
                            wait(pool, h_ready, 2 * (t - 1))
                            pool.tensor_tensor(rstd[0:m, tt:tt + 1], ve[0:m, tt:tt + 1], mhalf[0:m, tt:tt + 1],
                                               ALU.pow).then_inc(rstd_ready, 1)
                if flags[1]:
                    if L0:
                        pool.wait_ge(job_read, nth(t + 1, last_tok))
                    else:
                        pool.wait_ge(loaded[j], loads_until(t + 1, j))
                    wait(pool, r_ready, 2 * t)
                    for tt, (t0, m) in enumerate(qtiles):
                        ins = pool.tensor_tensor(xres[j][0:m, tt, :], xtok[j][0:m, tt, 0:E], W["bo"][0:m, :],
                                                 ALU.add)
                    ins.then_inc(xres_ready, 1)

            run(pool, body)


def ffn(nc, layer, NC, src_d, dst_d, W, masks, ident, sem, sb, pb):
    L0 = layer == 0
    NE = NEXP if L0 else 1
    SL = NE * KD
    LAG = 2
    GC = 4 if L0 else 32
    NR = 3
    n_ = lambda s: f"f{layer}_{s}"
    w1h, w1l, w2h, w2l = W["w1h"], W["w1l"], W["w2h"], W["w2l"]

    xtok = [sb(n_(f"xtok{i}"), [P, CT, 256], F32) for i in range(2)]
    xh = [sb(n_(f"xh{i}"), [P, 2, CHUNK], F16) for i in range(2)]
    xl = [sb(n_(f"xl{i}"), [P, CHUNK], F16) for i in range(2)]
    hid = [sb(n_(f"hid{i}"), [P, CHUNK], F32) for i in range(2)]
    hh = [sb(n_(f"hh{i}"), [P, CHUNK], F16) for i in range(3)]
    hl = [sb(n_(f"hl{i}"), [P, CHUNK], F16) for i in range(3)]
    acc = sb(n_("acc"), [P, CT, E], F32)
    ones2 = sb(n_("ones2"), [P, P], F16)
    hout = [sb(n_(f"h{i}"), [P, CT, E], F32) for i in range(2)]
    st6 = sb(n_("st6"), [P, CT, 6], F32)
    mv = sb(n_("mv"), [P, CT, 2], F32)
    ve = sb(n_("ve"), [P, CT], F32)
    rstd = sb(n_("rstd"), [P, CT], F32)
    mhalf = sb(n_("mhalf"), [P, CT], F32)
    lg = sb(n_("lg"), [P, CT, 4], F32)
    top = sb(n_("top"), [P, CT], F32)
    if L0:
        seen = sb(n_("seen"), [P, CT, NEXP + 1], F32)
        chosen = [sb(n_(f"chosen{i}"), [P, CT, NEXP], F32) for i in range(2)]
    else:
        base_e = sb(n_("base_e"), [P, CT, NR], F32)
        pr = sb(n_("pr"), [P, CT, NR], F32)
        den = sb(n_("den"), [P, CT], F32)
        least = sb(n_("least"), [P, CT], F32)
        eq = sb(n_("eq"), [P, CT, NR + 1], F32)
        out_ = sb(n_("out"), [P, CT, NR], F32)
        comb = sb(n_("comb"), [P, CT, NR], F32)
        low = sb(n_("low"), [P, CT, NR * 8], F32)
        lowc = sb(n_("lowc"), [P, CT, 32], F32)
        lowT = [sb(n_(f"lowT{i}"), [32, CHUNK], F32) for i in range(2)]
    U = [pb(n_(f"U{i}"), [P, CHUNK], F32) for i in range(2)]
    Y = [pb(n_(f"Y{i}"), [P, E], F32) for i in range(CT)]
    X = [pb(n_(f"X{i}"), [P, CHUNK], F32) for i in range(2)]
    G = pb(n_("G"), [P, CHUNK], F32)

    loaded = [sem(n_(f"loaded{i}")) for i in range(2)]
    xT_done = sem(n_("xT_done"))
    xh_ready = sem(n_("xh_ready"))
    xl_ready = sem(n_("xl_ready"))
    gate_done = sem(n_("gate_done"))
    gate_step = sem(n_("gate_step"))
    low_ready = sem(n_("low_ready"))
    lowT_done = sem(n_("lowT_done"))
    lowT_ready = sem(n_("lowT_ready"))
    up_done = sem(n_("up_done"))
    gelu_done = sem(n_("gelu_done"))
    hh_ready = sem(n_("hh_ready"))
    hl_ready = sem(n_("hl_ready"))
    down_done = sem(n_("down_done"))
    y_done = sem(n_("y_done"))
    y_read = sem(n_("y_read"))
    st_ready = sem(n_("st_ready"))
    rstd_ready = sem(n_("rstd_ready"))
    h_ready = sem(n_("h_ready"))
    stored = [sem(n_(f"stored{i}")) for i in range(2)]
    const_ready = sem(n_("const_ready"))
    GS = 7 if L0 else 19
    NS = 2 * CT + 1
    FRONT = 6 if L0 else 4
    LOWT = 5

    def loads_until(t, i):
        half = t // 2 if isinstance(t, int) else (t - i) // 2
        return 32 * (half + 1)

    def tok_view(d, t):
        s = slice(t * CHUNK, t * CHUNK + CHUNK) if isinstance(t, int) else bass.ds(t * CHUNK, CHUNK)
        return d[s, :].rearrange("(c p) f -> p c f", c=CT)

    def run(eng, body):
        run_steps(eng, NC, body)

    def carried(t, n, core, tail):
        if n >= LAG:
            return (t, n - LAG) if core else None
        return (t - 1, SL - LAG + n) if tail else None

    with nc.Block() as block:

        @block.sync
        def _(sp):
            def body(t, i, front, core, tail):
                j = 1 - i
                if front:
                    wait(sp, y_read, CT * NE * t)
                    v = tok_view(src_d, t + 1)
                    sp.dma_start(xtok[j][:, :, 0:E], v).then_inc(loaded[j], 16)
                    sp.dma_start(xtok[j][:, :, E:256], v[:, :, EA:E]).then_inc(loaded[j], 16)
                if tail:
                    sp.wait_ge(h_ready, CT * t)
                    sp.dma_start(tok_view(dst_d, t - 1), hout[j][:, :, :]).then_inc(stored[j], 16)

            run(sp, body)
            for i in range(2):
                sp.wait_ge(stored[i], 16 * ((NC + 1 - i) // 2))

        @block.tensor
        def _(pe):
            pe.wait_ge(const_ready, 1)

            def up(t, i, n):
                wait(pe, gelu_done, t * SL + n - 1)
                if n == 0:
                    pe.wait_ge(xl_ready, 2 * t + 2)
                five_passes(nc, U[n % 2][:, :], xh[i], xl[i], w1h, w1l, slice(n * P, n * P + P),
                            slice(0, CHUNK), False).then_inc(up_done, 1)

            def down(t, i, n):
                e, k = n // KD, n % KD
                pe.wait_ge(hl_ready, t * SL + n + 1)
                hi, lo = hh[n % 3], hl[n % 3]
                if not L0 and k == KD - 1:
                    pe.wait_ge(lowT_ready, t + 1)
                for c in range(CT):
                    tok = slice(c * P, c * P + P)
                    if k == 0:
                        wait(pe, y_read, CT * (t * NE + e) - CT + c + 1)
                        nc.tensor.matmul(Y[c][:, :], ones2[:, :], W["b2"][:, e, :], start=True, stop=False)
                    nc.tensor.matmul(Y[c][:, :], hi[:, tok], w2h[:, n, :], start=False, stop=False)
                    nc.tensor.matmul(Y[c][:, :], hi[:, tok], w2l[:, n, :], start=False, stop=False)
                    ins = nc.tensor.matmul(Y[c][:, :], lo[:, tok], w2h[:, n, :], start=False,
                                           stop=k == KD - 1 and L0)
                    if k == KD - 1:
                        if not L0:
                            ins = nc.tensor.matmul(Y[c][:, :], lowT[i][:, tok], W["wup"][:, :], start=False, stop=True)
                        ins.then_inc(y_done, 1)
                    elif c == CT - 1:
                        ins.then_inc(down_done, 1)

            def transposes(t, i):
                pe.wait_ge(loaded[i], loads_until(t, i))
                for a in range(2):
                    wait(pe, xl_ready, 2 * (t - 1) + a + 1)
                    for c in range(CT):
                        ins = nc.tensor.transpose(X[a][:, c * P:c * P + P], xtok[i][:, c, a * EA:a * EA + P],
                                                  ident[:, :])
                    ins.then_inc(xT_done, 1)

            def body(t, i, front, core, tail):
                j = 1 - i
                for n in range(SL if core else LAG):
                    if core:
                        up(t, i, n)
                    if core and n == 0:
                        wait(pe, gate_step if L0 else lowT_ready, GS * t if L0 else t)
                        for c in range(CT):
                            ins = v5(G[:, c * GC:c * GC + GC], i, slice(c * P, c * P + P), c)
                        ins.then_inc(gate_done, 1)
                    if n == FRONT and front:
                        transposes(t + 1, j)
                    if n == LOWT and not L0:
                        pe.wait_ge(gate_step, GS * (t + 1))
                        for c in range(CT):
                            ins = nc.tensor.transpose(G[0:32, c * P:c * P + P], lowc[:, c, :], ident[:, :])
                        ins.then_inc(lowT_done, 1)
                    if (d := carried(t, n, core, tail)) is not None:
                        down(d[0], i if n >= LAG else j, d[1])

            def v5(out, i, tok, c):
                pairs = [(xh[i][:, 0, tok], W["wgh"][:, 0, :]), (xl[i][:, tok], W["wgh"][:, 0, :]),
                         (xh[i][:, 0, tok], W["wgl"][:, 0, :]), (xh[i][:, 1, tok], W["wgh"][:, 1, :]),
                         (xh[i][:, 1, tok], W["wgl"][:, 1, :])]
                for m, (l, r) in enumerate(pairs):
                    ins = nc.tensor.matmul(out, l, r, start=m == 0 and c == 0, stop=m == 4, skip_group_check=True)
                return ins

            transposes(0, 0)
            def shifted(t, i, front, core, tail):
                if not isinstance(t, int) or t >= 0:
                    body(t, i, front, core, tail)
            run(pe, shifted)

        @block.scalar
        def _(act):
            def split(t, i):
                for a in range(2):
                    act.wait_ge(xT_done, 2 * t + a + 1)
                    nc.scalar.activation(xh[i][:, a, :], X[a][:, :], ACT.Copy).then_inc(xh_ready, 1)

            def body(t, i, front, core, tail):
                j = 1 - i
                if core:
                    for n in range(SL):
                        act.wait_ge(up_done, t * SL + n + 1)
                        wait(act, hl_ready, t * SL + n - 1)
                        nc.scalar.activation(hid[n % 2][:, :], U[n % 2][:, :], ACT.Gelu,
                                             bias=W["b1"][:, n:n + 1]).then_inc(gelu_done, 1)
                        act.wait_ge(gelu_done, t * SL + n + 1)
                        act_free(t, n)
                        nc.scalar.activation(hh[n % 3][:, :], hid[n % 2][:, :], ACT.Copy).then_inc(hh_ready, 1)
                        if n == 0 and not L0:
                            act.wait_ge(gate_done, t + 1)
                            g = G[:, 0:CT * GC].rearrange("p (c k) -> p c k", c=CT)
                            wait(act, gate_step, GS * t)
                            nc.scalar.activation(low[:, :, :], g[:, :, 8:32], ACT.Gelu).then_inc(low_ready, 1)
                        if n == FRONT and front:
                            split(t + 1, j)
                        if n == LOWT and not L0:
                            act.wait_ge(lowT_done, t + 1)
                            nc.scalar.activation(lowT[i][:, :], G[0:32, :], ACT.Copy).then_inc(lowT_ready, 1)

            def act_free(t, n):
                m = t * SL + n - 3
                if isinstance(m, int) and m < 0:
                    return
                k = (n - 3) % KD
                e_before = (n - 3) // KD
                if k == KD - 1:
                    act.wait_ge(y_done, CT * (t * NE + e_before + 1))
                else:
                    act.wait_ge(down_done, (t * NE + e_before) * (KD - 1) + k + 1)

            split(0, 0)
            def shifted(t, i, front, core, tail):
                if not isinstance(t, int) or t >= 0:
                    body(t, i, front, core, tail)
            run(act, shifted)

        @block.vector
        def _(dve):
            def split(t, i):
                for a in range(2):
                    dve.wait_ge(xh_ready, 2 * t + a + 1)
                    if a == 0:
                        nc.vector.tensor_tensor(xl[i][:, :], X[0][:, :], xh[i][:, 0, :], ALU.subtract).then_inc(xl_ready, 1)
                    else:
                        nc.vector.tensor_tensor(xh[i][EB:P, 1, :], X[1][EB:P, :], xh[i][EB:P, 1, :],
                                                ALU.subtract).then_inc(xl_ready, 1)

            def steps(t, done):
                s = [done]

                def then(ins):
                    s[0] += 1
                    ins.then_inc(gate_step, 1)
                    dve.wait_ge(gate_step, GS * t + s[0])
                return then

            wide = lambda a: a.unsqueeze(2).broadcast_to([P, CT, NEXP if L0 else NR])

            def logits(t, then):
                n = NEXP if L0 else NR
                g = G[:, 0:CT * GC].rearrange("p (c k) -> p c k", c=CT)
                bias = W["bg"][:, 0:n].unsqueeze(1).broadcast_to([P, CT, n])
                dve.wait_ge(gate_done if L0 else low_ready, t + 1)
                then(nc.vector.tensor_tensor(lg[:, :, 0:n], g[:, :, 0:n], bias, ALU.add))
                then(nc.vector.tensor_reduce(out=top[:, :], in_=lg[:, :, 0:n], op=ALU.max, axis=AX.X))

            def choice(t, i):
                then = steps(t, 0)
                logits(t, then)
                then(nc.vector.tensor_tensor(seen[:, :, 1:NEXP + 1], lg[:, :, :], wide(top[:, :]), ALU.is_ge))
                for k in range(2, NEXP + 1):
                    then(nc.vector.tensor_tensor(seen[:, :, k:k + 1], seen[:, :, k:k + 1], seen[:, :, k - 1:k], ALU.max))
                then(nc.vector.tensor_tensor(chosen[i][:, :, :], seen[:, :, 1:], seen[:, :, 0:NEXP], ALU.subtract))

            def router_logits(t, i):
                then = steps(t, 0)
                logits(t, then)
                nc.vector.tensor_tensor(lg[:, :, 0:NR], lg[:, :, 0:NR], wide(top[:, :]),
                                        ALU.subtract).then_inc(gate_step, 1)

            def router_probs(t, i):
                dve.wait_ge(gate_step, GS * t + 4)
                then = steps(t, 4)
                then(nc.vector.tensor_reduce(out=den[:, :], in_=pr[:, :, :], op=ALU.add, axis=AX.X))
                then(nc.vector.reciprocal(den[:, :], den[:, :]))
                then(nc.vector.tensor_tensor(pr[:, :, :], pr[:, :, :], wide(den[:, :]), ALU.mult))
                then(nc.vector.tensor_reduce(out=least[:, :], in_=pr[:, :, :], op=ALU.min, axis=AX.X))
                then(nc.vector.tensor_tensor(eq[:, :, 0:NR], pr[:, :, :], wide(least[:, :]), ALU.is_le))

            def router_best(t, i):
                then = steps(t, 9)
                then(nc.vector.tensor_tensor(eq[:, :, 1:2], eq[:, :, 1:2], eq[:, :, 2:3], ALU.max))
                then(nc.vector.memset(eq[:, :, 0:1], 1.0))
                then(nc.vector.tensor_tensor(out_[:, :, :], eq[:, :, 0:NR], eq[:, :, 1:NR + 1], ALU.subtract))
                then(nc.vector.tensor_tensor(out_[:, :, :], out_[:, :, :], pr[:, :, :], ALU.mult))
                then(nc.vector.tensor_tensor(pr[:, :, :], pr[:, :, :], out_[:, :, :], ALU.subtract))
                then(nc.vector.tensor_reduce(out=den[:, :], in_=pr[:, :, :], op=ALU.add, axis=AX.X))
                then(nc.vector.tensor_scalar(den[:, :], den[:, :], 1e-6, None, ALU.add))
                then(nc.vector.reciprocal(den[:, :], den[:, :]))
                then(nc.vector.tensor_tensor(comb[:, :, :], pr[:, :, :], wide(den[:, :]), ALU.mult))
                nc.vector.tensor_tensor(lowc[:, :, 8:32].rearrange("p c (e r) -> p c e r", e=NR),
                                        low[:, :, :].rearrange("p c (e r) -> p c e r", e=NR),
                                        comb[:, :, :].unsqueeze(3).broadcast_to([P, CT, NR, 8]),
                                        ALU.mult).then_inc(gate_step, 1)

            gate_parts = {1: choice} if L0 else {0: router_logits, 1: router_probs, 3: router_best}

            def body(t, i, front, core, tail):
                j = 1 - i
                for n in range(SL if core else LAG + 3):
                    d = carried(t, n, core, tail)
                    if d is not None and d[1] % KD == KD - 1:
                        combine(d[0], i if n >= LAG else j, d[1] // KD)
                    if core:
                        dve.wait_ge(hh_ready, t * SL + n + 1)
                        nc.vector.tensor_tensor(hl[n % 3][:, :], hid[n % 2][:, :], hh[n % 3][:, :],
                                                ALU.subtract).then_inc(hl_ready, 1)
                    if core and n in gate_parts:
                        gate_parts[n](t, i)
                    if n == FRONT and front:
                        split(t + 1, j)
                    if tail and n == LAG:
                        stats(t - 1)
                    if tail and n == LAG + 2:
                        dve.wait_ge(rstd_ready, t)
                        wait_stored(t, j)
                        for c in range(CT):
                            nc.vector.tensor_scalar(hout[j][:, c, :], acc[:, c, :], mv[:, c, 0:1], rstd[:, c:c + 1],
                                                    ALU.subtract, ALU.mult).then_inc(h_ready, 1)

            def combine(t, i, e):
                if e == 0:
                    wait(dve, h_ready, CT * t)
                for c in range(CT):
                    g = CT * (t * NE + e) + c
                    dve.wait_ge(y_done, g + 1)
                    if not L0:
                        nc.vector.tensor_tensor(acc[:, c, :], Y[c][:, :], xtok[i][:, c, 0:E], ALU.add).then_inc(y_read, 1)
                        continue
                    if e:
                        dve.wait_ge(y_read, g - CT + 1)
                    prev = acc[:, c, :] if e else xtok[i][:, c, 0:E]
                    nc.vector.scalar_tensor_tensor(acc[:, c, :], Y[c][:, :], chosen[i][:, c, e:e + 1], prev,
                                                   ALU.mult, ALU.add).then_inc(y_read, 1)

            def stats(t):
                for c in range(CT):
                    dve.wait_ge(y_read, CT * (t * NE + NE - 1) + c + 1)
                    nc.vector.bn_stats(st6[:, c, :], acc[:, c, :]).then_inc(st_ready, 1)
                dve.wait_ge(st_ready, NS * t + CT)
                nc.vector.memset(ve[:, :], 0.0)
                for c in range(CT):
                    nc.vector.bn_aggr(mv[:, c, :], st6[:, c, :]).then_inc(st_ready, 1)
                dve.wait_ge(st_ready, NS * t + 2 * CT)
                nc.vector.tensor_scalar(ve[:, :], mv[:, :, 1], EPS, None, ALU.add).then_inc(st_ready, 1)

            def wait_stored(t, j):
                if isinstance(t, int):
                    wait(dve, stored[j], 16 * ((t - 1 - j) // 2))
                else:
                    dve.wait_ge(stored[j], (t - 1 - j) * 8)

            dve.wait_ge(const_ready, 1)
            split(0, 0)
            def shifted(t, i, front, core, tail):
                if not isinstance(t, int) or t >= 0:
                    body(t, i, front, core, tail)
            run(dve, shifted)

        @block.gpsimd
        def _(pool):
            pool.memset(mhalf[:, :], -0.5)
            if L0:
                pool.memset(seen[:, :, 0:1], 0.0)
            else:
                pool.memset(base_e[:, :, :], 2.718281828459045)
                pool.memset(lowc[:, :, 0:8], 0.0)
                pool.memset(eq[:, :, NR:NR + 1], 0.0)
            pool.tensor_scalar(ones2[:, :], ident[:, :], 0.0, masks[:, C_ROW01:C_ROW01 + 1], ALU.mult,
                               ALU.add).then_inc(const_ready, 1)

            def body(t, i, front, core, tail):
                if core and not L0:
                    pool.wait_ge(gate_step, GS * t + 3)
                    pool.tensor_tensor(pr[:, :, :], base_e[:, :, :], lg[:, :, 0:NR], ALU.pow).then_inc(gate_step, 1)
                if tail:
                    pool.wait_ge(st_ready, NS * t)
                    pool.tensor_tensor(rstd[:, :], ve[:, :], mhalf[:, :], ALU.pow).then_inc(rstd_ready, 1)

            def shifted(t, i, front, core, tail):
                if not isinstance(t, int) or t >= 0:
                    body(t, i, front, core, tail)
            run(pool, shifted)


def vit_tower(nc, NB, a, out):
    NC = -(-NB * NT // CHUNK)
    TOK = NC * CHUNK
    scratch = [nc.dram_tensor(f"h{n}", (TOK, E), F32, kind="Internal").ap() for n in range(3)]
    flat = lambda t: t[:, :].rearrange("p a -> p a") if len(t.shape) == 2 else t[:, :, :].rearrange("p a b -> p (a b)")
    with ExitStack() as whole:
        keep = lambda name, shape, dt: whole.enter_context(nc.sbuf_tensor("sb_" + name, shape, dt))
        masks, ident, ident16 = keep("masks", [P, C_N], F32), keep("ident", [P, P], F32), keep("ident16", [P, P], F16)
        loads = []

        def halves(name, src, shape, rows=P):
            hi, lo = keep(name + "_hi", shape, F16), keep(name + "_lo", shape, F16)
            size = 1
            for s in shape[1:]:
                size *= s
            loads.append((flat(src), flat(hi), flat(lo), size, rows))
            return hi, lo

        def single(name, src, shape):
            t = keep(name, shape, F32)
            size = 1
            for s in shape[1:]:
                size *= s
            loads.append((flat(src), flat(t), None, size, shape[0]))
            return t

        def two_rows(name, src, shape):
            t = keep(name, shape, F16)
            loads.append((flat(src), flat(t), None, shape[1] * shape[2], P))
            return t

        wa = []
        for n in range(2):
            w = {}
            w["wh"], w["wl"] = halves(f"attn{n}", a[f"wattn{n}"], [P, 2, 2 * NG * P + 2 * E])
            w["bqk"] = single(f"bqk{n}", a[f"bqk{n}"], [P, 2 * NG])
            w["bv"] = single(f"bv{n}", a[f"bv{n}"], [P, E])
            w["bo"] = single(f"bo{n}", a[f"bo{n}"], [P, E])
            wa.append(w)
        wa[0]["wtok"] = single("wtok", a["wtok"], [P, KD, E])
        pos = single("pos", a["pos"], [P, 2, E])
        tokb = single("tokb", a["tokb"], [P, 2, E])
        wa[0]["addend"] = keep("addend", [P, 2, E], F32)
        wa[0]["xp_d"] = a["xp"]
        wa[1]["sc_d"] = a["sc"]
        wf = []
        for n, ne in ((0, NEXP), (1, 1)):
            w = {}
            w["w1h"], w["w1l"] = halves(f"w1_{n}", a[f"w1_{n}"], [P, 2, ne * KD * P])
            w["w2h"], w["w2l"] = halves(f"w2_{n}", a[f"w2_{n}"], [P, ne * KD, E])
            w["b1"] = single(f"b1_{n}", a[f"b1_{n}"], [P, ne * KD])
            w["b2"] = two_rows(f"b2_{n}", a[f"b2_{n}"], [P, ne, E])
            w["wgh"], w["wgl"] = halves(f"wg{n}", a[f"wg{n}"], [P, 2, 4 if n == 0 else 32])
            w["bg"] = single(f"bg{n}", a[f"bg{n}"], [P, 4])
            wf.append(w)
        wf[1]["wup"] = single("wup", a["wup"], [32, E])

        def phase(f, *args):
            with ExitStack() as own:
                sb = lambda name, shape, dt: own.enter_context(nc.sbuf_tensor(name, shape, dt))
                pb = lambda name, shape, dt: own.enter_context(nc.psum_tensor(name, shape, dt))
                sem = lambda name: own.enter_context(nc.semaphore(name))
                f(sem, sb, pb, *args)

        phase(lambda sem, sb, pb: setup(nc, loads, a["consts"], masks, ident, ident16, sem, sb,
                                        (pos, tokb, wa[0]["addend"]), scratch, a["pos"], NB * NT))
        phase(lambda sem, sb, pb: attention(nc, 0, NB, None, scratch[0], wa[0], masks, ident, ident16, sem, sb, pb))
        phase(lambda sem, sb, pb: ffn(nc, 0, NC, scratch[0], scratch[1], wf[0], masks, ident, sem, sb, pb))
        phase(lambda sem, sb, pb: attention(nc, 1, NB, scratch[1], scratch[2], wa[1], masks, ident, ident16, sem, sb, pb))
        phase(lambda sem, sb, pb: ffn(nc, 1, NC, scratch[2], out, wf[1], masks, ident, sem, sb, pb))


def lay_out(inputs, np):
    f = {k: np.asarray(v) for k, v in inputs.items()}
    NB = f["x"].shape[0]
    d = {}
    x = f["x"].reshape(NB, 14, 16, 14, 16, 3).transpose(5, 2, 4, 0, 1, 3).reshape(KD, P, NB, NSC)
    xp = np.zeros((P, NB, KD, NT), np.float32)
    xp[:, :, :, 1:] = x.transpose(1, 2, 0, 3)
    d["xp"] = xp
    d["wtok"] = f["L0_tok_W"].T.reshape(KD, P, E).transpose(1, 0, 2)
    pos = np.zeros((P, 2, E), np.float32)
    pos[:, 0], pos[:T1, 1] = f["L0_tok_pos_embed"][0, :P], f["L0_tok_pos_embed"][0, P:]
    d["pos"] = pos
    tokb = np.broadcast_to(f["L0_tok_b"], (P, 2, E)).copy()
    tokb[0, 0] = f["L0_tok_cls_token"][0, 0]
    d["tokb"] = tokb

    def two_tiles(w):
        return np.stack([w[:EA], np.concatenate([w[EA:], w[EA:]])], 1)

    def heads_twice(w):
        w = w.reshape(*w.shape[:-1], HEADS, 1, HD)
        return np.concatenate([w, w], -2).reshape(*w.shape[:-3], HEADS * 2 * HD)

    for n, (qkv, o) in enumerate((("L0_attn_W_qkv", "L0_attn_W_out"), ("L1_attn_W_qkv", "L1_attn_W_proj"))):
        w = f[qkv]
        d[f"wattn{n}"] = two_tiles(np.concatenate(
            [heads_twice(w[:, :E]), heads_twice(w[:, E:2 * E]), w[:, 2 * E:], f[o]], 1))
    bq = f["L0_attn_b_qkv"]
    b = np.concatenate([heads_twice(bq[:E]), heads_twice(bq[E:2 * E])])
    rows = lambda v: np.broadcast_to(v, (P, v.shape[0]))
    d["bqk0"], d["bqk1"] = b.reshape(2 * NG, P).T, np.zeros((P, 2 * NG), np.float32)
    d["bv0"], d["bv1"] = rows(bq[2 * E:]), np.zeros((P, E), np.float32)
    d["bo0"], d["bo1"] = rows(f["L0_attn_b_out"]), rows(f["L1_attn_b_proj"])
    sc = np.zeros((P, 2, 256), np.float32)
    s = f["L1_attn_sc_token"][0]
    s = np.concatenate([s, s[:, EA:]], 1)
    sc[:, 0], sc[:NSC - P, 1] = s[:P], s[P:]
    d["sc"] = sc

    def two_rows(b):
        out = np.zeros((P, *b.shape), np.float32)
        out[0], out[1] = b, b
        return out

    w1 = f["L0_ffn_W1"].transpose(1, 0, 2).reshape(E, NEXP * KD * P)
    d["w1_0"], d["w1_1"] = two_tiles(w1), two_tiles(f["L1_ffn_w1"])
    d["w2_0"] = f["L0_ffn_W2"].reshape(NEXP * KD, P, E).transpose(1, 0, 2)
    d["w2_1"] = f["L1_ffn_w2"].reshape(KD, P, E).transpose(1, 0, 2)
    d["b1_0"] = f["L0_ffn_b1"].reshape(NEXP * KD, P).T
    d["b1_1"] = f["L1_ffn_b1"].reshape(KD, P).T
    d["b2_0"], d["b2_1"] = two_rows(f["L0_ffn_b2"]), two_rows(f["L1_ffn_b2"][None])
    d["wg0"] = two_tiles(f["L0_ffn_Wg"])
    low = f["L1_ffn_w_down"].transpose(1, 0, 2).reshape(E, 24)
    d["wg1"] = two_tiles(np.concatenate([f["L1_ffn_router_w"], np.zeros((E, 5), np.float32), low], 1))
    d["bg0"] = rows(f["L0_ffn_bg"])
    d["bg1"] = rows(np.concatenate([f["L1_ffn_router_b"], np.zeros(1, np.float32)]))
    wup = np.zeros((32, E), np.float32)
    wup[8:] = f["L1_ffn_w_up"].reshape(24, E)
    d["wup"] = wup
    consts = np.zeros((P, C_N + P), np.float32)
    p = np.arange(P)
    for h in range(HG):
        consts[:, C_HEAD + h] = p // 32 == h
        consts[:, C_HEADHI + h] = (p // 32 == h) & (p % 32 < HD)
        consts[:, C_HEADONE + h] = p == 32 * h + HD
    consts[:, C_LO], consts[:, C_HI] = p % 32 >= HD, p % 32 < HD
    consts[:, C_ROW1], consts[:, C_ROW01] = p == 1, p < 2
    consts[:, C_N:] = np.eye(P)
    d["consts"] = consts
    return {k: np.ascontiguousarray(v) for k, v in d.items()}


def kernel(**inputs):
    import numpy as _np
    import concourse.bacc as _bacc
    from concourse import mybir as _mybir
    from concourse.bass_utils import run_bass_kernel_spmd as _run

    arrays = lay_out(inputs, _np)
    NB = _np.asarray(inputs["x"]).shape[0]
    tokens = -(-NB * NT // CHUNK) * CHUNK
    nc = _bacc.Bacc("TRN2", target_bir_lowering=False, num_devices=1)
    args = {k: nc.dram_tensor(k, v.shape, _mybir.dt.from_np(v.dtype), kind="ExternalInput").ap()
            for k, v in arrays.items()}
    out = nc.dram_tensor("out", (tokens, E), F32, kind="ExternalOutput").ap()
    vit_tower(nc, NB, args, out)
    r = _run(nc, [arrays], core_ids=[0])
    return r.results[0]["out"][:NB * NT].reshape(NB, NT, E)
```

```python
import concourse.bass as bass
from concourse import mybir
from contextlib import ExitStack

F32 = mybir.dt.float32
F16 = mybir.dt.float16
ALU = mybir.AluOpType
ACT = mybir.ActivationFunctionType
AX = mybir.AxisListType

P = 128
E = 192
EA = 128
EB = E - EA
NT = 197
NSC = 196
T1 = NT - P
HEADS, HD = 12, 16
HG = 4
NG = HEADS // HG
KD = 768 // P
NEXP = 4
CT = 3
CHUNK = CT * P
EPS = 1e-5

C_HEAD, C_HEADHI, C_HEADONE, C_LO, C_HI, C_ROW1, C_ROW01, C_LOROWS, C_N = 0, 4, 8, 12, 13, 14, 15, 16, 17


def wait(eng, semaphore, value):
    if isinstance(value, int) and value <= 0:
        return
    eng.wait_ge(semaphore, value)


def token_tiles(n):
    return [(0, P), (P, n - P)]


def five_passes(nc, out, xh, xl, wh, wl, cols, tok, x_stationary, first=True, last=True):
    pairs = [(xh[:, 0, tok], wh[:, 0, cols]), (xl[:, tok], wh[:, 0, cols]), (xh[:, 0, tok], wl[:, 0, cols]),
             (xh[:, 1, tok], wh[:, 1, cols]), (xh[:, 1, tok], wl[:, 1, cols])]
    for n, (x, w) in enumerate(pairs):
        l, r = (x, w) if x_stationary else (w, x)
        ins = nc.tensor.matmul(out, l, r, start=first and n == 0, stop=last and n == len(pairs) - 1)
    return ins


def run_steps(eng, n, body):
    body(-1, 1, True, False, False)
    body(0, 0, n > 1, True, False)
    pairs = max(0, (n - 2) // 2)
    if pairs:
        with eng.Fori(0, pairs) as pair:
            body(pair * 2 + 1, 1, True, True, True)
            body(pair * 2 + 2, 0, True, True, True)
    for t in range(2 * pairs + 1, n + 1):
        body(t, t % 2, t + 1 < n, t < n, True)


def setup(nc, loads_all, consts_d, masks, ident, ident16, sem, sb, sums, scratch, fill_d, tokens):
    loads = [x for x in loads_all if x[1].dtype == F16]
    ST = 3
    stage = [sb(f"stage{n}", [P, max(x[3] for x in loads)], F32) for n in range(ST)]
    staged = [sem(f"staged{n}") for n in range(ST)]
    hi_done, lo_done, const_done = sem("hi_done"), sem("lo_done"), sem("const_done")
    padded = sem("padded")
    with nc.Block() as block:

        @block.sync
        def _(sp):
            sp.dma_start(masks[:, :], consts_d[:, 0:C_N]).then_inc(const_done, 16)
            sp.dma_start(ident[:, :], consts_d[:, C_N:C_N + P]).then_inc(const_done, 16)
            direct = [x for x in loads_all if x[1].dtype == F32]
            for src, dst, _, _, _ in direct:
                sp.dma_start(dst, src).then_inc(const_done, 16)
            for n, (src, hi, lo, size, rows) in enumerate(loads):
                if n >= ST:
                    sp.wait_ge(lo_done, n - ST + 1)
                sp.dma_start(stage[n % ST][0:rows, 0:size], src).then_inc(staged[n % ST], 16)
            pads = scratch[0].shape[0] - tokens
            for n, h in enumerate(scratch if pads else []):
                for at in range(tokens, tokens + pads, P):
                    m = min(P, tokens + pads - at)
                    sp.dma_start(h[at:at + m, :], fill_d[0:m, 0, :]).then_inc(padded, 16)
            if pads:
                sp.wait_ge(padded, 16 * len(scratch) * -(-pads // P))

        @block.scalar
        def _(act):
            act.wait_ge(const_done, 16 * (2 + len(loads_all) - len(loads)))
            nc.scalar.activation(ident16[:, :], ident[:, :], ACT.Copy)
            for n, (src, hi, lo, size, rows) in enumerate(loads):
                act.wait_ge(staged[n % ST], 16 * (n // ST + 1))
                if isinstance(lo, int):
                    nc.scalar.activation(hi, stage[n % ST][0:rows, 0:size], ACT.Copy,
                                         scale=masks[:, lo:lo + 1]).then_inc(hi_done, 1)
                else:
                    nc.scalar.activation(hi, stage[n % ST][0:rows, 0:size], ACT.Copy).then_inc(hi_done, 1)

        @block.vector
        def _(dve):
            for n, (src, hi, lo, size, rows) in enumerate(loads):
                dve.wait_ge(hi_done, n + 1)
                target = hi if isinstance(lo, int) else lo
                nc.vector.tensor_tensor(target, stage[n % ST][0:rows, 0:size], hi, ALU.subtract).then_inc(lo_done, 1)
            dve.wait_ge(lo_done, len(loads))
            pos, tokb, addend = sums
            nc.vector.tensor_tensor(addend[:, :, :], pos[:, :, :], tokb[:, :, :], ALU.add)


def attention(nc, layer, NB, src_d, dst_d, W, masks, ident, ident16, later, sem, sb, pb):
    L0 = layer == 0
    wh, wl = W["wh"], W["wl"]
    qcol = lambda g: slice(P * g, P * g + P)
    kcol = lambda g: slice(NG * P + P * g, NG * P + P * g + P)
    vcol, ocol = slice(2 * NG * P, 2 * NG * P + E), slice(2 * NG * P + E, 2 * NG * P + 2 * E)
    scale = float(E) ** -0.5 if L0 else float(HD) ** -0.5
    ktiles = [("own", 0, P), ("own", 1, T1)] + ([] if L0 else [("ctx", 0, P), ("ctx", 1, NSC - P)])
    NK = len(ktiles)
    SLOTS = NG * NK
    NKEYS = NT if L0 else NT + NSC

    n_ = lambda s: f"a{layer}_{s}"
    xtok = [sb(n_(f"xtok{i}"), [P, 2, 256], F32) for i in range(2)]
    xres = [sb(n_(f"xres{i}"), [P, 2, E], F32) for i in range(2)]
    xh = [sb(n_(f"xh{i}"), [P, 2, NT], F16) for i in range(2)]
    xl = [sb(n_(f"xl{i}"), [P, NT], F16) for i in range(2)]
    patches = [sb(n_(f"patch{i}"), [P, KD, NT], F32) for i in range(2)] if L0 else None
    ones2 = sb(n_("ones2"), [P, P], F16) if L0 else None
    ph = sb(n_("ph"), [P, KD, NT], F16) if L0 else None
    pl = sb(n_("pl"), [P, KD, NT], F16) if L0 else None
    khi = sb(n_("khi"), [P, NG, NT], F16)
    khl = sb(n_("khl"), [P, NG, NT], F16)
    k1 = [sb(n_(f"k1_{i}"), [P, NG, HG, NT], F16) for i in range(2)]
    k2 = [sb(n_(f"k2_{i}"), [P, NG, HG, NT], F16) for i in range(2)]
    q1 = [sb(n_(f"q1_{i}"), [P, NG, NT], F16) for i in range(2)]
    ql = [sb(n_(f"ql{i}"), [P, NG, NT], F16) for i in range(2)]
    q2 = [sb(n_(f"q2_{i}"), [P, NG, NT], F16) for i in range(2)]
    vaug = [sb(n_(f"v{i}"), [P, 2, HEADS, 32], F32) for i in range(2)]
    nmax = sb(n_("nmax"), [P, 2, NG * P], F16)
    probs = [sb(n_(f"p{i}"), [P, HG, NT], F32) for i in range(2)]
    osb = [sb(n_(f"o{i}"), [P, NG, NT], F32) for i in range(2)]
    rsum = sb(n_("rsum"), [P, 2, HEADS], F32)
    otok = sb(n_("otok"), [P, 2, 256], F32)
    oh = sb(n_("oh"), [P, 2, NT], F16)
    ol = sb(n_("ol"), [P, NT], F16)
    r = sb(n_("r"), [P, 2, E], F32)
    st6 = sb(n_("st6"), [P, 2, 6], F32)
    mv = sb(n_("mv"), [P, 2, 2], F32)
    ve = sb(n_("ve"), [P, 2], F32)
    rstd = sb(n_("rstd"), [P, 2], F32)
    mhalf = sb(n_("mhalf"), [P, 2], F32)
    tick = sb(n_("tick"), [P, 1], F32)
    hout = [sb(n_(f"h{i}"), [P, 2, E], F32) for i in range(2)]
    bk_lo = sb(n_("bk_lo"), [P, NG], F32)
    if not L0:
        sctok = sb(n_("sctok"), [P, 2, 256], F32)
        k1s = sb(n_("k1s"), [P, NG, HG, NSC], F16)
        k2s = sb(n_("k2s"), [P, NG, HG, NSC], F16)
        vs = sb(n_("vs"), [P, 2, HEADS, 32], F32)
    F = [pb(n_(f"F{i}"), [P, 512], F32) for i in range(3)]
    S = [pb(n_(f"S{i}"), [P, 2, NT], F32) for i in range(2)]
    O = pb(n_("O"), [P, NT], F32)
    C = [pb(n_(f"C{i}"), [P, 512], F32) for i in range(2)]

    qtiles = token_tiles(NT)
    K, Q = [("K", g) for g in range(NG)], [("Q", g) for g in range(NG)]
    V, xT, h0, neg = ("V",), ("xT",), [("h0", 0), ("h0", 1)], [("nmaxT", g) for g in range(NG)]
    do, take = (lambda part: ("do", part)), (lambda part: ("take", part))
    if L0:
        mx = [[("max", g, tt, pr) for tt in range(2) for pr in range(2)] for g in range(NG)]
        a, b, c = mx
        by_slot = [[xT, c[0], ("patches",), c[1]],
                   [neg[1], c[2], K[0], do("divide"), K[1]],
                   [c[3], Q[0], take("divide0"), K[2], Q[1], take("divide1"), h0[0], Q[2]],
                   [neg[2], do("oT"), take("oT"), a[0], a[1]],
                   [a[2], do("oproj"), take("oproj"), take("stats"), a[3], h0[1], take("spread"), b[0], V, b[1], neg[0]],
                   [b[2], b[3], take("norm")]]
        this_image = [*c, neg[1], neg[2]]
    else:
        mx = [[("max", g, tt, pr) for tt in range(2) for pr in range(HG)] for g in range(NG)]
        a, b, c = mx
        by_slot = [[K[0], c[3], Q[0]],
                   [neg[1], K[1], Q[1], K[2], do("divide"), c[4], c[5], take("divide0")],
                   [c[6], c[7], take("divide1")],
                   [V, a[0]],
                   [a[1], neg[2], do("oT"), a[2], take("oT"), Q[2]],
                   [xT, a[3], a[4]],
                   [a[5], a[6], a[7]],
                   [b[0], b[1], neg[0]],
                   [b[2], do("oproj"), take("oproj")],
                   [b[3], take("stats"), b[4], b[5]],
                   [b[6], take("spread"), b[7]],
                   [c[0], c[1], c[2], take("norm")]]
        this_image = [*c[3:], neg[1], neg[2]]
    jobs = [j for slot in by_slot for j in slot if j[0] not in ("do", "take", "patches")]
    job_at = {j: n for n, j in enumerate(jobs)}
    J = -(-len(jobs) // 3) * 3
    splits = [j for j in jobs if j[0] in ("xT", "K", "Q", "V")]

    def ahead(job):
        return 2 if job[0] == ("h0" if L0 else "xT") else 0 if job in this_image else 1

    JS = 6
    sjobs = [] if L0 else [("xT",)] + [("K", g) for g in range(NG)] + [("V",)]
    base = 0 if L0 else JS
    cx = 0 if L0 else 1

    def present(job, flags):
        return flags[2 - ahead(job)]

    def before(job, flags, among):
        return max([n for n, x in enumerate(among[:among.index(job)]) if present(x, flags)], default=-1)

    def amount(job, flags, among, total):
        at = among.index(job)
        last = not any(present(x, flags) for x in among[at + 1:])
        return (total if last else at + 1) - 1 - before(job, flags, among)

    def entry(item, flags, tail, pe):
        if item[0] in ("do", "take"):
            return [("tail", item[1])] if tail and pe == (item[0] == "do") else []
        if item[0] == "patches":
            return [item] if flags[0] and not pe else []
        return [("job", item)] if present(item, flags) else []

    def plan(flags, core, tail, pe=False):
        out = []
        for n in range(SLOTS):
            js = [entry(j, flags, tail, pe) for j in by_slot[n]]
            pv = [("pv", SLOTS - 1)] if n == 0 and tail else [("pv", n - 1)] if n > 0 and core else []
            scores = [("scores", n, half) for half in range(2)] if core else []
            out += scores[0:1] + js[0] + scores[1:2] + sum(js[1:2], []) + pv + sum(js[2:], [])
        return out

    loaded = [sem(n_(f"loaded{i}")) for i in range(2)]
    ph_ready = sem(n_("ph_ready"))
    pl_ready = sem(n_("pl_ready"))
    job_done = sem(n_("job_done"))
    job_read = sem(n_("job_read"))
    hi_ready = sem(n_("hi_ready"))
    k_ready = sem(n_("k_ready"))
    scores_done = sem(n_("scores_done"))
    probs_ready = sem(n_("probs_ready"))
    pv_done = sem(n_("pv_done"))
    o_ready = sem(n_("o_ready"))
    div_done = sem(n_("div_done"))
    rec_ready = sem(n_("rec_ready"))
    otok_ready = sem(n_("otok_ready"))
    oT_done = sem(n_("oT_done"))
    oh_ready = sem(n_("oh_ready"))
    ol_ready = sem(n_("ol_ready"))
    oproj_done = sem(n_("oproj_done"))
    xres_ready = sem(n_("xres_ready"))
    r_ready = sem(n_("r_ready"))
    st_ready = sem(n_("st_ready"))
    rstd_ready = sem(n_("rstd_ready"))
    h_ready = sem(n_("h_ready"))
    stored = [sem(n_(f"stored{i}")) for i in range(2)]
    const_ready = sem(n_("const_ready"))
    weights_in = sem(n_("weights_in"))
    later_hi = sem(n_("later_hi"))
    later_raw = [sb(n_(f"later{n}"), [P, x[3]], F32) for n, x in enumerate(later)]
    bias_ready = sem(n_("bias_ready"))

    def nth(t, job, among=jobs, total=J):
        if isinstance(t, int) and t < 0:
            return sjobs.index(job) + 1 if t == -1 and job in sjobs else 0
        return base + (t - ahead(job) + 2) * total + among.index(job) + 1

    def nth_hi(t, job):
        if isinstance(t, int) and t < 0:
            return sjobs.index(job) + 1
        return 5 * cx + (t - ahead(job) + ahead(("xT",))) * len(splits) + splits.index(job) + 1

    last_tok = ("h0", 1)
    m_last = lambda g: mx[g][-1]

    def loads_until(t, i):
        half = t // 2 if isinstance(t, int) else (t - i) // 2
        return 16 * ((1 if not L0 and i == 0 else 0) + DL * (half + 1))

    def run(eng, body):
        def one(t):
            body(t, t % 2, (t + 2 < NB, 0 <= t + 1 < NB, 0 <= t < NB), 0 <= t < NB, 1 <= t)

        for t in (-2, -1, 0):
            one(t)
        pairs = max(0, (NB - 3) // 2)
        if pairs:
            with eng.Fori(0, pairs) as pair:
                body(pair * 2 + 1, 1, (True, True, True), True, True)
                body(pair * 2 + 2, 0, (True, True, True), True, True)
        for t in range(2 * pairs + 1, NB + 1):
            one(t)

    DL = 1 if L0 else 4
    rows = lambda d, t: d[bass.ds(t * NT, P), :] if not isinstance(t, int) else d[t * NT:t * NT + P, :]
    rows1 = lambda d, t: (d[bass.ds(t * NT + P, T1), :] if not isinstance(t, int)
                          else d[t * NT + P:t * NT + NT, :])

    with nc.Block() as block:

        @block.sync
        def _(sp):
            if not L0:
                sp.dma_start(sctok[:, :, :], W["sc_d"]).then_inc(loaded[0], 16)
                sp.wait_ge(loaded[0], 16)
            def load(t, i):
                if L0:
                    src = W["xp_d"][:, bass.ds(t, 1)] if not isinstance(t, int) else W["xp_d"][:, t:t + 1]
                    sp.dma_start(patches[i][:, :, :], src.rearrange("p a k t -> p (a k) t")).then_inc(loaded[i], 16)
                else:
                    a, b = rows(src_d, t), rows1(src_d, t)
                    sp.dma_start(xtok[i][:, 0, 0:E], a).then_inc(loaded[i], 16)
                    sp.dma_start(xtok[i][:, 0, E:256], a[:, EA:E]).then_inc(loaded[i], 16)
                    sp.dma_start(xtok[i][0:T1, 1, 0:E], b).then_inc(loaded[i], 16)
                    sp.dma_start(xtok[i][0:T1, 1, E:256], b[:, EA:E]).then_inc(loaded[i], 16)

            def step(t, i, more, tail):
                j = 1 - i
                if more and L0:
                    sp.wait_ge(pl_ready, t + 2)
                    load(t + 3, j)
                elif more:
                    sp.wait_ge(xres_ready, t + 1)
                    sp.wait_ge(job_done, nth(t, ("xT",)))
                    load(t + 2, i)
                if tail:
                    sp.wait_ge(h_ready, 2 * t)
                    sp.dma_start(rows(dst_d, t - 1), hout[j][:, 0, :]).then_inc(stored[j], 16)
                    sp.dma_start(rows1(dst_d, t - 1), hout[j][0:T1, 1, :]).then_inc(stored[j], 16)

            far = 3 if L0 else 2
            load(0, 0)
            load(1, 1)
            if L0 and NB > 2:
                sp.wait_ge(pl_ready, 1)
                load(2, 0)
            step(0, 0, far < NB, False)
            pairs = max(0, (NB - far - 1) // 2)
            if pairs:
                with sp.Fori(0, pairs) as pair:
                    step(pair * 2 + 1, 1, True, True)
                    step(pair * 2 + 2, 0, True, True)
            for t in range(2 * pairs + 1, NB + 1):
                step(t, t % 2, t + far < NB, True)
            for i in range(2):
                sp.wait_ge(stored[i], 32 * (NB // 2))

        @block.tensor
        def _(pe):
            def bank_of(n):
                return F[n % 3]

            pe.wait_ge(const_ready, 1)

            def front_job(job, n, t, i, free, buffers, ntok, ctx=False):
                xt, xhi, xlo = buffers
                bank = bank_of(n)
                kind = job[0]
                tiles = token_tiles(ntok)
                wait(pe, job_read, free)
                img = t + cx
                if kind == "h0":
                    if job[1] == 0:
                        pe.wait_ge(pl_ready, t + 1)
                    t0, m = tiles[job[1]]
                    for k in range(KD):
                        for part, (x, w) in enumerate(((ph, W["wth"]), (pl, W["wth"]), (ph, W["wtl"]))):
                            ins = nc.tensor.matmul(bank[0:m, 0:E], x[:, k, t0:t0 + m], w[:, k, :],
                                                   start=k == 0 and part == 0, stop=k == KD - 1 and part == 2)
                elif kind == "xT":
                    if L0:
                        pe.wait_ge(job_read, nth(t, last_tok))
                    elif not ctx:
                        pe.wait_ge(loaded[i], loads_until(t, i))
                    else:
                        pe.wait_ge(loaded[0], 16)
                    for f, col in ((0, 0), (EA, ntok)):
                        for tt, (t0, m) in enumerate(tiles):
                            ins = nc.tensor.transpose(bank[:, col + t0:col + t0 + m], xt[0:m, tt, f:f + P],
                                                      ident[0:m, 0:m])
                elif kind in "KQ":
                    if kind == "K" and job[1] == 0:
                        pe.wait_ge(job_read, nth(t, ("xT",)))
                    cols = kcol(job[1]) if kind == "K" else qcol(job[1])
                    ins = five_passes(nc, bank[:, 0:ntok], xhi, xlo, wh, wl, cols, slice(0, ntok), False)
                elif kind == "V":
                    for tt, (t0, m) in enumerate(tiles):
                        ins = v_passes(bank[0:m, tt * E:tt * E + E], xhi, xlo, slice(t0, t0 + m), vcol, tt)
                        if L0:
                            ins = nc.tensor.matmul(bank[0:m, tt * E:tt * E + E], ones2[:, 0:m], W["bv2"][:, 0, :],
                                                   start=False, stop=True, skip_group_check=True)
                elif kind == "max":
                    _, g, tt, pr = job
                    t0, m = tiles[tt]
                    if tt == 0 and pr == 0:
                        pe.wait_ge(k_ready, 3 * img + g + 1)
                        pe.wait_ge(hi_ready, nth_hi(t, ("Q", g)))
                    q = q1[i][:, g, t0:t0 + m]
                    if L0:
                        ins = nc.tensor.matmul(bank[0:m, 0:2 * NT].rearrange("p (h k) -> p h k", h=2), q,
                                               k1[i][:, g, 2 * pr:2 * pr + 2, :], start=True, stop=True)
                    else:
                        nc.tensor.matmul(bank[0:m, 0:NT], q, k1[i][:, g, pr, :], start=True, stop=True)
                        ins = nc.tensor.matmul(bank[0:m, NT:NKEYS], q, k1s[:, g, pr, :], start=True, stop=True)
                else:
                    g = job[1]
                    pe.wait_ge(job_read, nth(t, m_last(g)))
                    b16 = bank[:, 0:P].bitcast(F16)
                    for tt, (t0, m) in enumerate(tiles):
                        ins = nc.tensor.transpose(b16[:, t0:t0 + m + m % 2], nmax[0:m + m % 2, tt, P * g:P * g + P],
                                                  ident16[0:m + m % 2, 0:m + m % 2])
                return ins

            def v_passes(out, xhi, xlo, tok, cols, tt):
                pairs = [(xhi[:, 0, tok], wh[:, 0, cols]), (xlo[:, tok], wh[:, 0, cols]),
                         (xhi[:, 0, tok], wl[:, 0, cols]), (xhi[:, 1, tok], wh[:, 1, cols]),
                         (xhi[:, 1, tok], wl[:, 1, cols])]
                for n, (l, rr) in enumerate(pairs):
                    ins = nc.tensor.matmul(out, l, rr, start=n == 0 and tt == 0, stop=n == 4 and not (L0 and cols == vcol),
                                           skip_group_check=True)
                return ins

            if not L0:
                for n, job in enumerate(sjobs):
                    ins = front_job(job, n, -1, 0, n - 2, (sctok, xh[1], xl[1]), NSC, ctx=True)
                    ins.then_inc(job_done, 1 if n < len(sjobs) - 1 else JS - n)

            def body(t, i, flags, core, tail):
                j = 1 - i
                for step in plan(flags, core, tail, pe=True):
                    if step[0] == "job":
                        job = step[1]
                        n, k = job_at[job], j if ahead(job) == 1 else i
                        free = base + (t + 2) * J + min(n - 2, before(job, flags, jobs) + 1)
                        ins = front_job(job, n, t + ahead(job), k, free, (xtok[k], xh[k], xl[k]), NT)
                        ins.then_inc(job_done, amount(job, flags, jobs, J))
                    elif step[0] == "scores":
                        _, n, pr = step
                        g, (src, kt, m) = n // NK, ktiles[n % NK]
                        ka, kb = (k1[i], k2[i]) if src == "own" else (k1s, k2s)
                        if n % NK == 0 and pr == 0:
                            pe.wait_ge(job_read, nth(t, ("nmaxT", g)))
                        wait(pe, probs_ready, 2 * (t * SLOTS + n) - 1 + pr)
                        keys = slice(kt * P, kt * P + m)
                        for hh in range(2):
                            h = 2 * pr + hh
                            nc.tensor.matmul(S[pr][0:m, hh, :], ka[:, g, h, keys], q1[i][:, g, :],
                                             start=hh == 0, stop=False, skip_group_check=True)
                            ins = nc.tensor.matmul(S[pr][0:m, hh, :], kb[:, g, h, keys], q2[i][:, g, :],
                                                   start=False, stop=True, skip_group_check=True)
                        ins.then_inc(scores_done, 1)
                    elif step[0] == "pv":
                        n = step[1]
                        ti, vi = (t, i) if n < SLOTS - 1 else (t - 1, j)
                        g, (src, kt, m) = n // NK, ktiles[n % NK]
                        v = vaug[vi] if src == "own" else vs
                        pe.wait_ge(probs_ready, 2 * (ti * SLOTS + n) + 2)
                        if n % NK == 0:
                            wait(pe, o_ready, 3 * ti + g)
                        for h in range(HG):
                            ins = nc.tensor.matmul(O[32 * h:32 * h + 32, :], v[0:m, kt, HG * g + h, :],
                                                   probs[n % 2][0:m, h, :], start=n % NK == 0, stop=n % NK == NK - 1)
                        ins.then_inc(pv_done, 1)
                    elif step[1] == "divide":
                        pe.wait_ge(o_ready, 3 * t)
                        for tt, (t0, m) in enumerate(qtiles):
                            wait(pe, ol_ready if tt == 0 else r_ready, (t - 1) if tt == 0 else 2 * (t - 1))
                            for g in range(NG):
                                ins = nc.tensor.transpose(C[tt][0:m, P * g:P * g + P], osb[j][:, g, t0:t0 + m],
                                                          ident[:, :])
                            ins.then_inc(div_done, 1)
                    elif step[1] == "oT":
                        pe.wait_ge(otok_ready, 2 * t)
                        for f, col in ((0, 0), (EA, NT)):
                            for tt, (t0, m) in enumerate(qtiles):
                                ins = nc.tensor.transpose(C[0][:, col + t0:col + t0 + m], otok[0:m, tt, f:f + P],
                                                          ident[0:m, 0:m])
                        ins.then_inc(oT_done, 1)
                    elif step[1] == "oproj":
                        pe.wait_ge(ol_ready, t)
                        for tt, (t0, m) in enumerate(qtiles):
                            ins = v_passes(C[1][0:m, tt * E:tt * E + E], oh, ol, slice(t0, t0 + m), ocol, tt)
                        ins.then_inc(oproj_done, 1)

            run(pe, body)

        @block.scalar
        def _(act):
            def front(job, t, i, flags, xhi, ntok, vd, ctx=False):
                kind, bank = job[0], F[(job_at[job] if not ctx else sjobs.index(job)) % 3]
                inc = 1 if ctx else amount(job, flags, splits, len(splits))
                if kind == "xT":
                    act.wait_ge(job_done, nth(t, job))
                    src = bank[:, 0:2 * ntok].rearrange("p (a t) -> p a t", a=2)
                    nc.scalar.activation(xhi[:, :, 0:ntok], src, ACT.Copy).then_inc(hi_ready, inc)
                elif kind == "K":
                    g = job[1]
                    act.wait_ge(job_done, nth(t, job))
                    if g == 0:
                        wait(act, job_read, nth(t - 1, ("K", NG - 1)))
                    nc.scalar.activation(khi[:, g, 0:ntok], bank[:, 0:ntok], ACT.Identity,
                                         bias=bk_lo[:, g:g + 1],
                                         scale=masks[:, C_LO:C_LO + 1]).then_inc(hi_ready, inc)
                elif kind == "Q":
                    g = job[1]
                    act.wait_ge(job_done, nth(t, job))
                    nc.scalar.activation(q1[i][:, g, :], bank[:, 0:NT], ACT.Identity,
                                         bias=W["bqk"][:, g:g + 1]).then_inc(hi_ready, inc)
                elif kind == "V":
                    act.wait_ge(job_done, nth(t, job))
                    wait(act, pv_done, (t - 1) * SLOTS)
                    for tt, (t0, m) in enumerate(token_tiles(ntok)):
                        src = bank[0:m, tt * E:tt * E + E].rearrange("p (h d) -> p h d", h=HEADS)
                        ins = nc.scalar.activation(vd[0:m, tt, :, 0:HD], src, ACT.Copy)
                    ins.then_inc(hi_ready, inc)

            for raw, (src, hi, lo, size, rows) in zip(later_raw, later):
                act.dma_start(raw[:, :], src).then_inc(weights_in, 16)
            act.wait_ge(bias_ready, 1)
            if not L0:
                for job in sjobs:
                    front(job, -1, 0, None, xh[1], NSC, vs, ctx=True)

            def body(t, i, flags, core, tail):
                j = 1 - i

                def copy_out(n):
                    ti, oi = (t, i) if n < SLOTS - 1 else (t - 1, j)
                    act.wait_ge(pv_done, ti * SLOTS + n + 1)
                    nc.scalar.activation(osb[oi][:, n // NK, :], O[:, :], ACT.Copy).then_inc(o_ready, 1)

                for step in plan(flags, core, tail):
                    if step[0] == "job":
                        k = j if ahead(step[1]) == 1 else i
                        if step[1] in splits:
                            front(step[1], t + ahead(step[1]), k, flags, xh[k], NT, vaug[k])
                    elif step[0] == "patches":
                        act.wait_ge(loaded[i], loads_until(t + 2, i))
                        wait(act, job_done, nth(t + 1, last_tok))
                        nc.scalar.activation(ph[:, :, :], patches[i][:, :, :], ACT.Copy).then_inc(ph_ready, 1)
                    elif step[0] == "scores":
                        _, n, pr = step
                        m = ktiles[n % NK][2]
                        act.wait_ge(scores_done, 2 * (t * SLOTS + n) + pr + 1)
                        if pr == 0:
                            wait(act, pv_done, t * SLOTS + n - 1)
                        nc.scalar.activation(probs[n % 2][0:m, 2 * pr:2 * pr + 2, :], S[pr][0:m, :, :], ACT.Exp,
                                             scale=scale).then_inc(probs_ready, 1)
                    elif step[0] == "pv":
                        if step[1] % NK == NK - 1:
                            copy_out(step[1])
                    elif step[1] == "oT":
                        act.wait_ge(oT_done, t)
                        src = C[0][:, 0:2 * NT].rearrange("p (a t) -> p a t", a=2)
                        wait(act, oproj_done, t - 1)
                        nc.scalar.activation(oh[:, :, :], src, ACT.Copy).then_inc(oh_ready, 1)

            run(act, body)
            if later:
                act.wait_ge(weights_in, 16 * len(later))
            for raw, (src, hi, lo, size, rows) in zip(later_raw, later):
                nc.scalar.activation(hi, raw[:, :], ACT.Copy).then_inc(later_hi, 1)

        @block.vector
        def _(dve):
            def front(job, t, i, flags, buffers, ntok, ctx=False):
                xhi, xlo = buffers
                kind = job[0]
                n = job_at[job] if not ctx else sjobs.index(job)
                bank = F[n % 3]
                if ctx:
                    inc = 1 if n < len(sjobs) - 1 else JS - n
                else:
                    inc = amount(job, flags, jobs, J)
                img = t + cx
                tiles = token_tiles(ntok)
                if kind == "h0":
                    tt = job[1]
                    t0, m = tiles[tt]
                    dve.wait_ge(job_done, nth(t, job))
                    wait(dve, xres_ready, t - 1)
                    nc.vector.tensor_tensor(xtok[i][0:m, tt, 0:E], bank[0:m, 0:E], W["addend"][0:m, tt, :], ALU.add)
                    nc.vector.tensor_tensor(xtok[i][0:m, tt, E:256], bank[0:m, EA:E], W["addend"][0:m, tt, EA:E],
                                            ALU.add).then_inc(job_read, inc)
                elif kind == "xT":
                    dve.wait_ge(hi_ready, nth_hi(t, job))
                    nc.vector.tensor_tensor(xlo[:, 0:ntok], bank[:, 0:ntok], xhi[:, 0, 0:ntok], ALU.subtract)
                    nc.vector.tensor_tensor(xhi[EB:P, 1, 0:ntok], bank[EB:P, ntok:2 * ntok], xhi[EB:P, 1, 0:ntok],
                                            ALU.subtract).then_inc(job_read, inc)
                elif kind == "K":
                    g = job[1]
                    dve.wait_ge(hi_ready, nth_hi(t, job))
                    wait(dve, k_ready, 3 * (img - 1) + g + 1)
                    nc.vector.scalar_tensor_tensor(khl[:, g, 0:ntok], bank[:, 0:ntok],
                                                   W["bqk"][:, NG + g:NG + g + 1], khi[:, g, 0:ntok],
                                                   ALU.add, ALU.subtract).then_inc(job_read, inc)
                elif kind == "Q":
                    g = job[1]
                    dve.wait_ge(hi_ready, nth_hi(t, job))
                    nc.vector.scalar_tensor_tensor(ql[i][:, g, :], bank[:, 0:NT], W["bqk"][:, g:g + 1], q1[i][:, g, :],
                                                   ALU.add, ALU.subtract).then_inc(job_read, inc)
                elif kind == "V":
                    dve.wait_ge(hi_ready, nth_hi(t, job))
                    nc.vector.memset(tick[:, :], 0.0).then_inc(job_read, inc)
                elif kind == "max":
                    _, g, tt, pr = job
                    m = tiles[tt][1]
                    dve.wait_ge(job_done, nth(t, job))
                    if L0:
                        src = bank[0:m, 0:2 * NT].rearrange("p (h k) -> p h k", h=2)
                        out = nmax[0:m, tt, P * g + 64 * pr:P * g + 64 * pr + 64].rearrange(
                            "p (h c) -> p h c", h=2)[:, :, HD]
                    else:
                        src = bank[0:m, 0:NKEYS]
                        out = nmax[0:m, tt, P * g + 32 * pr + HD:P * g + 32 * pr + HD + 1]
                    with nc.allow_low_precision("a shift of the exponent, the same for all keys"):
                        nc.vector.tensor_reduce(out=out, in_=src, op=ALU.max, axis=AX.X,
                                                negate=True).then_inc(job_read, inc)
                else:
                    dve.wait_ge(job_done, nth(t, job))
                    g = job[1]
                    dve.wait_ge(job_read, nth(t, ("Q", g)))
                    ins = nc.vector.scalar_tensor_tensor(q2[i][:, g, :], ql[i][:, g, :], masks[:, C_HI:C_HI + 1],
                                                         bank[:, 0:P].bitcast(F16)[:, 0:NT], ALU.mult, ALU.add)
                    ins.then_inc(job_read, inc)

            nc.vector.tensor_scalar(bk_lo[:, :], W["bqk"][:, NG:2 * NG], masks[:, C_LO:C_LO + 1], None,
                                    ALU.mult).then_inc(bias_ready, 1)
            dve.wait_ge(const_ready, 1)
            if not L0:
                for n, job in enumerate(sjobs):
                    front(job, -1, 0, None, (xh[1], xl[1]), NSC, ctx=True)

            def body(t, i, flags, core, tail):
                j = 1 - i
                for step in plan(flags, core, tail):
                    if step[0] == "job":
                        k = j if ahead(step[1]) == 1 else i
                        front(step[1], t + ahead(step[1]), k, flags, (xh[k], xl[k]), NT)
                    elif step[0] != "tail":
                        continue
                    elif step[1] in ("divide0", "divide1"):
                        for tt, (t0, m) in list(enumerate(qtiles))[int(step[1][-1]):][:1]:
                            dve.wait_ge(div_done, 2 * (t - 1) + tt + 1)
                            o = C[tt][0:m, 0:NG * P].rearrange("p (h c) -> p h c", h=HEADS)
                            nc.vector.reciprocal(rsum[0:m, tt, :], o[:, :, HD]).then_inc(rec_ready, 1)
                            dve.wait_ge(rec_ready, 2 * (t - 1) + tt + 1)
                            inv = rsum[0:m, tt, :].unsqueeze(2)
                            nc.vector.tensor_tensor(otok[0:m, tt, 0:E].rearrange("p (h d) -> p h d", h=HEADS),
                                                    o[:, :, 0:HD], inv.broadcast_to([m, HEADS, HD]), ALU.mult)
                            nc.vector.tensor_tensor(otok[0:m, tt, E:256].rearrange("p (h d) -> p h d", h=HG),
                                                    o[:, EA // HD:, 0:HD],
                                                    inv[:, EA // HD:].broadcast_to([m, HG, HD]),
                                                    ALU.mult).then_inc(otok_ready, 1)
                    elif step[1] == "oT":
                        dve.wait_ge(oh_ready, t)
                        nc.vector.tensor_tensor(ol[:, :], C[0][:, 0:NT], oh[:, 0, :], ALU.subtract)
                        nc.vector.tensor_tensor(oh[EB:P, 1, :], C[0][EB:P, NT:2 * NT], oh[EB:P, 1, :],
                                                ALU.subtract).then_inc(ol_ready, 1)
                    elif step[1] == "oproj":
                        dve.wait_ge(oproj_done, t)
                        dve.wait_ge(xres_ready, t)
                        wait(dve, h_ready, 2 * (t - 1))
                        for tt, (t0, m) in enumerate(qtiles):
                            nc.vector.tensor_tensor(r[0:m, tt, :], C[1][0:m, tt * E:tt * E + E], xres[j][0:m, tt, :],
                                                    ALU.add).then_inc(r_ready, 1)
                    elif step[1] == "stats":
                        for tt, (t0, m) in enumerate(qtiles):
                            dve.wait_ge(r_ready, 2 * (t - 1) + tt + 1)
                            nc.vector.bn_stats(st6[0:m, tt, :], r[0:m, tt, :]).then_inc(st_ready, 1)
                    elif step[1] == "spread":
                        dve.wait_ge(st_ready, 6 * (t - 1) + 2)
                        nc.vector.memset(ve[:, :], 0.0)
                        for tt, (t0, m) in enumerate(qtiles):
                            nc.vector.bn_aggr(mv[0:m, tt, :], st6[0:m, tt, :]).then_inc(st_ready, 1)
                        for tt, (t0, m) in enumerate(qtiles):
                            dve.wait_ge(st_ready, 6 * (t - 1) + tt + 3)
                            nc.vector.tensor_scalar(ve[0:m, tt:tt + 1], mv[0:m, tt, 1:2], EPS, None,
                                                    ALU.add).then_inc(st_ready, 1)
                    elif step[1] == "norm":
                        dve.wait_ge(rstd_ready, 2 * t)
                        wait_stored(t, j)
                        for tt, (t0, m) in enumerate(qtiles):
                            nc.vector.tensor_scalar(hout[j][0:m, tt, :], r[0:m, tt, :], mv[0:m, tt, 0:1],
                                                    rstd[0:m, tt:tt + 1], ALU.subtract, ALU.mult).then_inc(h_ready, 1)

            def wait_stored(t, j):
                if isinstance(t, int):
                    wait(dve, stored[j], 32 * ((t - 1 - j) // 2))
                else:
                    dve.wait_ge(stored[j], (t - 1 - j) * 16)

            run(dve, body)
            for n, (raw, (src, hi, lo, size, rows)) in enumerate(zip(later_raw, later)):
                dve.wait_ge(later_hi, n + 1)
                nc.vector.tensor_tensor(lo, raw[:, :], hi, ALU.subtract)

        @block.gpsimd
        def _(pool):
            pool.memset(nmax[:, :, :], 0.0)
            for v in vaug + ([] if L0 else [vs]):
                pool.memset(v[:, :, :, HD + 1:32], 0.0)
                pool.memset(v[:, :, :, HD:HD + 1], 1.0)
            if L0:
                pool.tensor_scalar(ones2[:, :], ident[:, :], 0.0, masks[:, C_ROW01:C_ROW01 + 1], ALU.mult, ALU.add)
            pool.memset(mhalf[:, :], -0.5).then_inc(const_ready, 1)
            pool.wait_ge(const_ready, 1)

            def mask_keys(g, t, kd1, kd2, ntok):
                pool.wait_ge(job_read, nth(t, ("K", g)))
                for h in range(HG):
                    pool.tensor_tensor(kd1[:, g, h, 0:ntok], khl[:, g, 0:ntok],
                                       masks[:, C_HEAD + h:C_HEAD + h + 1].broadcast_to([P, ntok]), ALU.mult)
                    ins = pool.tensor_scalar(kd2[:, g, h, 0:ntok], khl[:, g, 0:ntok],
                                             masks[:, C_HEADHI + h:C_HEADHI + h + 1],
                                             masks[:, C_HEADONE + h:C_HEADONE + h + 1], ALU.mult, ALU.add)
                ins.then_inc(k_ready, 1)

            if not L0:
                for g in range(NG):
                    mask_keys(g, -1, k1s, k2s, NSC)

            def body(t, i, flags, core, tail):
                j = 1 - i
                for step in plan(flags, core, tail):
                    if step[0] == "job" and step[1][0] == "K":
                        mask_keys(step[1][1], t + 1, k1[j], k2[j], NT)
                    elif step[0] == "patches":
                        pool.wait_ge(ph_ready, t + 3)
                        pool.tensor_tensor(pl[:, :, :], patches[i][:, :, :], ph[:, :, :],
                                           ALU.subtract).then_inc(pl_ready, 1)
                    elif step == ("tail", "spread"):
                        for tt, (t0, m) in enumerate(qtiles):
                            pool.wait_ge(st_ready, 6 * (t - 1) + tt + 5)
                            wait(pool, h_ready, 2 * (t - 1))
                            pool.tensor_tensor(rstd[0:m, tt:tt + 1], ve[0:m, tt:tt + 1], mhalf[0:m, tt:tt + 1],
                                               ALU.pow).then_inc(rstd_ready, 1)
                if flags[1]:
                    if L0:
                        pool.wait_ge(job_read, nth(t + 1, last_tok))
                    else:
                        pool.wait_ge(loaded[j], loads_until(t + 1, j))
                    wait(pool, r_ready, 2 * t)
                    for tt, (t0, m) in enumerate(qtiles):
                        ins = pool.tensor_tensor(xres[j][0:m, tt, :], xtok[j][0:m, tt, 0:E], W["bo"][0:m, :],
                                                 ALU.add)
                    ins.then_inc(xres_ready, 1)

            run(pool, body)


def ffn(nc, layer, NC, src_d, dst_d, W, masks, ident, sem, sb, pb):
    L0 = layer == 0
    NE = NEXP if L0 else 1
    SL = NE * KD
    LAG = 2
    GC = 4 if L0 else 32
    NR = 3
    LR = 32
    n_ = lambda s: f"f{layer}_{s}"
    w1h, w1l, w2h, w2l = W["w1h"], W["w1l"], W["w2h"], W["w2l"]

    xtok = [sb(n_(f"xtok{i}"), [P, CT, 256], F32) for i in range(2)]
    xh = [sb(n_(f"xh{i}"), [P, 2, CHUNK], F16) for i in range(2)]
    xl = [sb(n_(f"xl{i}"), [P, CHUNK], F16) for i in range(2)]
    hid = [sb(n_(f"hid{i}"), [P, CHUNK], F32) for i in range(2)]
    hh = [sb(n_(f"hh{i}"), [P, CHUNK], F16) for i in range(3)]
    hl = [sb(n_(f"hl{i}"), [P, CHUNK], F16) for i in range(3)]
    acc = sb(n_("acc"), [P, CT, E], F32)
    xres = [sb(n_(f"xres{i}"), [P, CT, E], F32) for i in range(2)]
    bsel = sb(n_("bsel"), [P, CT, E], F32) if L0 else None
    hout = [sb(n_(f"h{i}"), [P, CT, E], F32) for i in range(2)]
    st6 = sb(n_("st6"), [P, CT, 6], F32)
    mv = sb(n_("mv"), [P, CT, 2], F32)
    ve = sb(n_("ve"), [P, CT], F32)
    rstd = sb(n_("rstd"), [P, CT], F32)
    mhalf = sb(n_("mhalf"), [P, CT], F32)
    lg = sb(n_("lg"), [P, CT, 4], F32)
    top = sb(n_("top"), [P, CT], F32)
    if L0:
        seen = sb(n_("seen"), [P, CT, NEXP + 1], F32)
        chosen = [sb(n_(f"chosen{i}"), [P, CT, NEXP], F32) for i in range(2)]
    else:
        base_e = sb(n_("base_e"), [P, CT, NR], F32)
        pr = sb(n_("pr"), [P, CT, NR], F32)
        den = sb(n_("den"), [P, CT], F32)
        least = sb(n_("least"), [P, CT], F32)
        eq = sb(n_("eq"), [P, CT, NR + 1], F32)
        out_ = sb(n_("out"), [P, CT, NR], F32)
        comb = sb(n_("comb"), [P, CT, NR], F32)
        low = sb(n_("low"), [P, CT, NR * 8], F32)
        lowc = sb(n_("lowc"), [P, CT, 3 * LR], F32)
        lowT = [sb(n_(f"lowT{i}"), [3 * LR, CHUNK], F16) for i in range(2)]
    U = [pb(n_(f"U{i}"), [P, CHUNK], F32) for i in range(2)]
    Y = [pb(n_(f"Y{i}"), [P, E], F32) for i in range(CT)]
    X = [pb(n_(f"X{i}"), [P, CHUNK], F32) for i in range(2)]
    G = pb(n_("G"), [P, CHUNK], F32)

    loaded = [sem(n_(f"loaded{i}")) for i in range(2)]
    xT_done = sem(n_("xT_done"))
    xh_ready = sem(n_("xh_ready"))
    xl_ready = sem(n_("xl_ready"))
    gate_done = sem(n_("gate_done"))
    gate_step = sem(n_("gate_step"))
    low_ready = sem(n_("low_ready"))
    lowT_done = sem(n_("lowT_done"))
    lowT_ready = sem(n_("lowT_ready"))
    lowlo_ready = sem(n_("lowlo_ready"))
    up_done = sem(n_("up_done"))
    gelu_done = sem(n_("gelu_done"))
    hh_ready = sem(n_("hh_ready"))
    hl_ready = sem(n_("hl_ready"))
    down_done = sem(n_("down_done"))
    y_done = sem(n_("y_done"))
    y_read = sem(n_("y_read"))
    st_ready = sem(n_("st_ready"))
    rstd_ready = sem(n_("rstd_ready"))
    h_ready = sem(n_("h_ready"))
    stored = [sem(n_(f"stored{i}")) for i in range(2)]
    const_ready = sem(n_("const_ready"))
    xres_step = sem(n_("xres_step"))
    GS = 7 if L0 else 19
    XS = 2 * NEXP if L0 else 1
    NS = 2 * CT + 1
    FRONT = 6 if L0 else 3
    GATE = 10 if L0 else 0
    LOWT = 5

    def loads_until(t, i):
        half = t // 2 if isinstance(t, int) else (t - i) // 2
        return 32 * (half + 1)

    def tok_view(d, t):
        s = slice(t * CHUNK, t * CHUNK + CHUNK) if isinstance(t, int) else bass.ds(t * CHUNK, CHUNK)
        return d[s, :].rearrange("(c p) f -> p c f", c=CT)

    def run(eng, body):
        run_steps(eng, NC, body)

    def carried(t, n, core, tail):
        if n >= LAG:
            return (t, n - LAG) if core else None
        return (t - 1, SL - LAG + n) if tail else None

    with nc.Block() as block:

        @block.sync
        def _(sp):
            def body(t, i, front, core, tail):
                j = 1 - i
                if front:
                    wait(sp, xres_step, XS * t)
                    v = tok_view(src_d, t + 1)
                    sp.dma_start(xtok[j][:, :, 0:E], v).then_inc(loaded[j], 16)
                    sp.dma_start(xtok[j][:, :, E:256], v[:, :, EA:E]).then_inc(loaded[j], 16)
                if tail:
                    sp.wait_ge(h_ready, CT * t)
                    sp.dma_start(tok_view(dst_d, t - 1), hout[j][:, :, :]).then_inc(stored[j], 16)

            run(sp, body)
            for i in range(2):
                sp.wait_ge(stored[i], 16 * ((NC + 1 - i) // 2))

        @block.tensor
        def _(pe):
            pe.wait_ge(const_ready, 1)

            def up(t, i, n):
                wait(pe, gelu_done, t * SL + n - 1)
                if n == 0:
                    pe.wait_ge(xl_ready, 2 * t + 2)
                five_passes(nc, U[n % 2][:, :], xh[i], xl[i], w1h, w1l, slice(n * P, n * P + P),
                            slice(0, CHUNK), False).then_inc(up_done, 1)

            def down(t, i, n):
                e, k = n // KD, n % KD
                pe.wait_ge(hl_ready, t * SL + n + 1)
                hi, lo = hh[n % 3], hl[n % 3]
                if not L0 and k == KD - 1:
                    pe.wait_ge(lowlo_ready, t + 1)
                for c in range(CT):
                    tok = slice(c * P, c * P + P)
                    if k == 0:
                        wait(pe, y_read, CT * (t * NE + e) - CT + c + 1)
                    nc.tensor.matmul(Y[c][:, :], hi[:, tok], w2h[:, n, :], start=k == 0, stop=False)
                    nc.tensor.matmul(Y[c][:, :], hi[:, tok], w2l[:, n, :], start=False, stop=False)
                    ins = nc.tensor.matmul(Y[c][:, :], lo[:, tok], w2h[:, n, :], start=False,
                                           stop=k == KD - 1 and L0)
                    if k == KD - 1:
                        if not L0:
                            ins = nc.tensor.matmul(Y[c][:, :], lowT[i][:, tok], W["wup"][0:3 * LR, :], start=False, stop=True)
                        ins.then_inc(y_done, 1)
                    elif c == CT - 1:
                        ins.then_inc(down_done, 1)

            def transposes(t, i):
                pe.wait_ge(loaded[i], loads_until(t, i))
                for a in range(2):
                    wait(pe, xl_ready, 2 * (t - 1) + a + 1)
                    for c in range(CT):
                        ins = nc.tensor.transpose(X[a][:, c * P:c * P + P], xtok[i][:, c, a * EA:a * EA + P],
                                                  ident[:, :])
                    ins.then_inc(xT_done, 1)

            def body(t, i, front, core, tail):
                j = 1 - i
                for n in range(SL if core else LAG):
                    if core:
                        up(t, i, n)
                    if n == FRONT and front:
                        transposes(t + 1, j)
                    if (d := carried(t, n, core, tail)) is not None:
                        down(d[0], i if n >= LAG else j, d[1])
                    if n == GATE and (front if L0 else core):
                        gate_products(t + 1 if L0 else t, j if L0 else i)
                    if n == LOWT and not L0:
                        pe.wait_ge(gate_step, GS * (t + 1))
                        for c in range(CT):
                            ins = nc.tensor.transpose(G[0:3 * LR, c * P:c * P + P], lowc[:, c, :], ident[:, :])
                        ins.then_inc(lowT_done, 1)

            def gate_products(t, i):
                if L0:
                    pe.wait_ge(xl_ready, 2 * t + 2)
                wait(pe, gate_step if L0 else lowlo_ready, GS * t if L0 else t)
                for c in range(CT):
                    ins = v5(G[:, c * GC:c * GC + GC], i, slice(c * P, c * P + P), c)
                ins.then_inc(gate_done, 1)

            def v5(out, i, tok, c):
                pairs = [(xh[i][:, 0, tok], W["wgh"][:, 0, :]), (xl[i][:, tok], W["wgh"][:, 0, :]),
                         (xh[i][:, 0, tok], W["wgl"][:, 0, :]), (xh[i][:, 1, tok], W["wgh"][:, 1, :]),
                         (xh[i][:, 1, tok], W["wgl"][:, 1, :])]
                for m, (l, r) in enumerate(pairs):
                    ins = nc.tensor.matmul(out, l, r, start=m == 0 and c == 0, stop=m == 4, skip_group_check=True)
                return ins

            transposes(0, 0)
            if L0:
                gate_products(0, 0)
            def shifted(t, i, front, core, tail):
                if not isinstance(t, int) or t >= 0:
                    body(t, i, front, core, tail)
            run(pe, shifted)

        @block.scalar
        def _(act):
            def split(t, i):
                for a in range(2):
                    act.wait_ge(xT_done, 2 * t + a + 1)
                    nc.scalar.activation(xh[i][:, a, :], X[a][:, :], ACT.Copy).then_inc(xh_ready, 1)

            def body(t, i, front, core, tail):
                j = 1 - i
                if core:
                    for n in range(SL):
                        act.wait_ge(up_done, t * SL + n + 1)
                        wait(act, hl_ready, t * SL + n - 1)
                        nc.scalar.activation(hid[n % 2][:, :], U[n % 2][:, :], ACT.Gelu,
                                             bias=W["b1"][:, n:n + 1]).then_inc(gelu_done, 1)
                        act.wait_ge(gelu_done, t * SL + n + 1)
                        act_free(t, n)
                        nc.scalar.activation(hh[n % 3][:, :], hid[n % 2][:, :], ACT.Copy).then_inc(hh_ready, 1)
                        if n == 0 and not L0:
                            act.wait_ge(gate_done, t + 1)
                            g = G[:, 0:CT * GC].rearrange("p (c k) -> p c k", c=CT)
                            wait(act, gate_step, GS * t)
                            nc.scalar.activation(low[:, :, :], g[:, :, 8:32], ACT.Gelu).then_inc(low_ready, 1)
                        if n == FRONT and front:
                            split(t + 1, j)
                        if n == LOWT and not L0:
                            act.wait_ge(lowT_done, t + 1)
                            nc.scalar.activation(lowT[i][:, :], G[0:3 * LR, :], ACT.Copy).then_inc(lowT_ready, 1)

            def act_free(t, n):
                m = t * SL + n - 3
                if isinstance(m, int) and m < 0:
                    return
                k = (n - 3) % KD
                e_before = (n - 3) // KD
                if k == KD - 1:
                    act.wait_ge(y_done, CT * (t * NE + e_before + 1))
                else:
                    act.wait_ge(down_done, (t * NE + e_before) * (KD - 1) + k + 1)

            split(0, 0)
            def shifted(t, i, front, core, tail):
                if not isinstance(t, int) or t >= 0:
                    body(t, i, front, core, tail)
            run(act, shifted)

        @block.vector
        def _(dve):
            def split(t, i):
                for a in range(2):
                    dve.wait_ge(xh_ready, 2 * t + a + 1)
                    if a == 0:
                        nc.vector.tensor_tensor(xl[i][:, :], X[0][:, :], xh[i][:, 0, :], ALU.subtract).then_inc(xl_ready, 1)
                    else:
                        nc.vector.tensor_tensor(xh[i][EB:P, 1, :], X[1][EB:P, :], xh[i][EB:P, 1, :],
                                                ALU.subtract).then_inc(xl_ready, 1)

            def steps(t, done):
                s = [done]

                def then(ins):
                    s[0] += 1
                    ins.then_inc(gate_step, 1)
                    dve.wait_ge(gate_step, GS * t + s[0])
                return then

            wide = lambda a: a.unsqueeze(2).broadcast_to([P, CT, NEXP if L0 else NR])

            def logits(t, then):
                n = NEXP if L0 else NR
                g = G[:, 0:CT * GC].rearrange("p (c k) -> p c k", c=CT)
                bias = W["bg"][:, 0:n].unsqueeze(1).broadcast_to([P, CT, n])
                dve.wait_ge(gate_done if L0 else low_ready, t + 1)
                then(nc.vector.tensor_tensor(lg[:, :, 0:n], g[:, :, 0:n], bias, ALU.add))
                then(nc.vector.tensor_reduce(out=top[:, :], in_=lg[:, :, 0:n], op=ALU.max, axis=AX.X))

            def choice(t, i):
                then = steps(t, 0)
                logits(t, then)
                then(nc.vector.tensor_tensor(seen[:, :, 1:NEXP + 1], lg[:, :, :], wide(top[:, :]), ALU.is_ge))
                for k in range(2, NEXP + 1):
                    then(nc.vector.tensor_tensor(seen[:, :, k:k + 1], seen[:, :, k:k + 1], seen[:, :, k - 1:k], ALU.max))
                then(nc.vector.tensor_tensor(chosen[i][:, :, :], seen[:, :, 1:], seen[:, :, 0:NEXP], ALU.subtract))

            def router_logits(t, i):
                then = steps(t, 0)
                logits(t, then)
                nc.vector.tensor_tensor(lg[:, :, 0:NR], lg[:, :, 0:NR], wide(top[:, :]),
                                        ALU.subtract).then_inc(gate_step, 1)

            def router_probs(t, i):
                dve.wait_ge(gate_step, GS * t + 4)
                then = steps(t, 4)
                then(nc.vector.tensor_reduce(out=den[:, :], in_=pr[:, :, :], op=ALU.add, axis=AX.X))
                then(nc.vector.reciprocal(den[:, :], den[:, :]))
                then(nc.vector.tensor_tensor(pr[:, :, :], pr[:, :, :], wide(den[:, :]), ALU.mult))
                then(nc.vector.tensor_reduce(out=least[:, :], in_=pr[:, :, :], op=ALU.min, axis=AX.X))
                then(nc.vector.tensor_tensor(eq[:, :, 0:NR], pr[:, :, :], wide(least[:, :]), ALU.is_le))

            def router_best(t, i):
                then = steps(t, 9)
                then(nc.vector.tensor_tensor(eq[:, :, 1:2], eq[:, :, 1:2], eq[:, :, 2:3], ALU.max))
                then(nc.vector.memset(eq[:, :, 0:1], 1.0))
                then(nc.vector.tensor_tensor(out_[:, :, :], eq[:, :, 0:NR], eq[:, :, 1:NR + 1], ALU.subtract))
                then(nc.vector.tensor_tensor(out_[:, :, :], out_[:, :, :], pr[:, :, :], ALU.mult))
                then(nc.vector.tensor_tensor(pr[:, :, :], pr[:, :, :], out_[:, :, :], ALU.subtract))
                then(nc.vector.tensor_reduce(out=den[:, :], in_=pr[:, :, :], op=ALU.add, axis=AX.X))
                then(nc.vector.tensor_scalar(den[:, :], den[:, :], 1e-6, None, ALU.add))
                then(nc.vector.reciprocal(den[:, :], den[:, :]))
                then(nc.vector.tensor_tensor(comb[:, :, :], pr[:, :, :], wide(den[:, :]), ALU.mult))
                for k in range(3):
                    ins = nc.vector.tensor_tensor(
                        lowc[:, :, LR * k + 8:LR * k + 32].rearrange("p c (e r) -> p c e r", e=NR),
                        low[:, :, :].rearrange("p c (e r) -> p c e r", e=NR),
                        comb[:, :, :].unsqueeze(3).broadcast_to([P, CT, NR, 8]), ALU.mult)
                ins.then_inc(gate_step, 1)

            def low_lo(t, i):
                dve.wait_ge(lowT_ready, t + 1)
                nc.vector.tensor_tensor(lowT[i][LR:2 * LR, :], G[LR:2 * LR, :], lowT[i][LR:2 * LR, :],
                                        ALU.subtract).then_inc(lowlo_ready, 1)

            gate_parts = {} if L0 else {0: router_logits, 1: router_probs, 3: router_best}

            def body(t, i, front, core, tail):
                j = 1 - i
                for n in range(SL if core else LAG + 3):
                    d = carried(t, n, core, tail)
                    if d is not None and d[1] % KD == KD - 1:
                        combine(d[0], i if n >= LAG else j, d[1] // KD)
                    if core:
                        dve.wait_ge(hh_ready, t * SL + n + 1)
                        nc.vector.tensor_tensor(hl[n % 3][:, :], hid[n % 2][:, :], hh[n % 3][:, :],
                                                ALU.subtract).then_inc(hl_ready, 1)
                    if L0 and front and n == GATE + 1:
                        choice(t + 1, j)
                    if core and n in gate_parts:
                        gate_parts[n](t, i)
                    if core and not L0 and n == LOWT:
                        low_lo(t, i)
                    if n == FRONT and front:
                        split(t + 1, j)
                    if tail and n == LAG:
                        stats(t - 1)
                    if tail and n == LAG + 2:
                        dve.wait_ge(rstd_ready, t)
                        wait_stored(t, j)
                        for c in range(CT):
                            nc.vector.tensor_scalar(hout[j][:, c, :], acc[:, c, :], mv[:, c, 0:1], rstd[:, c:c + 1],
                                                    ALU.subtract, ALU.mult).then_inc(h_ready, 1)

            def combine(t, i, e):
                if e == 0:
                    wait(dve, h_ready, CT * t)
                    dve.wait_ge(xres_step, XS * (t + 1))
                for c in range(CT):
                    g = CT * (t * NE + e) + c
                    dve.wait_ge(y_done, g + 1)
                    if not L0:
                        nc.vector.tensor_tensor(acc[:, c, :], Y[c][:, :], xres[i][:, c, :], ALU.add).then_inc(y_read, 1)
                        continue
                    if e:
                        dve.wait_ge(y_read, g - CT + 1)
                    prev = acc[:, c, :] if e else xres[i][:, c, :]
                    nc.vector.scalar_tensor_tensor(acc[:, c, :], Y[c][:, :], chosen[i][:, c, e:e + 1], prev,
                                                   ALU.mult, ALU.add).then_inc(y_read, 1)

            def stats(t):
                for c in range(CT):
                    dve.wait_ge(y_read, CT * (t * NE + NE - 1) + c + 1)
                    nc.vector.bn_stats(st6[:, c, :], acc[:, c, :]).then_inc(st_ready, 1)
                dve.wait_ge(st_ready, NS * t + CT)
                nc.vector.memset(ve[:, :], 0.0)
                for c in range(CT):
                    nc.vector.bn_aggr(mv[:, c, :], st6[:, c, :]).then_inc(st_ready, 1)
                dve.wait_ge(st_ready, NS * t + 2 * CT)
                nc.vector.tensor_scalar(ve[:, :], mv[:, :, 1], EPS, None, ALU.add).then_inc(st_ready, 1)

            def wait_stored(t, j):
                if isinstance(t, int):
                    wait(dve, stored[j], 16 * ((t - 1 - j) // 2))
                else:
                    dve.wait_ge(stored[j], (t - 1 - j) * 8)

            dve.wait_ge(const_ready, 1)
            split(0, 0)
            if L0:
                choice(0, 0)
            def shifted(t, i, front, core, tail):
                if not isinstance(t, int) or t >= 0:
                    body(t, i, front, core, tail)
            run(dve, shifted)

        @block.gpsimd
        def _(pool):
            pool.memset(mhalf[:, :], -0.5)
            if L0:
                pool.memset(seen[:, :, 0:1], 0.0)
            else:
                pool.memset(base_e[:, :, :], 2.718281828459045)
                for k in range(3):
                    pool.memset(lowc[:, :, LR * k:LR * k + 8], 0.0)
                pool.memset(eq[:, :, NR:NR + 1], 0.0)
            pool.memset(rstd[:, :], 0.0).then_inc(const_ready, 1)

            def residual(t, i):
                pool.wait_ge(loaded[i], loads_until(t, i))
                wait(pool, y_read, CT * NE * (t - 1))
                if not L0:
                    pool.wait_ge(xT_done, 2 * t + 2)
                    pool.tensor_tensor(xres[i][:, :, :], xtok[i][:, :, 0:E],
                                       W["b2"][:, 0:1, :].broadcast_to([P, CT, E]), ALU.add).then_inc(xres_step, 1)
                    return
                pool.wait_ge(gate_step, GS * (t + 1))
                for e in range(NE):
                    wait(pool, xres_step, XS * t + 2 * e)
                    pool.tensor_tensor(bsel[:, :, :], W["b2"][:, e:e + 1, :].broadcast_to([P, CT, E]),
                                       chosen[i][:, :, e:e + 1].broadcast_to([P, CT, E]),
                                       ALU.mult).then_inc(xres_step, 1)
                    pool.wait_ge(xres_step, XS * t + 2 * e + 1)
                    prev = xres[i][:, :, :] if e else xtok[i][:, :, 0:E]
                    pool.tensor_tensor(xres[i][:, :, :], prev, bsel[:, :, :], ALU.add).then_inc(xres_step, 1)

            if L0:
                residual(0, 0)

            def body(t, i, front, core, tail):
                if core and not L0:
                    residual(t, i)
                    pool.wait_ge(gate_step, GS * t + 3)
                    pool.tensor_tensor(pr[:, :, :], base_e[:, :, :], lg[:, :, 0:NR], ALU.pow).then_inc(gate_step, 1)
                if tail:
                    pool.wait_ge(st_ready, NS * t)
                    pool.tensor_tensor(rstd[:, :], ve[:, :], mhalf[:, :], ALU.pow).then_inc(rstd_ready, 1)
                if L0 and front:
                    residual(t + 1, 1 - i)

            def shifted(t, i, front, core, tail):
                if not isinstance(t, int) or t >= 0:
                    body(t, i, front, core, tail)
            run(pool, shifted)


def vit_tower(nc, NB, a, out):
    NC = -(-NB * NT // CHUNK)
    TOK = NC * CHUNK
    scratch = [nc.dram_tensor(f"h{n}", (TOK, E), F32, kind="Internal").ap() for n in range(3)]
    flat = lambda t: t[:, :].rearrange("p a -> p a") if len(t.shape) == 2 else t[:, :, :].rearrange("p a b -> p (a b)")
    with ExitStack() as whole:
        keep = lambda name, shape, dt: whole.enter_context(nc.sbuf_tensor("sb_" + name, shape, dt))
        masks, ident, ident16 = keep("masks", [P, C_N], F32), keep("ident", [P, P], F32), keep("ident16", [P, P], F16)
        loads, later = [], []

        def halves(name, src, shape, late=False):
            hi, lo = keep(name + "_hi", shape, F16), keep(name + "_lo", shape, F16)
            size = 1
            for s in shape[1:]:
                size *= s
            (later if late else loads).append((flat(src), flat(hi), flat(lo), size, P))
            return hi, lo

        def single(name, src, shape):
            t = keep(name, shape, F32)
            size = 1
            for s in shape[1:]:
                size *= s
            loads.append((flat(src), flat(t), None, size, shape[0]))
            return t

        def two_rows(name, src, shape):
            t = keep(name, shape, F16)
            loads.append((flat(src), flat(t), C_ROW1, shape[1] * shape[2], P))
            return t

        wa = []
        for n in range(2):
            w = {}
            w["wh"], w["wl"] = halves(f"attn{n}", a[f"wattn{n}"], [P, 2, 2 * NG * P + 2 * E])
            w["bqk"] = single(f"bqk{n}", a[f"bqk{n}"], [P, 2 * NG])
            if n == 0:
                w["bv2"] = two_rows("bv0", a["bv0"], [P, 1, E])
            w["bo"] = single(f"bo{n}", a[f"bo{n}"], [P, E])
            wa.append(w)
        wa[0]["wth"], wa[0]["wtl"] = halves("wtok", a["wtok"], [P, KD, E])
        pos = single("pos", a["pos"], [P, 2, E])
        tokb = single("tokb", a["tokb"], [P, 2, E])
        wa[0]["addend"] = keep("addend", [P, 2, E], F32)
        wa[0]["xp_d"] = a["xp"]
        wa[1]["sc_d"] = a["sc"]
        wf = []
        for n, ne in ((0, NEXP), (1, 1)):
            w = {}
            w["w1h"], w["w1l"] = halves(f"w1_{n}", a[f"w1_{n}"], [P, 2, ne * KD * P], late=n == 0)
            w["w2h"], w["w2l"] = halves(f"w2_{n}", a[f"w2_{n}"], [P, ne * KD, E], late=n == 0)
            w["b1"] = single(f"b1_{n}", a[f"b1_{n}"], [P, ne * KD])
            w["b2"] = single(f"b2_{n}", a[f"b2_{n}"], [P, ne, E])
            w["wgh"], w["wgl"] = halves(f"wg{n}", a[f"wg{n}"], [P, 2, 4 if n == 0 else 32])
            w["bg"] = single(f"bg{n}", a[f"bg{n}"], [P, 4])
            wf.append(w)
        wf[1]["wup"] = keep("wup", [P, E], F16)
        loads.append((flat(a["wup"]), flat(wf[1]["wup"]), C_LOROWS, E, P))

        def phase(f, *args):
            with ExitStack() as own:
                sb = lambda name, shape, dt: own.enter_context(nc.sbuf_tensor(name, shape, dt))
                pb = lambda name, shape, dt: own.enter_context(nc.psum_tensor(name, shape, dt))
                sem = lambda name: own.enter_context(nc.semaphore(name))
                f(sem, sb, pb, *args)

        phase(lambda sem, sb, pb: setup(nc, loads, a["consts"], masks, ident, ident16, sem, sb,
                                        (pos, tokb, wa[0]["addend"]), scratch, a["pos"], NB * NT))
        phase(lambda sem, sb, pb: attention(nc, 0, NB, None, scratch[0], wa[0], masks, ident, ident16, later, sem, sb, pb))
        phase(lambda sem, sb, pb: ffn(nc, 0, NC, scratch[0], scratch[1], wf[0], masks, ident, sem, sb, pb))
        phase(lambda sem, sb, pb: attention(nc, 1, NB, scratch[1], scratch[2], wa[1], masks, ident, ident16, [], sem, sb, pb))
        phase(lambda sem, sb, pb: ffn(nc, 1, NC, scratch[2], out, wf[1], masks, ident, sem, sb, pb))


def lay_out(inputs, np):
    f = {k: np.asarray(v) for k, v in inputs.items()}
    NB = f["x"].shape[0]
    d = {}
    x = f["x"].reshape(NB, 14, 16, 14, 16, 3).transpose(5, 2, 4, 0, 1, 3).reshape(KD, P, NB, NSC)
    xp = np.zeros((P, NB, KD, NT), np.float32)
    xp[:, :, :, 1:] = x.transpose(1, 2, 0, 3)
    d["xp"] = xp
    d["wtok"] = f["L0_tok_W"].T.reshape(KD, P, E).transpose(1, 0, 2)
    pos = np.zeros((P, 2, E), np.float32)
    pos[:, 0], pos[:T1, 1] = f["L0_tok_pos_embed"][0, :P], f["L0_tok_pos_embed"][0, P:]
    d["pos"] = pos
    tokb = np.broadcast_to(f["L0_tok_b"], (P, 2, E)).copy()
    tokb[0, 0] = f["L0_tok_cls_token"][0, 0]
    d["tokb"] = tokb

    def two_tiles(w):
        return np.stack([w[:EA], np.concatenate([w[EA:], w[EA:]])], 1)

    def heads_twice(w):
        w = w.reshape(*w.shape[:-1], HEADS, 1, HD)
        return np.concatenate([w, w], -2).reshape(*w.shape[:-3], HEADS * 2 * HD)

    for n, (qkv, o) in enumerate((("L0_attn_W_qkv", "L0_attn_W_out"), ("L1_attn_W_qkv", "L1_attn_W_proj"))):
        w = f[qkv]
        d[f"wattn{n}"] = two_tiles(np.concatenate(
            [heads_twice(w[:, :E]), heads_twice(w[:, E:2 * E]), w[:, 2 * E:], f[o]], 1))
    bq = f["L0_attn_b_qkv"]
    b = np.concatenate([heads_twice(bq[:E]), heads_twice(bq[E:2 * E])])
    rows = lambda v: np.broadcast_to(v, (P, v.shape[0]))
    d["bqk0"], d["bqk1"] = b.reshape(2 * NG, P).T, np.zeros((P, 2 * NG), np.float32)
    d["bo0"], d["bo1"] = rows(f["L0_attn_b_out"]), rows(f["L1_attn_b_proj"])
    sc = np.zeros((P, 2, 256), np.float32)
    s = f["L1_attn_sc_token"][0]
    s = np.concatenate([s, s[:, EA:]], 1)
    sc[:, 0], sc[:NSC - P, 1] = s[:P], s[P:]
    d["sc"] = sc

    def two_rows(b):
        out = np.zeros((P, *b.shape), np.float32)
        out[0], out[1] = b, b
        return out

    w1 = f["L0_ffn_W1"].transpose(1, 0, 2).reshape(E, NEXP * KD * P)
    d["w1_0"], d["w1_1"] = two_tiles(w1), two_tiles(f["L1_ffn_w1"])
    d["w2_0"] = f["L0_ffn_W2"].reshape(NEXP * KD, P, E).transpose(1, 0, 2)
    d["w2_1"] = f["L1_ffn_w2"].reshape(KD, P, E).transpose(1, 0, 2)
    d["b1_0"] = f["L0_ffn_b1"].reshape(NEXP * KD, P).T
    d["b1_1"] = f["L1_ffn_b1"].reshape(KD, P).T
    d["bv0"] = two_rows(bq[None, 2 * E:])
    d["b2_0"] = np.broadcast_to(f["L0_ffn_b2"], (P, NEXP, E))
    d["b2_1"] = np.broadcast_to(f["L1_ffn_b2"], (P, 1, E))
    d["wg0"] = two_tiles(f["L0_ffn_Wg"])
    low = f["L1_ffn_w_down"].transpose(1, 0, 2).reshape(E, 24)
    d["wg1"] = two_tiles(np.concatenate([f["L1_ffn_router_w"], np.zeros((E, 5), np.float32), low], 1))
    d["bg0"] = rows(f["L0_ffn_bg"])
    d["bg1"] = rows(np.concatenate([f["L1_ffn_router_b"], np.zeros(1, np.float32)]))
    wup = np.zeros((P, E), np.float32)
    for k in range(3):
        wup[32 * k + 8:32 * k + 32] = f["L1_ffn_w_up"].reshape(24, E)
    d["wup"] = wup
    consts = np.zeros((P, C_N + P), np.float32)
    p = np.arange(P)
    for h in range(HG):
        consts[:, C_HEAD + h] = p // 32 == h
        consts[:, C_HEADHI + h] = (p // 32 == h) & (p % 32 < HD)
        consts[:, C_HEADONE + h] = p == 32 * h + HD
    consts[:, C_LO], consts[:, C_HI] = p % 32 >= HD, p % 32 < HD
    consts[:, C_ROW1], consts[:, C_ROW01], consts[:, C_LOROWS] = p == 1, p < 2, p >= 64
    consts[:, C_N:] = np.eye(P)
    d["consts"] = consts
    return {k: np.ascontiguousarray(v) for k, v in d.items()}


def kernel(**inputs):
    import numpy as _np
    import concourse.bacc as _bacc
    from concourse import mybir as _mybir
    from concourse.bass_utils import run_bass_kernel_spmd as _run

    arrays = lay_out(inputs, _np)
    NB = _np.asarray(inputs["x"]).shape[0]
    tokens = -(-NB * NT // CHUNK) * CHUNK
    nc = _bacc.Bacc("TRN2", target_bir_lowering=False, num_devices=1)
    args = {k: nc.dram_tensor(k, v.shape, _mybir.dt.from_np(v.dtype), kind="ExternalInput").ap()
            for k, v in arrays.items()}
    out = nc.dram_tensor("out", (tokens, E), F32, kind="ExternalOutput").ap()
    vit_tower(nc, NB, args, out)
    r = _run(nc, [arrays], core_ids=[0])
    return r.results[0]["out"][:NB * NT].reshape(NB, NT, E)
```
